# Optimizing a Trainium2 kernel written in Bass

```python
import numpy as np
import jax
import jax.numpy as jnp

def _softmax(x, axis=-1):
    return jax.nn.softmax(x, axis=axis)

def _gelu(x):
    return jax.nn.gelu(x, approximate=True)

def _silu(x):
    return jax.nn.silu(x)

def _sigmoid(x):
    return jax.nn.sigmoid(x)

def _layernorm(x, axis=-1, eps=1e-05):
    m = jnp.mean(x, axis=axis, keepdims=True)
    v = jnp.var(x, axis=axis, keepdims=True)
    return (x - m) / jnp.sqrt(v + eps)

def _scatter_add(tgt, idx, src, axis=0):
    return tgt.at[idx].add(src)

def _segment_sum(src, seg, n):
    return jax.ops.segment_sum(src, seg, n)
kernel_name = 'mk_hybrid_d1_jaxref_r8_ecb210'

def setup_inputs(seed: int=0):
    np.random.seed(seed)
    _w = jnp.asarray

    def _L0_attn_a_setup():
        import jax, jax.numpy as jnp
        import numpy as np
        import math
        HEADS = 16
        LN_EPS = 1e-05

        def _layernorm(x, w, b):
            mu = jnp.mean(x, axis=-1, keepdims=True)
            var = jnp.mean((x - mu) ** 2, axis=-1, keepdims=True)
            return (x - mu) * jax.lax.rsqrt(var + LN_EPS) * w + b
        key = jax.random.key(seed)
        ks = jax.random.split(key, 8)
        b, t, e = (2, 256, 128)
        s = e // HEADS
        sc = 1.0 / math.sqrt(e)
        inp = {'x': jax.random.normal(ks[0], (b, t, e), dtype=jnp.float32), 'Wk': jax.random.normal(ks[1], (e, e), dtype=jnp.float32) * sc, 'Wq': jax.random.normal(ks[2], (e, e), dtype=jnp.float32) * sc, 'Wv': jax.random.normal(ks[3], (e, e), dtype=jnp.float32) * sc, 'Wo': jax.random.normal(ks[4], (e, e), dtype=jnp.float32) * sc, 'bo': jnp.zeros((e,), dtype=jnp.float32), 'kln_w': jnp.ones((s,), dtype=jnp.float32), 'kln_b': jnp.zeros((s,), dtype=jnp.float32), 'qln_w': jnp.ones((s,), dtype=jnp.float32), 'qln_b': jnp.zeros((s,), dtype=jnp.float32)}
        return inp
    _L0_attn_a_in = _L0_attn_a_setup()

    def _L0_attn_b_setup():
        import jax, jax.numpy as jnp
        import numpy as np
        BSZ, SEQ, DZ = (4, 256, 128)
        C, R = (16, 64)
        SCALE = 0.03125
        REG_H = 1.0
        key = jax.random.key(seed)
        k1, k2, k3 = jax.random.split(key, 3)
        qz = jax.random.normal(k1, (BSZ, SEQ, DZ), dtype=jnp.float32)
        ternary_factor_u = jax.random.normal(k2, (C * R, DZ), dtype=jnp.float32) * 0.02
        ternary_factor_v = jax.random.normal(k3, (C * R, DZ), dtype=jnp.float32) * 0.02
        return {'qz': qz, 'ternary_factor_u': ternary_factor_u, 'ternary_factor_v': ternary_factor_v}
    _L0_attn_b_in = _L0_attn_b_setup()

    def _L0_ffn_setup():
        import jax, jax.numpy as jnp
        import numpy as np
        HIDDEN = 128
        INTER = 512
        NUM_EXPERTS = 8
        TOP_K = 2
        EPS = 1e-05

        def _layer_norm(x, g, b):
            m = jnp.mean(x, axis=-1, keepdims=True)
            v = jnp.mean(jnp.square(x - m), axis=-1, keepdims=True)
            return (x - m) * jax.lax.rsqrt(v + EPS) * g + b
        key = jax.random.key(seed)
        ks = jax.random.split(key, 8)
        s = 0.02
        return {'x': jax.random.normal(ks[0], (4, 256, HIDDEN), dtype=jnp.float32), 'ln1_g': jnp.ones((HIDDEN,), jnp.float32), 'ln1_b': jnp.zeros((HIDDEN,), jnp.float32), 'attn_w': jax.random.normal(ks[1], (HIDDEN, HIDDEN), jnp.float32) * s, 'ln2_g': jnp.ones((HIDDEN,), jnp.float32), 'ln2_b': jnp.zeros((HIDDEN,), jnp.float32), 'gate_w': jax.random.normal(ks[2], (NUM_EXPERTS, HIDDEN), jnp.float32) * s, 'gate_proj': jax.random.normal(ks[3], (NUM_EXPERTS, INTER, HIDDEN), jnp.float32) * s, 'up_proj': jax.random.normal(ks[4], (NUM_EXPERTS, INTER, HIDDEN), jnp.float32) * s, 'down_proj': jax.random.normal(ks[5], (NUM_EXPERTS, HIDDEN, INTER), jnp.float32) * s}
    _L0_ffn_in = _L0_ffn_setup()
    _d = {'L0_attn_a_x': _L0_attn_a_in['x'], 'L0_attn_a_Wk': _L0_attn_a_in['Wk'], 'L0_attn_a_Wq': _L0_attn_a_in['Wq'], 'L0_attn_a_Wv': _L0_attn_a_in['Wv'], 'L0_attn_a_Wo': _L0_attn_a_in['Wo'], 'L0_attn_a_bo': _L0_attn_a_in['bo'], 'L0_attn_a_kln_w': _L0_attn_a_in['kln_w'], 'L0_attn_a_kln_b': _L0_attn_a_in['kln_b'], 'L0_attn_a_qln_w': _L0_attn_a_in['qln_w'], 'L0_attn_a_qln_b': _L0_attn_a_in['qln_b'], 'L0_attn_b_ternary_factor_u': _L0_attn_b_in['ternary_factor_u'], 'L0_attn_b_ternary_factor_v': _L0_attn_b_in['ternary_factor_v'], 'L0_ffn_ln1_g': _L0_ffn_in['ln1_g'], 'L0_ffn_ln1_b': _L0_ffn_in['ln1_b'], 'L0_ffn_attn_w': _L0_ffn_in['attn_w'], 'L0_ffn_ln2_g': _L0_ffn_in['ln2_g'], 'L0_ffn_ln2_b': _L0_ffn_in['ln2_b'], 'L0_ffn_gate_w': _L0_ffn_in['gate_w'], 'L0_ffn_gate_proj': _L0_ffn_in['gate_proj'], 'L0_ffn_up_proj': _L0_ffn_in['up_proj'], 'L0_ffn_down_proj': _L0_ffn_in['down_proj']}
    _x0 = _d['L0_attn_a_x']
    _d['L0_attn_a_x'] = jax.random.normal(jax.random.fold_in(jax.random.key(seed), 1), (4, 1024, 128), dtype=_x0.dtype)
    del _x0
    return _d

def reference(L0_attn_a_x, L0_attn_a_Wk, L0_attn_a_Wq, L0_attn_a_Wv, L0_attn_a_Wo, L0_attn_a_bo, L0_attn_a_kln_w, L0_attn_a_kln_b, L0_attn_a_qln_w, L0_attn_a_qln_b, L0_attn_b_ternary_factor_u, L0_attn_b_ternary_factor_v, L0_ffn_ln1_g, L0_ffn_ln1_b, L0_ffn_attn_w, L0_ffn_ln2_g, L0_ffn_ln2_b, L0_ffn_gate_w, L0_ffn_gate_proj, L0_ffn_up_proj, L0_ffn_down_proj):

    def _L0_attn_a_ref(x, Wk, Wq, Wv, Wo, bo, kln_w, kln_b, qln_w, qln_b):
        import jax, jax.numpy as jnp
        import numpy as np
        import math
        HEADS = 16
        LN_EPS = 1e-05

        def _layernorm(x, w, b):
            mu = jnp.mean(x, axis=-1, keepdims=True)
            var = jnp.mean((x - mu) ** 2, axis=-1, keepdims=True)
            return (x - mu) * jax.lax.rsqrt(var + LN_EPS) * w + b
        b, t, e = x.shape
        h = HEADS
        s = e // h
        scale = 1.0 / math.sqrt(s)
        k = (x @ Wk).reshape(b, t, h, s)
        q = (x @ Wq).reshape(b, t, h, s)
        v = (x @ Wv).reshape(b, t, h, s)
        k = _layernorm(k, kln_w, kln_b)
        q = _layernorm(q, qln_w, qln_b)
        dot = jnp.einsum('bqhs,bkhs->bhqk', q, k) * scale
        causal = jnp.tril(jnp.ones((t, t), dtype=bool))
        dot = jnp.where(causal, dot, -jnp.inf)
        attn = jax.nn.softmax(dot, axis=-1)
        out = jnp.einsum('bhqk,bkhs->bqhs', attn, v).reshape(b, t, e)
        return out @ Wo + bo

    def _L0_attn_b_ref(qz, ternary_factor_u, ternary_factor_v):
        import jax, jax.numpy as jnp
        import numpy as np
        BSZ, SEQ, DZ = (4, 256, 128)
        C, R = (16, 64)
        SCALE = 0.03125
        REG_H = 1.0
        bsz, seq_len, _ = qz.shape
        qz_u = qz @ ternary_factor_u.T * SCALE
        qz_v = qz @ ternary_factor_v.T * SCALE
        qz_u = qz_u.reshape(bsz, seq_len, C, R).transpose(0, 2, 1, 3)
        qz_v = qz_v.reshape(bsz, seq_len, C, R).transpose(0, 2, 1, 3)
        message_F = jnp.einsum('bcsr,bctr->bcst', qz_u, qz_v)
        qh = jax.nn.sigmoid(message_F / REG_H)
        qh_v1 = jnp.einsum('bcst,bctr->bcsr', qh, qz_v)
        qh_v2 = jnp.einsum('bcst,bcsr->bctr', qh, qz_u)
        qh_v1 = qh_v1.transpose(0, 2, 1, 3).reshape(bsz, seq_len, C * R)
        qh_v2 = qh_v2.transpose(0, 2, 1, 3).reshape(bsz, seq_len, C * R)
        message_G = (qh_v1 @ ternary_factor_u + qh_v2 @ ternary_factor_v) * SCALE
        return message_G

    def _L0_ffn_ref(x, ln1_g, ln1_b, attn_w, ln2_g, ln2_b, gate_w, gate_proj, up_proj, down_proj):
        import jax, jax.numpy as jnp
        import numpy as np
        HIDDEN = 128
        INTER = 512
        NUM_EXPERTS = 8
        TOP_K = 2
        EPS = 1e-05

        def _layer_norm(x, g, b):
            m = jnp.mean(x, axis=-1, keepdims=True)
            v = jnp.mean(jnp.square(x - m), axis=-1, keepdims=True)
            return (x - m) * jax.lax.rsqrt(v + EPS) * g + b
        B, S, H = x.shape
        h = x + jnp.einsum('bsh,oh->bso', _layer_norm(x, ln1_g, ln1_b), attn_w)
        t = _layer_norm(h, ln2_g, ln2_b).reshape(-1, H)
        T = t.shape[0]
        logits = jnp.einsum('th,eh->te', t, gate_w)
        top_vals, top_idx = jax.lax.top_k(logits, TOP_K)
        rw = jax.nn.softmax(top_vals, axis=-1)
        comb = jnp.zeros((T, NUM_EXPERTS), dtype=t.dtype)
        comb = comb.at[jnp.arange(T)[:, None], top_idx].add(rw)
        out = jnp.zeros_like(t)
        for e in range(NUM_EXPERTS):
            g = jnp.einsum('th,ih->ti', t, gate_proj[e])
            u = jnp.einsum('th,ih->ti', t, up_proj[e])
            oe = jnp.einsum('ti,hi->th', jax.nn.silu(g) * u, down_proj[e])
            out = out + comb[:, e:e + 1] * oe
        return h + out.reshape(B, S, H)
    x = L0_attn_a_x
    x = x + _L0_attn_a_ref(_layernorm(x, axis=-1), L0_attn_a_Wk, L0_attn_a_Wq, L0_attn_a_Wv, L0_attn_a_Wo, L0_attn_a_bo, L0_attn_a_kln_w, L0_attn_a_kln_b, L0_attn_a_qln_w, L0_attn_a_qln_b)
    x = x + _L0_ffn_ref(_layernorm(x, axis=-1), L0_ffn_ln1_g, L0_ffn_ln1_b, L0_ffn_attn_w, L0_ffn_ln2_g, L0_ffn_ln2_b, L0_ffn_gate_w, L0_ffn_gate_proj, L0_ffn_up_proj, L0_ffn_down_proj)
    x = x + _L0_attn_b_ref(_layernorm(x, axis=-1), L0_attn_b_ternary_factor_u, L0_attn_b_ternary_factor_v)
    x = x + _L0_ffn_ref(_layernorm(x, axis=-1), L0_ffn_ln1_g, L0_ffn_ln1_b, L0_ffn_attn_w, L0_ffn_ln2_g, L0_ffn_ln2_b, L0_ffn_gate_w, L0_ffn_gate_proj, L0_ffn_up_proj, L0_ffn_down_proj)
    return x

_drawn_inputs = setup_inputs


def setup_inputs(seed=0):
    import zlib

    import numpy as np

    out = dict(_drawn_inputs(seed))
    spreads = {'L0_attn_a_bo': (0.0, 0.1),
     'L0_attn_a_kln_w': (1.0, 0.6),
     'L0_attn_a_kln_b': (0.0, 0.8),
     'L0_attn_a_qln_w': (1.0, 0.6),
     'L0_attn_a_qln_b': (0.0, 0.677),
     'L0_ffn_ln1_g': (1.0, 0.2),
     'L0_ffn_ln1_b': (0.0, 0.417),
     'L0_ffn_ln2_g': (1.0, 0.6),
     'L0_ffn_ln2_b': (0.0, 0.8)}
    factors = {'L0_attn_b_ternary_factor_u': 8.0,
     'L0_attn_b_ternary_factor_v': 8.0,
     'L0_ffn_gate_w': 8.0,
     'L0_ffn_gate_proj': 8.0,
     'L0_ffn_up_proj': 8.0,
     'L0_ffn_down_proj': 8.0}
    for name, (base, spread) in spreads.items():
        noise = np.random.default_rng([zlib.crc32(name.encode()), seed]).standard_normal(out[name].shape)
        drawn = base * np.exp(spread * noise) if base else spread * noise
        out[name] = jnp.asarray(drawn.astype(out[name].dtype))
    for name, factor in factors.items():
        out[name] = (out[name] * factor).astype(out[name].dtype)
    return out
```

```python
from contextlib import ExitStack

import concourse.bass as bass
from concourse import mybir

F32 = mybir.dt.float32
F32R = mybir.dt.float32r
BF16 = mybir.dt.bfloat16
U32 = mybir.dt.uint32
ALU = mybir.AluOpType
ACT = mybir.ActivationFunctionType
AX = mybir.AxisListType

P = 128
BATCH, SEQ, DIM = 4, 1024, 128
TILES = SEQ // P
ALL = BATCH * TILES
HALF = 512
EPS = 1e-5

HEADS, HD = 16, 8
GROUP = 4
GROUPS = HEADS // GROUP
STACK = P // GROUP
MASKED = -1e30

CH, RANK = 16, 64
MSG_SCALE = 0.03125

EXPERTS, INTER = 8, 512
BLOCKS = INTER // P
UNITS = EXPERTS * BLOCKS
GTOK = 4


def ds(start, size):
    return bass.DynSlice(start, size)


class Link:

    def __init__(self, eng, sem, base=0):
        self.eng, self.sem, self.base, self.n = eng, sem, base, 0

    def __call__(self, ins):
        self.n += 1
        ins.then_inc(self.sem, 1)
        self.eng.wait_ge(self.sem, self.base + self.n)


def row_moments(dve, link, stats, mean, spread, work, tiles):
    even, odd = stats[:, 0:tiles, 1], stats[:, 0:tiles, 4]
    link(dve.tensor_tensor(mean, even, odd, ALU.add))
    link(dve.tensor_tensor(work, even, odd, ALU.subtract))
    link(dve.scalar_tensor_tensor(out=work, in0=work, scalar=0.25, in1=work, op0=ALU.mult, op1=ALU.mult))
    link(dve.tensor_tensor(spread, stats[:, 0:tiles, 2], stats[:, 0:tiles, 5], ALU.add))
    link(dve.scalar_tensor_tensor(out=spread, in0=spread, scalar=1.0 / DIM, in1=work, op0=ALU.mult, op1=ALU.add))
    link(dve.tensor_scalar(mean, mean, 0.5, None, ALU.mult))
    return dve.tensor_scalar(spread, spread, EPS, None, ALU.add)


MOMENT_LINKS = 6


def start_free(eng, *sems):
    for s in sems:
        eng.sem_inc(s, 1)


def setup_phase(nc, d, k):
    with ExitStack() as ctx:
        def sb(name, shape, dt=F32):
            return ctx.enter_context(nc.sbuf_tensor(name, shape, dt))

        def sem(name):
            return ctx.enter_context(nc.semaphore(name))

        small_raw = sb("small_raw", [P, 2, DIM])
        vec_row = sb("vec_row", [1, 4 * HD + DIM])
        ones_row = sb("ones_row", [1, P])
        turn = [ctx.enter_context(nc.psum_tensor(f"turn{i}", [P, HALF], F32)) for i in range(2)]

        x_in, attn_in, uv_in, small_in, vec_in, col_in = (
            sem(n) for n in ("x_in", "attn_in", "uv_in", "small_in", "vec_in", "col_in"))
        ident_zero, ident_done, consts_done, ones_done, ident16_done, uv_scaled = (
            sem(n) for n in ("ident_zero", "ident_done", "consts_done", "ones_done", "ident16_done", "uv_scaled"))
        turn_full = sem("turn_full")
        turn_free = [sem(f"turn_free{i}") for i in range(2)]
        block = ctx.enter_context(nc.Block())

        order = [("vec", 0), ("small", 0)] + [("uv", i) for i in range(CH // 4)]

        @block.sync
        def _(sp):
            sp.dma_start(k["x"][:, :].rearrange("p (n e) -> p n e", e=DIM),
                         d["x"].rearrange("b (n p) e -> p (b n) e", p=P)).then_inc(x_in, 16)
            for i, name in enumerate(("qln_w", "qln_b", "kln_w", "kln_b")):
                sp.dma_start(vec_row[0:1, i * HD:(i + 1) * HD],
                             d[name].rearrange("(a s) -> a s", a=1)).then_inc(vec_in, 16)
            sp.dma_start(vec_row[0:1, 4 * HD:], d["bo"].rearrange("(a s) -> a s", a=1)).then_inc(vec_in, 16)
            for i, name in enumerate(("Wq", "Wk", "Wv")):
                sp.dma_start(k["w_qkv"][:, i * DIM:(i + 1) * DIM], d[name]).then_inc(attn_in, 16)
            sp.dma_start(k["w_o"][:, :], d["Wo"]).then_inc(attn_in, 16)
            sp.dma_start(small_raw[:, 0, :], d["attn_w"]).then_inc(small_in, 16)
            sp.dma_start(small_raw[0:EXPERTS, 1, :], d["gate_w"]).then_inc(small_in, 16)
            for i, name in enumerate(("ln1_g", "ln1_b", "ln2_g", "ln2_b")):
                sp.dma_start(k["ln_cols"][:, i:i + 1], d[name].rearrange("(p a) -> p a", a=1)).then_inc(col_in, 16)
            sp.wait_ge(x_in, 16)
            sp.wait_ge(attn_in, 64)
            sp.wait_ge(col_in, 64)

        @block.scalar
        def _(act):
            uv = k["uv"][:, :].rearrange("p (c z) -> p c z", z=DIM)
            act.dma_start(uv[0:RANK], d["u"].rearrange("(c r) z -> r c z", r=RANK)).then_inc(uv_in, 16)
            act.dma_start(uv[RANK:P], d["v"].rearrange("(c r) z -> r c z", r=RANK)).then_inc(uv_in, 16)
            for n, (kind, i) in enumerate(order):
                if n % 2 == 0:
                    continue
                act.wait_ge(turn_full, n + 1)
                if kind == "small":
                    act.copy(k["attn_wT"][:, :], turn[1][:, 0:DIM])
                    ins = act.copy(k["gate_wT"][:, :], turn[1][:, DIM:DIM + EXPERTS])
                else:
                    ins = act.copy(k["uvT"][:, i * HALF:(i + 1) * HALF], turn[1][:, :])
                ins.then_inc(turn_free[1], 1)

        @block.gpsimd
        def _(pool):
            pool.memset(k["ident"][:, :], 0.0).then_inc(ident_zero, 1)
            pool.memset(k["mask"][:, :], 0.0).then_inc(ident_zero, 1)
            pool.wait_ge(ident_zero, 2)
            pool.affine_select(out=k["ident"][:, :], in_=k["ident"][:, :], compare_op=ALU.not_equal, fill=1.0,
                               base=0, pattern=[[-1, P]], channel_multiplier=1).then_inc(ident_done, 1)
            pool.affine_select(out=k["mask"][:, :], in_=k["mask"][:, :], compare_op=ALU.is_ge, fill=MASKED,
                               base=0, pattern=[[-1, P]], channel_multiplier=1).then_inc(consts_done, 1)

        @block.vector
        def _(dve):
            dve.memset(ones_row[:, :], 1.0).then_inc(ones_done, 1)
            dve.wait_ge(ident_done, 1)
            dve.tensor_copy(k["ident16"][:, :], k["ident"][:, :]).then_inc(ident16_done, 1)
            dve.wait_ge(uv_in, 32)
            dve.tensor_scalar(k["uv"][:, :], k["uv"][:, :], MSG_SCALE, None, ALU.mult).then_inc(uv_scaled, 1)
            for n, (kind, i) in enumerate(order):
                if n % 2 == 1:
                    continue
                dve.wait_ge(turn_full, n + 1)
                if kind == "vec":
                    dve.tensor_scalar(k["ln_rows"][:, 0:2 * HD], turn[0][:, 0:2 * HD], HD ** -0.5, None, ALU.mult)
                    dve.tensor_copy(k["ln_rows"][:, 2 * HD:4 * HD], turn[0][:, 2 * HD:4 * HD])
                    ins = dve.tensor_copy(k["bo_rows"][:, :], turn[0][:, 4 * HD:4 * HD + DIM])
                else:
                    ins = dve.tensor_copy(k["uvT"][:, i * HALF:(i + 1) * HALF], turn[0][:, :])
                ins.then_inc(turn_free[0], 1)

        @block.tensor
        def _(pe):
            pe.wait_ge(ident_done, 1)
            pe.wait_ge(ones_done, 1)
            loaded = {"vec": (vec_in, 80), "small": (small_in, 32), "uv": (uv_scaled, 1)}
            for n, (kind, i) in enumerate(order):
                out = turn[n % 2]
                pe.wait_ge(*loaded[kind])
                pe.wait_ge(turn_free[n % 2], n // 2)
                if kind == "vec":
                    mm = pe.matmul(out[:, 0:4 * HD + DIM], ones_row[:, :], vec_row[:, :], start=True, stop=True)
                elif kind == "small":
                    pe.transpose(out[:, 0:DIM], small_raw[:, 0, :], k["ident"][:, :])
                    mm = pe.transpose(out[:, DIM:DIM + EXPERTS], small_raw[0:EXPERTS, 1, :],
                                      k["ident"][0:EXPERTS, 0:EXPERTS])
                else:
                    for j in range(4):
                        c = 4 * i + j
                        mm = pe.transpose(out[:, j * P:(j + 1) * P], k["uv"][:, c * DIM:(c + 1) * DIM], k["ident"][:, :])
                mm.then_inc(turn_full, 1)


def attention_phase(nc, k):
    STEPS_BATCH = GROUPS * TILES
    SCORE_UNITS = GROUPS * 22
    MAX_UNITS = 43
    UNITS_BATCH = 2 + TILES + GROUPS * (4 + MAX_UNITS + 2 + 2) + 4
    LINKS = MOMENT_LINKS + 2 + 17 + GROUPS * (2 + 2) + 2
    with ExitStack() as ctx:
        def sb(name, shape, dt=F32):
            return ctx.enter_context(nc.sbuf_tensor(name, shape, dt))

        def sem(name):
            return ctx.enter_context(nc.semaphore(name))

        stats, mean, spread, work, dev, rstd = (sb(n, [P, TILES, 6] if n == "a_stats" else [P, TILES]) for n in
                                                ("a_stats", "a_mean", "a_spread", "a_work", "a_dev", "a_rstd"))
        z = sb("a_z", [P, TILES, DIM])
        zT = sb("a_zT", [P, SEQ])
        qk = sb("a_qk", [P, TILES, 2, HEADS, HD])
        prob = [sb(f"a_prob{i}", [P, GROUP, SEQ]) for i in range(2)]
        qk_sq = prob[0][:, 0:2, :].rearrange("p a (g s) -> p (a g) s", s=HD)
        qk_sum, qk_var, qk_dev, qk_rstd = (sb(n, [P, TILES * 2 * HEADS]) for n in ("a_qk_sum", "a_qk_var", "a_qk_dev", "a_qk_rstd"))
        v1 = sb("a_v1", [P, TILES, HEADS, STACK])
        q_st = sb("a_q_st", [P, TILES, HEADS, STACK])
        k_st = sb("a_k_st", [P, TILES, HEADS, STACK])
        qT = [sb(f"a_qT{i}", [P, SEQ], F32R) for i in range(2)]
        qmT = [sb(f"a_qmT{i}", [P, SEQ], F32R) for i in range(2)]
        kT = [sb(f"a_kT{i}", [P, GROUP, SEQ], F32R) for i in range(2)]
        maxima = sb("a_maxima", [P, TILES, GROUP, 2])
        oT = sb("a_oT", [P, SEQ])
        o_den = [sb(f"a_o_den{i}", [P, 4, GROUP]) for i in range(2)]
        o_tok = z[:, :, :].rearrange("p t (h s) -> p t h s", s=HD)
        o_tokT = zT
        proj = [sb(f"a_proj{i}", [P, 4, DIM]) for i in range(2)]

        score = [ctx.enter_context(nc.psum_tensor(f"a_score{i}", [P, SEQ], F32)) for i in range(2)]
        o_acc = ctx.enter_context(nc.psum_tensor("a_o_acc", [P, SEQ], F32))
        unit = [ctx.enter_context(nc.psum_tensor(f"a_unit{i}", [P, HALF], F32)) for i in range(2)]

        cleared, link_sem, var_ready, dev_ready, z_ready, stack_ready, shift_ready = (
            sem(n) for n in ("a_cleared", "a_link", "a_var_ready", "a_dev_ready", "a_z_ready", "a_stack_ready", "a_shift_ready"))
        unit_full, score_full, o_free, kT_cleared = (sem(n) for n in ("a_unit_full", "a_score_full", "a_o_free", "a_kT_cleared"))
        unit_free = [sem(f"a_unit_free{i}") for i in range(2)]
        prob_ready = [sem(f"a_prob_ready{i}") for i in range(2)]
        pv_done = [sem(f"a_pv_done{i}") for i in range(2)]
        block = ctx.enter_context(nc.Block())

        def max_units():
            for qt in range(TILES):
                w = (qt + 1) * P
                if w <= HALF:
                    per = min(GROUP, HALF // w) if w != 384 else 1
                    for h in range(0, GROUP, per):
                        yield qt, range(h, h + per), 0, w, True, 0
                else:
                    for h in range(GROUP):
                        yield qt, range(h, h + 1), 0, HALF, False, 0
                        yield qt, range(h, h + 1), HALF, w - HALF, True, 1

        MAXES = list(max_units())
        assert len(MAXES) == MAX_UNITS

        def max_slice(j):
            return range((j - 1) * 8, min(j * 8, MAX_UNITS)) if 1 <= j <= 6 else range(0)

        def score_units(j):
            per = 1 if j < 4 else 2 if j < 6 else 4
            return [range(h, h + per) for h in range(0, GROUP, per)], SEQ // per

        class Units:

            def __init__(self, b):
                self.b, self.n = b, -1

            def next(self):
                self.n += 1
                return unit[self.n % 2]

            def wait_empty(self, eng):
                eng.wait_ge(unit_free[self.n % 2], self.b * (UNITS_BATCH // 2) + self.n // 2 + 1)

            def wait_full(self, eng):
                eng.wait_ge(unit_full, self.b * UNITS_BATCH + self.n + 1)

            def wait_emptied(self, eng, n):
                eng.wait_ge(unit_free[n % 2], self.b * (UNITS_BATCH // 2) + n // 2 + 2)

            def free(self):
                return unit_free[self.n % 2]

        @block.tensor
        def _(pe):
            pe.wait_ge(cleared, 5)
            with pe.Fori(0, BATCH) as b:
                u = Units(b)
                scores_made = [0]

                def turn(srcs):
                    out = u.next()
                    u.wait_empty(pe)
                    for i, s in enumerate(srcs):
                        mm = pe.transpose(out[:, i * P:(i + 1) * P], s, k["ident"][:, :])
                    mm.then_inc(unit_full, 1)
                    return u.n

                def heads_of(stack, g, t):
                    return stack[:, t, g * GROUP:(g + 1) * GROUP, :].rearrange("p h s -> p (h s)")

                def turn_stacks(g):
                    return [turn([heads_of(s, g, t) for t in range(4 * i, 4 * i + 4)])
                            for s in (q_st, k_st) for i in range(2)]

                def maxima_unit(g, n):
                    qt, heads, first, width, masked, _ = MAXES[n]
                    out = u.next()
                    u.wait_empty(pe)
                    for i, h in enumerate(heads):
                        o = out[:, i * width:(i + 1) * width]
                        mm = pe.matmul(o, qT[g % 2][:, qt * P:(qt + 1) * P], kT[g % 2][:, h, first:first + width],
                                       start=True, stop=not masked)
                        if masked:
                            mm = pe.matmul(o[:, width - P:width], k["ident16"][:, :], k["mask"][:, :],
                                           start=False, stop=True)
                    mm.then_inc(unit_full, 1)

                def turn_shifted(g):
                    pe.wait_ge(shift_ready, b * GROUPS + g + 1)
                    return [turn([heads_of(q_st, g, t) for t in range(4 * i, 4 * i + 4)]) for i in range(2)]

                def scores(g, j):
                    groups, width = score_units(j)
                    lo = j * P
                    base = SEQ - width
                    for heads in groups:
                        s = scores_made[0]
                        scores_made[0] += 1
                        out = score[s % 2]
                        pe.wait_ge(prob_ready[s % 2], b * (SCORE_UNITS // 2) + s // 2 + 1)
                        for i, h in enumerate(heads):
                            at = i * width - base
                            lhs = kT[g % 2][:, h, lo:lo + P]
                            first = True
                            for q0, q1 in ((lo, max(lo, HALF)), (max(lo, HALF), SEQ)):
                                if q0 == q1:
                                    continue
                                mm = pe.matmul(out[:, at + q0:at + q1], lhs, qmT[g % 2][:, q0:q1], start=True, stop=not first)
                                if first:
                                    mm = pe.matmul(out[:, at + lo:at + lo + P], k["mask"][:, :], k["ident16"][:, :],
                                                   start=False, stop=True)
                                first = False
                        mm.then_inc(score_full, 1)

                def weigh(g, j):
                    step = g * TILES + j
                    if j == 0:
                        pe.wait_ge(o_free, b * GROUPS + g + 1)
                    done = scores_done[step]
                    for i in range(2):
                        pe.wait_ge(prob_ready[i], b * (SCORE_UNITS // 2) + (done + 1 - i) // 2 + 1)
                    lo = j * P
                    for q0, q1 in ((lo, max(lo, HALF)), (max(lo, HALF), SEQ)):
                        if q0 == q1:
                            continue
                        for h in range(GROUP):
                            mm = pe.matmul(o_acc[h * STACK:(h + 1) * STACK, q0:q1], v1[:, j, g * GROUP + h, :],
                                           prob[step % 2][:, h, q0:q1], start=(j == 0),
                                           stop=(j == (3 if q1 == HALF else TILES - 1)))
                    mm.then_inc(pv_done[step % 2], 1)

                def turn_out(g):
                    pe.wait_ge(o_free, b * GROUPS + g + 2)
                    for i in range(2):
                        out = u.next()
                        u.wait_empty(pe)
                        for t in range(4):
                            mm = pe.transpose(out[:, t * P:(t + 1) * P], oT[:, (4 * i + t) * P:(4 * i + t + 1) * P], k["ident"][:, :])
                        mm.then_inc(unit_full, 1)
                    return u.n

                scores_done = []
                n = 0
                for g in range(GROUPS):
                    for j in range(TILES):
                        n += len(score_units(j)[0])
                        scores_done.append(n)

                pe.wait_ge(z_ready, b + 1)
                for i in range(2):
                    turn([z[:, t, :] for t in range(4 * i, 4 * i + 4)])
                z0 = u.n - 1
                for t in range(TILES):
                    out = u.next()
                    u.wait_emptied(pe, z0 + t // 4)
                    u.wait_empty(pe)
                    pe.matmul(out[:, 0:3 * DIM], zT[:, t * P:(t + 1) * P], k["w_qkv"][:, :], start=True, stop=True)\
                      .then_inc(unit_full, 1)
                pe.wait_ge(stack_ready, b + 1)
                for n in turn_stacks(0):
                    u.wait_emptied(pe, n)
                for n in range(MAX_UNITS):
                    maxima_unit(0, n)
                shifted = turn_shifted(0)
                for g in range(GROUPS):
                    for n in shifted:
                        u.wait_emptied(pe, n)
                    for j in range(TILES):
                        scores(g, j)
                        if g + 1 < GROUPS:
                            if j == 0:
                                stacks = turn_stacks(g + 1)
                            if j == 1:
                                for n in stacks:
                                    u.wait_emptied(pe, n)
                            for n in max_slice(j):
                                maxima_unit(g + 1, n)
                            if j == 7:
                                shifted = turn_shifted(g + 1)
                        if j == 2 and g > 0:
                            turn_out(g - 1)
                        if j >= 1:
                            weigh(g, j - 1)
                    weigh(g, TILES - 1)
                last = turn_out(GROUPS - 1)
                for n in (last - 1, last):
                    u.wait_emptied(pe, n)
                out_units = [turn([o_tok[:, t, :, :].rearrange("p h s -> p (h s)") for t in range(4 * i, 4 * i + 4)])
                             for i in range(2)]
                for i in range(2):
                    u.wait_emptied(pe, out_units[i])
                    out = u.next()
                    u.wait_empty(pe)
                    for t in range(4):
                        mm = pe.matmul(out[:, t * P:(t + 1) * P], o_tokT[:, (4 * i + t) * P:(4 * i + t + 1) * P],
                                       k["w_o"][:, :], start=True, stop=True)
                    mm.then_inc(unit_full, 1)
                assert u.n + 1 == UNITS_BATCH, (u.n + 1, UNITS_BATCH)

        @block.scalar
        def _(act):
            act.wait_ge(kT_cleared, 1)
            with act.Fori(0, BATCH) as b:
                u = Units(b)
                s = 0
                act.wait_ge(var_ready, 2 * b + 1)
                act.activation(dev[:, :], spread[:, :], ACT.Sqrt).then_inc(dev_ready, 1)
                u.n += 2
                for t in range(TILES):
                    src = u.next()
                    u.wait_full(act)
                    act.copy(qk[:, t, :, :, :].rearrange("p a h s -> p (a h s)"), src[:, 0:2 * DIM])
                    act.copy(v1[:, t, :, 0:HD], src[:, 2 * DIM:3 * DIM].rearrange("p (h s) -> p h s", s=HD))\
                       .then_inc(u.free(), 1)
                act.wait_ge(var_ready, 2 * b + 2)
                act.activation(qk_dev[:, :], qk_var[:, :], ACT.Sqrt).then_inc(dev_ready, 1)

                def spread_keys(g):
                    u.n += 2
                    for i in range(2):
                        src = u.next()
                        u.wait_full(act)
                        for h in range(GROUP):
                            rows = slice(h * STACK, (h + 1) * STACK)
                            ins = act.copy(kT[g % 2][rows, h, i * HALF:(i + 1) * HALF], src[rows, :])
                        ins.then_inc(u.free(), 1)

                spread_keys(0)
                u.n += MAX_UNITS + 2
                for g in range(GROUPS):
                    for j in range(TILES):
                        step = g * TILES + j
                        groups, width = score_units(j)
                        lo, base = j * P, SEQ - width
                        act.wait_ge(pv_done[step % 2], b * (STEPS_BATCH // 2) + step // 2 + 1)
                        for heads in groups:
                            act.wait_ge(score_full, b * SCORE_UNITS + s + 1)
                            src = score[s % 2][:, :].rearrange("p (h q) -> p h q", q=width)
                            act.activation(prob[step % 2][:, heads[0]:heads[-1] + 1, lo:SEQ], src[:, :, lo - base:width],
                                           ACT.Exp).then_inc(prob_ready[s % 2], 1)
                            s += 1
                        if g + 1 < GROUPS:
                            if j == 0:
                                spread_keys(g + 1)
                            u.n += len(max_slice(j))
                            if j == 7:
                                u.n += 2
                        if j == 2 and g > 0:
                            u.n += 2
                            act.wait_ge(unit_full, b * UNITS_BATCH + u.n + 1)
                    act.wait_ge(pv_done[1], b * (STEPS_BATCH // 2) + (g + 1) * TILES // 2 + 1)
                    act.copy(oT[:, :], o_acc[:, :]).then_inc(o_free, 1)
                u.n += 2
                for i in range(2):
                    src = u.next()
                    u.wait_full(act)
                    act.copy(o_tokT[:, i * HALF:(i + 1) * HALF], src[:, :]).then_inc(u.free(), 1)
                u.n += 2
                assert u.n + 1 == UNITS_BATCH and s == SCORE_UNITS

        @block.gpsimd
        def _(pool):
            start_free(pool, *unit_free, *prob_ready, *pv_done, o_free)
            pool.memset(k_st[:, :, :, :], 0.0).then_inc(cleared, 1)
            pool.wait_ge(cleared, 1)
            pool.memset(k_st[:, :, :, 3 * HD:3 * HD + 2], 1.0).then_inc(cleared, 1)
            pool.memset(v1[:, :, :, HD + 1:STACK], 0.0).then_inc(cleared, 1)
            pool.memset(v1[:, :, :, HD:HD + 1], 1.0).then_inc(cleared, 1)
            pool.memset(q_st[:, :, :, :], 0.0).then_inc(cleared, 1)

        @block.vector
        def _(dve):
            for i in range(2):
                ins = dve.memset(kT[i][:, :, :].bitcast(F32), 0.0)
            ins.then_inc(kT_cleared, 1)
            dve.wait_ge(cleared, 5)
            with dve.Fori(0, BATCH) as b:
                u = Units(b)
                link = Link(dve, link_sem, b * LINKS)

                def x_tile(t):
                    return k["x"][:, ds((b * TILES + t) * DIM, DIM)]
                for t in range(TILES):
                    ins = dve.bn_stats(stats[:, t, :], x_tile(t))
                link(ins)
                row_moments(dve, link, stats, mean[:, :], spread[:, :], work[:, :], TILES).then_inc(var_ready, 1)
                dve.wait_ge(dev_ready, 2 * b + 1)
                link(dve.reciprocal(rstd[:, :], dev[:, :]))
                for t in range(TILES):
                    ins = dve.tensor_scalar(z[:, t, :], x_tile(t), mean[:, t:t + 1], rstd[:, t:t + 1], ALU.subtract, ALU.mult)
                ins.then_inc(z_ready, 1)
                for i in range(2):
                    src = u.next()
                    u.wait_full(dve)
                    dve.tensor_copy(zT[:, i * HALF:(i + 1) * HALF], src[:, :]).then_inc(u.free(), 1)

                u.n += TILES
                for n in (u.n - 1, u.n):
                    u.wait_emptied(dve, n)
                flat = qk[:, :, :, :, :].rearrange("p t a h s -> p (t a h) s")
                rows = [P, TILES * 2 * HEADS, HD]
                link(dve.tensor_reduce(qk_sum[:, :], flat, AX.X, ALU.add))
                link(dve.tensor_scalar(qk_sum[:, :], qk_sum[:, :], 1.0 / HD, None, ALU.mult))
                link(dve.tensor_tensor(flat, flat, qk_sum[:, :].unsqueeze(2).broadcast_to(rows), ALU.subtract))
                link(dve.tensor_tensor(qk_sq[:, :, :], flat, flat, ALU.mult))
                link(dve.tensor_reduce(qk_var[:, :], qk_sq[:, :, :], AX.X, ALU.add))
                dve.tensor_scalar(qk_var[:, :], qk_var[:, :], 1.0 / HD, EPS, ALU.mult, ALU.add).then_inc(var_ready, 1)
                dve.wait_ge(dev_ready, 2 * b + 2)
                link(dve.reciprocal(qk_rstd[:, :], qk_dev[:, :]))
                link(dve.tensor_tensor(flat, flat, qk_rstd[:, :].unsqueeze(2).broadcast_to(rows), ALU.mult))
                for a in range(2):
                    one = qk[:, :, a, :, :]
                    for i, op in enumerate((ALU.mult, ALU.add)):
                        w = k["ln_rows"][:, (2 * a + i) * HD:(2 * a + i + 1) * HD]
                        link(dve.tensor_tensor(one, one, w.unsqueeze(1).unsqueeze(1).broadcast_to([P, TILES, HEADS, HD]), op))
                q, kk = qk[:, :, 0, :, :], qk[:, :, 1, :, :]
                link(dve.tensor_copy(q_st[:, :, :, 0:HD].bitcast(F32R), q))
                link(dve.tensor_copy(k_st[:, :, :, 0:HD].bitcast(F32R), kk))
                link(dve.tensor_tensor(q_st[:, :, :, HD:2 * HD].bitcast(F32R), q, q_st[:, :, :, 0:HD], ALU.subtract))
                link(dve.tensor_copy(q_st[:, :, :, 2 * HD:3 * HD], q_st[:, :, :, 0:HD]))
                link(dve.tensor_tensor(k_st[:, :, :, 2 * HD:3 * HD].bitcast(F32R), kk, k_st[:, :, :, 0:HD], ALU.subtract))
                link(dve.tensor_copy(k_st[:, :, :, HD:2 * HD], k_st[:, :, :, 0:HD]))
                dve.memset(q_st[:, :, :, 3 * HD:3 * HD + 2], 0.0).then_inc(stack_ready, 1)

                def empty_queries(dst):
                    for i in range(2):
                        src = u.next()
                        u.wait_full(dve)
                        dve.tensor_copy(dst[:, i * HALF:(i + 1) * HALF], src[:, :]).then_inc(u.free(), 1)

                def maxima_unit(n):
                    qt, heads, _, width, _, part = MAXES[n]
                    src = u.next()
                    u.wait_full(dve)
                    dve.tensor_reduce(maxima[:, qt, heads[0]:heads[-1] + 1, part],
                                      src[:, 0:len(heads) * width].rearrange("p (h w) -> p h w", w=width),
                                      AX.X, ALU.max).then_inc(u.free(), 1)

                def shift(g):
                    u.wait_emptied(dve, u.n)
                    link(dve.tensor_tensor(maxima[:, 4:TILES, :, 0], maxima[:, 4:TILES, :, 0], maxima[:, 4:TILES, :, 1], ALU.max))
                    heads = slice(g * GROUP, (g + 1) * GROUP)
                    hi, lo = q_st[:, :, heads, 3 * HD], q_st[:, :, heads, 3 * HD + 1]
                    link(dve.tensor_scalar(hi.bitcast(F32R), maxima[:, :, :, 0], -1.0, None, ALU.mult))
                    dve.scalar_tensor_tensor(out=lo.bitcast(F32R), in0=maxima[:, :, :, 0], scalar=-1.0, in1=hi,
                                             op0=ALU.mult, op1=ALU.subtract).then_inc(shift_ready, 1)
                    empty_queries(qmT[g % 2])

                def normalise(g):
                    for i in range(2):
                        src = u.next()
                        u.wait_full(dve)
                        o = src[:, :].rearrange("p (t h s) -> p t h s", t=4, s=STACK)
                        link(dve.reciprocal(o_den[i][:, :, :], o[:, :, :, HD]))
                        ins = dve.tensor_tensor(o_tok[:, 4 * i:4 * i + 4, g * GROUP:(g + 1) * GROUP, :], o[:, :, :, 0:HD],
                                                o_den[i][:, :, :].unsqueeze(3).broadcast_to([P, 4, GROUP, HD]), ALU.mult)
                        ins.then_inc(u.free(), 1)

                empty_queries(qT[0])
                u.n += 2
                for n in range(MAX_UNITS):
                    maxima_unit(n)
                shift(0)
                for g in range(GROUPS):
                    for j in range(TILES):
                        if g + 1 < GROUPS:
                            if j == 0:
                                empty_queries(qT[(g + 1) % 2])
                                u.n += 2
                            for n in max_slice(j):
                                maxima_unit(n)
                            if j == 7:
                                shift(g + 1)
                        if j == 2 and g > 0:
                            normalise(g - 1)
                normalise(GROUPS - 1)
                u.n += 2
                for i in range(2):
                    src = u.next()
                    u.wait_full(dve)
                    o = src[:, :].rearrange("p (t e) -> p t e", e=DIM)
                    bo = k["bo_rows"][:, :].unsqueeze(1).broadcast_to([P, 4, DIM])
                    link(dve.tensor_tensor(proj[i][:, :, :], o, bo, ALU.add))
                    x4 = k["x"][:, ds(b * TILES * DIM + i * HALF, HALF)]
                    ins = dve.tensor_tensor(x4, x4, proj[i][:, :, :].rearrange("p t e -> p (t e)"), ALU.add)
                    ins.then_inc(u.free(), 1)
                assert u.n + 1 == UNITS_BATCH
                assert link.n == LINKS, (link.n, LINKS)


def moe_phase(nc, k, name, d=None):
    GROUPS_ALL = ALL // GTOK
    COLS = GTOK * DIM
    with ExitStack() as ctx:
        def sb(n, shape, dt=F32):
            return ctx.enter_context(nc.sbuf_tensor(f"{name}_{n}", shape, dt))

        def sem(n):
            return ctx.enter_context(nc.semaphore(f"{name}_{n}"))

        def pair(n):
            return [ctx.enter_context(nc.psum_tensor(f"{name}_{n}{i}", [P, HALF], F32)) for i in range(2)]

        stats = sb("stats", [P, ALL, 6])
        mean, spread, work, dev, rstd = (sb(n, [P, ALL]) for n in ("mean", "spread", "work", "dev", "rstd"))
        h = sb("h", [P, ALL * DIM])
        norm = [sb(f"norm{i}", [P, COLS]) for i in range(2)]
        normT = [sb(f"normT{i}", [P, COLS]) for i in range(2)]
        tT = sb("tT", [P, ALL * P])
        logits, pick, other = (sb(n, [P, ALL, EXPERTS]) for n in ("logits", "pick", "other"))
        comb = sb("comb", [P, ALL, EXPERTS])
        rank = sb("rank", [P, EXPERTS])
        best, second, first_at, ratio, share = (sb(n, [P, ALL]) for n in ("best", "second", "first_at", "ratio", "share"))
        silu = [sb(f"silu{i}", [P, HALF]) for i in range(2)]
        inner = [sb(f"inner{i}", [P, HALF]) for i in range(2)]
        gate, up, out = pair("gate"), pair("up"), pair("out")
        if d:
            gate_raw, up_raw = sb("gate_raw", [P, UNITS, DIM]), sb("up_raw", [P, UNITS, DIM])
            down_raw = sb("down_raw", [P, EXPERTS, INTER])
            raw_in = [sem(f"raw_in{i}") for i in range(3)]
            weight_full, weight_free = sem("weight_full"), sem("weight_free")

        link_sem, stats_done, var_ready, dev_ready, y_done, norm_ready, turn_full, normT_ready = (
            sem(n) for n in ("link", "stats_done", "var_ready", "dev_ready", "y_done", "norm_ready", "turn_full", "normT_ready"))
        product_full, product_free, gap_ready, ratio_ready, gu_full = (
            sem(n) for n in ("product_full", "product_free", "gap_ready", "ratio_ready", "gu_full"))
        tT_ready, silu_ready, inner_ready, down_done, out_free = (
            [sem(f"{n}{i}") for i in range(2)] for n in ("tT_ready", "silu_ready", "inner_ready", "down_done", "out_free"))
        block = ctx.enter_context(nc.Block())

        if d:
            @block.sync
            def _(sp):
                sp.dma_start(gate_raw[:, :, :], d["gate_proj"].rearrange("e (n p) h -> p (e n) h", p=P)).then_inc(raw_in[0], 16)
                sp.dma_start(up_raw[:, :, :], d["up_proj"].rearrange("e (n p) h -> p (e n) h", p=P)).then_inc(raw_in[1], 16)
                sp.dma_start(down_raw[:, :, :], d["down_proj"].rearrange("e h i -> h e i")).then_inc(raw_in[2], 16)

        def turned_weights():
            for m, dst in enumerate((k["w_gate"], k["w_up"], k["w_down"])):
                for n in range(0, UNITS, 4):
                    yield m, n, dst[:, n * P:(n + 4) * P]

        def raw_block(m, n):
            return down_raw[:, n // BLOCKS, (n % BLOCKS) * P:(n % BLOCKS + 1) * P] if m == 2 else (gate_raw, up_raw)[m][:, n, :]

        @block.tensor
        def _(pe):
            for i, (m, n, _) in enumerate(turned_weights() if d else ()):
                pe.wait_ge(raw_in[m], 16)
                if i >= 2:
                    pe.wait_ge(weight_free, i - 1)
                for j in range(4):
                    mm = pe.transpose(out[i % 2][:, j * P:(j + 1) * P], raw_block(m, n + j), k["ident"][:, :])
                mm.then_inc(weight_full, 1)
            for turn_no, w in enumerate((k["attn_wT"], k["gate_wT"])):
                cols = w.shape[1]
                with pe.Fori(0, GROUPS_ALL // 2) as gg:
                    before = turn_no * GROUPS_ALL + 2 * gg
                    for i in range(2):
                        pe.wait_ge(norm_ready, before + i + 1)
                        pe.wait_ge(normT_ready, before + 1)
                        for t in range(GTOK):
                            mm = pe.transpose(gate[i][:, t * P:(t + 1) * P], norm[i][:, t * DIM:(t + 1) * DIM], k["ident"][:, :])
                        mm.then_inc(turn_full, 1)
                    for i in range(2):
                        pe.wait_ge(normT_ready, before + i + 2)
                        pe.wait_ge(product_free, before + 1)
                        for t in range(GTOK):
                            mm = pe.matmul(up[i][:, t * cols:(t + 1) * cols], normT[i][:, t * P:(t + 1) * P], w[:, :],
                                           start=True, stop=True)
                        mm.then_inc(product_full, 1)
            if d:
                pe.wait_ge(weight_free, 3 * UNITS // 4)
            pe.wait_ge(product_free, 2 * GROUPS_ALL + 1)
            for i in range(2):
                pe.wait_ge(tT_ready[i], GROUPS_ALL // 2 + 1)
            with pe.Fori(0, GROUPS_ALL) as g:
                def down(n):
                    e, ib = divmod(n, BLOCKS)
                    pe.wait_ge(inner_ready[n % 2], g * (UNITS // 2) + n // 2 + 2)
                    if ib == 0:
                        pe.wait_ge(out_free[e % 2], g * (EXPERTS // 2) + e // 2 + 1)
                    for t in range(GTOK):
                        mm = pe.matmul(out[e % 2][:, t * DIM:(t + 1) * DIM], inner[n % 2][:, t * P:(t + 1) * P],
                                       k["w_down"][:, n * DIM:(n + 1) * DIM], start=(ib == 0 and t == 0), stop=(ib == BLOCKS - 1),
                                       skip_group_check=True)
                    mm.then_inc(down_done[n % 2], 1)
                for n in range(UNITS):
                    tokens = tT[:, ds(g * HALF, HALF)]
                    pe.wait_ge(silu_ready[n % 2], g * (UNITS // 2) + n // 2 + 1)
                    pe.matmul(gate[n % 2][:, :], k["w_gate"][:, n * P:(n + 1) * P], tokens, start=True, stop=True)
                    pe.wait_ge(inner_ready[n % 2], g * (UNITS // 2) + n // 2 + 1)
                    pe.matmul(up[n % 2][:, :], k["w_up"][:, n * P:(n + 1) * P], tokens, start=True, stop=True).then_inc(gu_full, 1)
                    if n:
                        down(n - 1)
                down(UNITS - 1)

        @block.scalar
        def _(act):
            for i in range(3):
                if i == 2 and d:
                    for n, (_, _, dst) in enumerate(turned_weights()):
                        act.wait_ge(weight_full, n + 1)
                        act.copy(dst, out[n % 2][:, :]).then_inc(weight_free, 1)
                act.wait_ge(var_ready, i + 1)
                act.activation(dev[:, :], spread[:, :], ACT.Sqrt).then_inc(dev_ready, 1)
            with act.Fori(0, GROUPS_ALL // 2) as gg:
                for i in range(2):
                    act.wait_ge(normT_ready, GROUPS_ALL + 2 * gg + i + 2)
                    act.copy(tT[:, ds((2 * gg + i) * HALF, HALF)], normT[i][:, :]).then_inc(tT_ready[i], 1)
            act.wait_ge(gap_ready, 1)
            act.activation(ratio[:, :], second[:, :], ACT.Exp).then_inc(ratio_ready, 1)
            with act.Fori(0, GROUPS_ALL) as g:
                for n in range(UNITS):
                    act.wait_ge(gu_full, g * UNITS + n + 1)
                    act.wait_ge(inner_ready[n % 2], g * (UNITS // 2) + n // 2 + 1)
                    act.activation(silu[n % 2][:, :], gate[n % 2][:, :], ACT.Silu).then_inc(silu_ready[n % 2], 1)

        @block.gpsimd
        def _(pool):
            start_free(pool, *tT_ready, *silu_ready, *inner_ready, *down_done, *out_free, normT_ready, product_free)

        @block.vector
        def _(dve):
            link = Link(dve, link_sem)
            for e in range(EXPERTS):
                ins = dve.memset(rank[:, e:e + 1], float(EXPERTS - e))
            link(ins)

            def moments(src, i):
                flat = stats[:, :, :].rearrange("p t s -> p (t s)")
                with dve.Fori(0, GROUPS_ALL) as g:
                    for t in range(GTOK):
                        at = g * GTOK + t
                        ins = dve.bn_stats(flat[:, ds(at * 6, 6)], src[:, ds(at * DIM, DIM)])
                    ins.then_inc(stats_done, 1)
                dve.wait_ge(stats_done, GROUPS_ALL * (i + 1))
                row_moments(dve, link, stats, mean[:, :], spread[:, :], work[:, :], ALL).then_inc(var_ready, 1)
                dve.wait_ge(dev_ready, i + 1)
                link(dve.reciprocal(rstd[:, :], dev[:, :]))

            def normalise(dst, src, g, t):
                at = g * GTOK + t
                return dve.tensor_scalar(dst, src[:, ds(at * DIM, DIM)], mean[:, ds(at, 1)], rstd[:, ds(at, 1)],
                                         ALU.subtract, ALU.mult)

            def turned(gg, turn_no):
                before = turn_no * GROUPS_ALL + 2 * gg
                for i in range(2):
                    for t in range(GTOK):
                        ins = normalise(norm[i][:, t * DIM:(t + 1) * DIM], h, 2 * gg + i, t)
                    ins.then_inc(norm_ready, 1)
                for i in range(2):
                    dve.wait_ge(turn_full, before + i + 1)
                    if turn_no:
                        dve.wait_ge(tT_ready[i], gg + 1)
                    dve.tensor_scalar(normT[i][:, :], gate[i][:, :], k["ln_cols"][:, 2 * turn_no:2 * turn_no + 1],
                                      k["ln_cols"][:, 2 * turn_no + 1:2 * turn_no + 2], ALU.mult, ALU.add).then_inc(normT_ready, 1)

            moments(k["x"], 0)
            with dve.Fori(0, GROUPS_ALL) as g:
                for t in range(GTOK):
                    ins = normalise(h[:, ds((g * GTOK + t) * DIM, DIM)], k["x"], g, t)
                ins.then_inc(y_done, 1)
            dve.wait_ge(y_done, GROUPS_ALL)
            moments(h, 1)
            with dve.Fori(0, GROUPS_ALL // 2) as gg:
                turned(gg, 0)
                for i in range(2):
                    dve.wait_ge(product_full, 2 * gg + i + 1)
                    mine = h[:, ds((2 * gg + i) * COLS, COLS)]
                    dve.tensor_tensor(mine, mine, up[i][:, :], ALU.add).then_inc(product_free, 1)
            dve.wait_ge(product_free, GROUPS_ALL + 1)
            moments(h, 2)
            with dve.Fori(0, GROUPS_ALL // 2) as gg:
                turned(gg, 1)
                for i in range(2):
                    g = 2 * gg + i
                    xs = k["x"][:, ds(g * COLS, COLS)]
                    dve.tensor_tensor(xs, xs, h[:, ds(g * COLS, COLS)], ALU.add)
                    dve.wait_ge(product_full, GROUPS_ALL + g + 1)
                    dve.tensor_copy(logits[:, :, :].rearrange("p t e -> p (t e)")[:, ds(g * GTOK * EXPERTS, GTOK * EXPERTS)],
                                    up[i][:, 0:GTOK * EXPERTS]).then_inc(product_free, 1)
            dve.wait_ge(product_free, 2 * GROUPS_ALL + 1)

            def over_experts(a):
                return a[:, :].unsqueeze(2).broadcast_to([P, ALL, EXPERTS])

            def pick_first(dst, values, top):
                link(dve.tensor_reduce(top[:, :], values[:, :, :], AX.X, ALU.max))
                link(dve.tensor_tensor(dst[:, :, :], values[:, :, :], over_experts(top), ALU.is_equal))
                ranks = rank[:, :].unsqueeze(1).broadcast_to([P, ALL, EXPERTS])
                link(dve.tensor_tensor(dst[:, :, :], dst[:, :, :], ranks, ALU.mult))
                link(dve.tensor_reduce(first_at[:, :], dst[:, :, :], AX.X, ALU.max))
                link(dve.tensor_tensor(dst[:, :, :], dst[:, :, :], over_experts(first_at), ALU.is_equal))

            pick_first(pick, logits, best)
            link(dve.scalar_tensor_tensor(out=logits[:, :, :], in0=pick[:, :, :], scalar=MASKED, in1=logits[:, :, :],
                                          op0=ALU.mult, op1=ALU.add))
            pick_first(other, logits, second)
            dve.tensor_tensor(second[:, :], second[:, :], best[:, :], ALU.subtract).then_inc(gap_ready, 1)
            dve.wait_ge(ratio_ready, 1)
            link(dve.tensor_scalar(share[:, :], ratio[:, :], 1.0, None, ALU.add))
            link(dve.reciprocal(share[:, :], share[:, :]))
            link(dve.tensor_tensor(ratio[:, :], ratio[:, :], share[:, :], ALU.mult))
            link(dve.tensor_tensor(pick[:, :, :], pick[:, :, :], over_experts(share), ALU.mult))
            link(dve.tensor_tensor(other[:, :, :], other[:, :, :], over_experts(ratio), ALU.mult))
            link(dve.tensor_tensor(comb[:, :, :], pick[:, :, :], other[:, :, :], ALU.add))

            weight = comb[:, :, :].rearrange("p t e -> p (t e)")
            with dve.Fori(0, GROUPS_ALL) as g:
                def add_expert(e):
                    last = (e + 1) * BLOCKS - 1
                    dve.wait_ge(down_done[last % 2], g * (UNITS // 2) + last // 2 + 2)
                    if e:
                        dve.wait_ge(out_free[(e - 1) % 2], g * (EXPERTS // 2) + (e - 1) // 2 + 2)
                    for t in range(GTOK):
                        at = g * GTOK + t
                        xs = k["x"][:, ds(at * DIM, DIM)]
                        ins = dve.scalar_tensor_tensor(out=xs, in0=out[e % 2][:, t * DIM:(t + 1) * DIM],
                                                       scalar=weight[:, ds(at * EXPERTS + e, 1)], in1=xs,
                                                       op0=ALU.mult, op1=ALU.add)
                    ins.then_inc(out_free[e % 2], 1)
                for n in range(UNITS):
                    e, ib = divmod(n, BLOCKS)
                    dve.wait_ge(silu_ready[n % 2], g * (UNITS // 2) + n // 2 + 2)
                    dve.wait_ge(down_done[n % 2], g * (UNITS // 2) + n // 2 + 1)
                    dve.tensor_tensor(inner[n % 2][:, :], silu[n % 2][:, :], up[n % 2][:, :], ALU.mult).then_inc(inner_ready[n % 2], 1)
                    if ib == 1 and e:
                        add_expert(e - 1)
                add_expert(EXPERTS - 1)


def message_phase(nc, k):
    PREP = 6
    UNITS_BATCH = 2 + PREP * CH + 2 + 2
    LINKS = MOMENT_LINKS + 2
    STEPS = CH * TILES
    with ExitStack() as ctx:
        def sb(n, shape, dt=F32):
            return ctx.enter_context(nc.sbuf_tensor(f"m_{n}", shape, dt))

        def sem(n):
            return ctx.enter_context(nc.semaphore(f"m_{n}"))

        stats = sb("stats", [P, TILES, 6])
        mean, spread, work, dev, rstd = (sb(n, [P, TILES]) for n in ("mean", "spread", "work", "dev", "rstd"))
        z = sb("z", [P, TILES, DIM])
        zT = sb("zT", [P, SEQ])
        twice = [sb(f"twice{i}", [P, 2, 2, RANK]) for i in range(2)]
        u_st = [sb(f"u_st{i}", [P, SEQ], F32R) for i in range(2)]
        v_hi = [sb(f"v_hi{i}", [P, SEQ], F32R) for i in range(2)]
        v_lo = [sb(f"v_lo{i}", [P, SEQ], F32R) for i in range(2)]
        uv_tok = [sb(f"uv_tok{i}", [P, TILES, 2, RANK]) for i in range(2)]
        f_sig = [sb(f"f_sig{i}", [P, SEQ]) for i in range(2)]
        t_sig = [sb(f"t_sig{i}", [P, SEQ]) for i in range(2)]
        vuT = sb("vuT", [P, CH * SEQ])
        msgT = zT
        f_ps, t_ps, vu_ps = (ctx.enter_context(nc.psum_tensor(f"m_{n}", [P, SEQ], F32)) for n in ("f_ps", "t_ps", "vu_ps"))
        unit = [ctx.enter_context(nc.psum_tensor(f"m_unit{i}", [P, HALF], F32)) for i in range(2)]

        link_sem, var_ready, dev_ready, z_ready, twice_ready, unit_full, hi_ready = (
            sem(n) for n in ("link", "var_ready", "dev_ready", "z_ready", "twice_ready", "unit_full", "hi_ready"))
        f_full, t_full, f_ready, t_ready, vu_free = (sem(n) for n in ("f_full", "t_full", "f_ready", "t_ready", "vu_free"))
        unit_free = [sem(f"unit_free{i}") for i in range(2)]
        used = [sem(f"used{i}") for i in range(2)]
        block = ctx.enter_context(nc.Block())

        class Units:

            def __init__(self, base, halves):
                self.base, self.halves, self.n = base, halves, -1

            def next(self):
                self.n += 1
                return unit[self.n % 2]

            def wait_empty(self, eng):
                eng.wait_ge(unit_free[self.n % 2], self.halves + self.n // 2 + 1)

            def wait_full(self, eng):
                eng.wait_ge(unit_full, self.base + self.n + 1)

            def wait_emptied(self, eng, n):
                eng.wait_ge(unit_free[n % 2], self.halves + n // 2 + 2)

            def free(self):
                return unit_free[self.n % 2]

        def units_at(b, pairs):
            return Units(b * UNITS_BATCH + pairs * 2, b * (UNITS_BATCH // 2) + pairs)

        def channels(eng, b, body):
            with eng.Fori(0, CH // 2 - 1) as cc:
                for p in range(2):
                    body(b, 2 * cc + p, p, False)
            for p in range(2):
                body(b, CH - 2 + p, p, True)

        @block.tensor
        def _(pe):
            def prepare(u, i, c, p, b):
                out = u.next()
                u.wait_empty(pe)
                if i == 0:
                    pe.wait_ge(twice_ready, b * CH + c + 1)
                if i < 4:
                    mm = pe.matmul(out[:, :], twice[p][:, i // 2, :, :].rearrange("p d r -> p (d r)"),
                                   zT[:, (i % 2) * HALF:(i % 2 + 1) * HALF], start=True, stop=True)
                else:
                    for t in range(4):
                        tile = (i - 4) * 4 + t
                        mm = pe.matmul(out[:, t * P:(t + 1) * P], zT[:, tile * P:(tile + 1) * P],
                                       k["uvT"][:, ds(c * P, P)], start=True, stop=True)
                mm.then_inc(unit_full, 1)

            def blocks(b, c, i, p):
                step = (b * CH + c) * TILES + i
                rows = slice(i * P, (i + 1) * P)
                pe.wait_ge(f_ready, step + 1)
                for n in range(2):
                    cols = slice(n * HALF, (n + 1) * HALF)
                    pe.matmul(f_ps[:, cols], u_st[p][:, rows], v_hi[p][:, cols], start=True, stop=False)
                    mm = pe.matmul(f_ps[:, cols], u_st[p][:, rows], v_lo[p][:, cols], start=False, stop=True)
                mm.then_inc(f_full, 1)
                pe.wait_ge(t_ready, step + 1)
                for n in range(2):
                    cols = slice(n * HALF, (n + 1) * HALF)
                    pe.matmul(t_ps[:, cols], v_hi[p][:, rows], u_st[p][:, cols], start=True, stop=False)
                    mm = pe.matmul(t_ps[:, cols], v_lo[p][:, rows], u_st[p][:, cols], start=False, stop=True)
                mm.then_inc(t_full, 1)

            def products(b, c, i, p):
                step = (b * CH + c) * TILES + i
                if i == 0:
                    pe.wait_ge(vu_free, b * CH + c + 1)
                pe.wait_ge(f_ready, step + 2)
                pe.wait_ge(t_ready, step + 2)
                for n in range(2):
                    cols = slice(n * HALF, (n + 1) * HALF)
                    pe.matmul(vu_ps[0:RANK, cols], uv_tok[p][:, i, 1, :], t_sig[i % 2][:, cols], start=(i == 0), stop=(i == TILES - 1))
                    mm = pe.matmul(vu_ps[RANK:P, cols], uv_tok[p][:, i, 0, :], f_sig[i % 2][:, cols], start=(i == 0), stop=(i == TILES - 1))
                mm.then_inc(used[i % 2], 1)

            with pe.Fori(0, BATCH) as b:
                u = units_at(b, 0)
                pe.wait_ge(z_ready, b + 1)
                for i in range(2):
                    out = u.next()
                    u.wait_empty(pe)
                    for t in range(4):
                        mm = pe.transpose(out[:, t * P:(t + 1) * P], z[:, 4 * i + t, :], k["ident"][:, :])
                    mm.then_inc(unit_full, 1)
                for n in (0, 1):
                    u.wait_emptied(pe, n)
                for i in range(PREP):
                    prepare(u, i, 0, 0, b)
                for n in (u.n - 1, u.n):
                    u.wait_emptied(pe, n)
                blocks(b, 0, 0, 0)

                def body(b, c, p, last_pair):
                    last = last_pair and p == 1
                    u = units_at(b, 1 + PREP // 2 * (c + 1))
                    for i in range(TILES):
                        if i < TILES - 1:
                            blocks(b, c, i + 1, p)
                        elif not last:
                            for n in (u.n - 1, u.n):
                                u.wait_emptied(pe, n)
                            blocks(b, c + 1, 0, 1 - p)
                        if i < PREP and not last:
                            prepare(u, i, c + 1, 1 - p, b)
                        products(b, c, i, p)
                channels(pe, b, body)

                u = units_at(b, 1 + PREP // 2 * CH)
                pe.wait_ge(vu_free, (b + 1) * CH + 1)
                for i in range(2):
                    out = u.next()
                    u.wait_empty(pe)
                    for c in range(CH):
                        mm = pe.matmul(out[:, :], k["uv"][:, c * DIM:(c + 1) * DIM], vuT[:, c * SEQ + i * HALF:c * SEQ + (i + 1) * HALF],
                                       start=(c == 0), stop=(c == CH - 1))
                    mm.then_inc(unit_full, 1)
                for i in range(2):
                    u.wait_emptied(pe, i)
                    out = u.next()
                    u.wait_empty(pe)
                    for t in range(4):
                        mm = pe.transpose(out[:, t * P:(t + 1) * P], msgT[:, (4 * i + t) * P:(4 * i + t + 1) * P], k["ident"][:, :])
                    mm.then_inc(unit_full, 1)

        @block.gpsimd
        def _(pool):
            start_free(pool, *unit_free, *used, f_ready, t_ready, vu_free)

        @block.scalar
        def _(act):
            def high_parts(u, p):
                for i in range(4):
                    src = u.next()
                    u.wait_full(act)
                    dst = (u_st, v_hi)[i // 2][p]
                    act.copy(dst[:, (i % 2) * HALF:(i % 2 + 1) * HALF], src[:, :]).then_inc(hi_ready, 1)
                u.n += 2

            def sigmoids(b, c, i):
                step = (b * CH + c) * TILES + i
                act.wait_ge(used[i % 2], (b * CH + c) * (TILES // 2) + i // 2 + 1)
                act.wait_ge(f_full, step + 1)
                act.activation(f_sig[i % 2][:, :], f_ps[:, :], ACT.Sigmoid).then_inc(f_ready, 1)
                act.wait_ge(t_full, step + 1)
                act.activation(t_sig[i % 2][:, :], t_ps[:, :], ACT.Sigmoid).then_inc(t_ready, 1)

            with act.Fori(0, BATCH) as b:
                act.wait_ge(var_ready, b + 1)
                act.activation(dev[:, :], spread[:, :], ACT.Sqrt).then_inc(dev_ready, 1)
                high_parts(units_at(b, 1), 0)
                sigmoids(b, 0, 0)

                def body(b, c, p, last_pair):
                    last = last_pair and p == 1
                    u = units_at(b, 1 + PREP // 2 * (c + 1))
                    for i in range(TILES):
                        if i < TILES - 1:
                            sigmoids(b, c, i + 1)
                        elif not last:
                            sigmoids(b, c + 1, 0)
                        if i < 4 and not last:
                            src = u.next()
                            u.wait_full(act)
                            dst = (u_st, v_hi)[i // 2][1 - p]
                            act.copy(dst[:, (i % 2) * HALF:(i % 2 + 1) * HALF], src[:, :]).then_inc(hi_ready, 1)
                channels(act, b, body)
                u = units_at(b, 1 + PREP // 2 * CH)
                for i in range(2):
                    src = u.next()
                    u.wait_full(act)
                    act.copy(msgT[:, i * HALF:(i + 1) * HALF], src[:, :]).then_inc(u.free(), 1)

        @block.vector
        def _(dve):
            def prepared(u, i, c, p, b):
                src = u.next()
                u.wait_full(dve)
                cols = slice((i % 2) * HALF, (i % 2 + 1) * HALF)
                if i < 4:
                    dve.wait_ge(hi_ready, (b * CH + c) * 4 + i + 1)
                if i < 2:
                    ins = dve.tensor_tensor(u_st[p][RANK:P, cols], src[RANK:P, :], u_st[p][RANK:P, cols].bitcast(F32), ALU.subtract)
                elif i < 4:
                    ins = dve.tensor_tensor(v_lo[p][:, cols], src[:, :], v_hi[p][:, cols].bitcast(F32), ALU.subtract)
                else:
                    ins = dve.tensor_copy(uv_tok[p][:, 4 * (i - 4):4 * (i - 3), :, :].rearrange("p t a r -> p (t a r)"), src[:, :])
                ins.then_inc(u.free(), 1)

            def double(c, p):
                src = k["uvT"][:, ds(c * P, P)].rearrange("p (a r) -> p a r", a=2)
                for i in range(2):
                    ins = dve.tensor_scalar(twice[p][:, :, i, :], src, 1.0, None, ALU.mult)
                ins.then_inc(twice_ready, 1)

            with dve.Fori(0, BATCH) as b:
                link = Link(dve, link_sem, b * LINKS)

                def x_tile(t):
                    return k["x"][:, ds((b * TILES + t) * DIM, DIM)]
                for t in range(TILES):
                    ins = dve.bn_stats(stats[:, t, :], x_tile(t))
                link(ins)
                row_moments(dve, link, stats, mean[:, :], spread[:, :], work[:, :], TILES).then_inc(var_ready, 1)
                for p in range(2):
                    double(p, p)
                dve.wait_ge(dev_ready, b + 1)
                link(dve.reciprocal(rstd[:, :], dev[:, :]))
                for t in range(TILES):
                    ins = dve.tensor_scalar(z[:, t, :], x_tile(t), mean[:, t:t + 1], rstd[:, t:t + 1], ALU.subtract, ALU.mult)
                ins.then_inc(z_ready, 1)
                u = units_at(b, 0)
                for i in range(2):
                    src = u.next()
                    u.wait_full(dve)
                    dve.tensor_copy(zT[:, i * HALF:(i + 1) * HALF], src[:, :]).then_inc(u.free(), 1)
                for i in range(PREP):
                    prepared(u, i, 0, 0, b)

                def body(b, c, p, last_pair):
                    last = last_pair and p == 1
                    u = units_at(b, 1 + PREP // 2 * (c + 1))
                    if not last_pair:
                        double(c + 2, p)
                    for i in range(PREP if not last else 0):
                        prepared(u, i, c + 1, 1 - p, b)
                    dve.wait_ge(used[1], (b * CH + c + 1) * (TILES // 2) + 1)
                    dve.tensor_copy(vuT[:, ds(c * SEQ, SEQ)], vu_ps[:, :]).then_inc(vu_free, 1)
                channels(dve, b, body)
                u = units_at(b, 1 + PREP // 2 * CH)
                u.n += 2
                for i in range(2):
                    src = u.next()
                    u.wait_full(dve)
                    x4 = k["x"][:, ds(b * TILES * DIM + i * HALF, HALF)]
                    dve.tensor_tensor(x4, x4, src[:, :], ALU.add).then_inc(u.free(), 1)


def store_phase(nc, k, out):
    with ExitStack() as ctx:
        stored = ctx.enter_context(nc.semaphore("stored"))
        block = ctx.enter_context(nc.Block())

        @block.sync
        def _(sp):
            sp.dma_start(out.rearrange("b (n p) e -> p (b n) e", p=P),
                         k["x"][:, :].rearrange("p (n e) -> p n e", e=DIM)).then_inc(stored, 16)
            sp.wait_ge(stored, 16)


def hybrid_kernel(nc, d, out):
    with ExitStack() as ctx:
        def sb(name, shape, dt=F32):
            return ctx.enter_context(nc.sbuf_tensor(name, shape, dt))

        k = {
            "x": sb("x", [P, ALL * DIM]),
            "ident": sb("ident", [P, P]), "ident16": sb("ident16", [P, P], BF16), "mask": sb("mask", [P, P], BF16),
            "w_qkv": sb("w_qkv", [P, 3 * DIM]), "w_o": sb("w_o", [P, DIM]),
            "ln_rows": sb("ln_rows", [P, 4 * HD]), "bo_rows": sb("bo_rows", [P, DIM]),
            "attn_wT": sb("attn_wT", [P, DIM]), "gate_wT": sb("gate_wT", [P, EXPERTS]), "ln_cols": sb("ln_cols", [P, 4]),
            "uv": sb("uv", [P, CH * DIM]), "uvT": sb("uvT", [P, CH * P]),
        }
        setup_phase(nc, d, k)
        attention_phase(nc, k)
        k.update(w_gate=sb("w_gate", [P, UNITS * P]), w_up=sb("w_up", [P, UNITS * P]), w_down=sb("w_down", [P, UNITS * DIM]))
        moe_phase(nc, k, "f1", d)
        message_phase(nc, k)
        moe_phase(nc, k, "f2")
        store_phase(nc, k, out)


_INS = {'x': 'L0_attn_a_x', 'Wk': 'L0_attn_a_Wk', 'Wq': 'L0_attn_a_Wq', 'Wv': 'L0_attn_a_Wv', 'Wo': 'L0_attn_a_Wo',
        'bo': 'L0_attn_a_bo', 'kln_w': 'L0_attn_a_kln_w', 'kln_b': 'L0_attn_a_kln_b', 'qln_w': 'L0_attn_a_qln_w',
        'qln_b': 'L0_attn_a_qln_b', 'u': 'L0_attn_b_ternary_factor_u', 'v': 'L0_attn_b_ternary_factor_v',
        'ln1_g': 'L0_ffn_ln1_g', 'ln1_b': 'L0_ffn_ln1_b', 'attn_w': 'L0_ffn_attn_w', 'ln2_g': 'L0_ffn_ln2_g',
        'ln2_b': 'L0_ffn_ln2_b', 'gate_w': 'L0_ffn_gate_w', 'gate_proj': 'L0_ffn_gate_proj',
        'up_proj': 'L0_ffn_up_proj', 'down_proj': 'L0_ffn_down_proj'}


def kernel(**inputs):
    import numpy as _np
    import concourse.bacc as _bacc
    from concourse import mybir as _mybir
    from concourse.bass_utils import run_bass_kernel_spmd as _run

    nc = _bacc.Bacc("TRN2", target_bir_lowering=False, num_devices=1)
    arrays, aps = {}, {}
    for short, name in _INS.items():
        a = _np.ascontiguousarray(inputs[name])
        arrays[f"in_{name}_dram"] = a
        aps[short] = nc.dram_tensor(f"in_{name}_dram", a.shape, _mybir.dt.from_np(a.dtype), kind="ExternalInput").ap()
    out = nc.dram_tensor("out_0_dram", (BATCH, SEQ, DIM), F32, kind="ExternalOutput").ap()
    hybrid_kernel(nc, aps, out)
    r = _run(nc, [arrays], core_ids=[0])
    return r.results[0]["out_0_dram"]
```

```python
from contextlib import ExitStack

import concourse.bass as bass
from concourse import mybir

F32 = mybir.dt.float32
F32R = mybir.dt.float32r
BF16 = mybir.dt.bfloat16
U32 = mybir.dt.uint32
I32 = mybir.dt.int32
ALU = mybir.AluOpType
ACT = mybir.ActivationFunctionType
AX = mybir.AxisListType

P = 128
BATCH, SEQ, DIM = 4, 1024, 128
TILES = SEQ // P
ALL = BATCH * TILES
HALF = 512
EPS = 1e-5

HEADS, HD = 16, 8
GROUP = 4
GROUPS = HEADS // GROUP
STACK = P // GROUP
MASKED = -1e30

CH, RANK = 16, 64
MSG_SCALE = 0.03125

EXPERTS, INTER = 8, 512
BLOCKS = INTER // P
UNITS = EXPERTS * BLOCKS
GTOK = 4
TOP = 2
UNROLL = 8
HALVES = 2
HALF_NB = -(-(TOP * ALL // HALVES + EXPERTS - 1) // UNROLL) * UNROLL
NB = HALVES * HALF_NB
AHEAD = 6
CONSTS = 4


def ds(start, size):
    return bass.DynSlice(start, size)


class Link:

    def __init__(self, eng, sem, base=0):
        self.eng, self.sem, self.base, self.n = eng, sem, base, 0

    def __call__(self, ins):
        self.n += 1
        ins.then_inc(self.sem, 1)
        self.eng.wait_ge(self.sem, self.base + self.n)


def row_moments(dve, link, stats, mean, spread, work, tiles, spread_twice=None):
    even, odd = stats[:, 0:tiles, 1], stats[:, 0:tiles, 4]
    link(dve.tensor_tensor(mean, even, odd, ALU.add))
    link(dve.tensor_tensor(work, even, odd, ALU.subtract))
    link(dve.scalar_tensor_tensor(out=work, in0=work, scalar=0.25, in1=work, op0=ALU.mult, op1=ALU.mult))
    link(dve.tensor_tensor(spread, stats[:, 0:tiles, 2], stats[:, 0:tiles, 5], ALU.add))
    link(dve.scalar_tensor_tensor(out=spread, in0=spread, scalar=1.0 / DIM, in1=work, op0=ALU.mult, op1=ALU.add))
    link(dve.tensor_scalar(mean, mean, 0.5, None, ALU.mult))
    if spread_twice is not None:
        link(dve.tensor_scalar(spread_twice, spread, 1.0 + EPS, EPS * EPS, ALU.mult, ALU.add))
    return dve.tensor_scalar(spread, spread, EPS, None, ALU.add)


MOMENT_LINKS = 6


def start_free(eng, *sems):
    for s in sems:
        eng.sem_inc(s, 1)


def clear_semaphores(nc, sems):
    with nc.Block() as block:
        @block.gpsimd
        def _(pool):
            numbers = sorted(s.num for s in sems)
            while numbers:
                n = 1
                while n < len(numbers) and numbers[n] == numbers[0] + n:
                    n += 1
                pool.sem_clear(range(numbers[0], numbers[0] + n))
                del numbers[:n]


def setup_phase(nc, d, k):
    with ExitStack() as ctx, ExitStack() as phase:
        def sb(name, shape, dt=F32):
            return ctx.enter_context(nc.sbuf_tensor(name, shape, dt))

        sems = []

        def sem(name):
            sems.append(ctx.enter_context(nc.semaphore(name)))
            return sems[-1]

        small_raw = sb("small_raw", [P, 2, DIM])
        vec_row = sb("vec_row", [1, 4 * HD + DIM])
        ones_row = sb("ones_row", [1, P])
        vec_rows = ctx.enter_context(nc.psum_tensor("vec_rows", [P, HALF], F32))
        small_turned = ctx.enter_context(nc.psum_tensor("small_turned", [P, HALF], F32))

        x_in, attn_in, small_in, vec_in, col_in = (
            sem(n) for n in ("x_in", "attn_in", "small_in", "vec_in", "col_in"))
        ident_zero, ident_done, consts_done, ones_done, ident16_done, vec_full, small_full, copied = (
            sem(n) for n in ("ident_zero", "ident_done", "consts_done", "ones_done", "ident16_done", "vec_full", "small_full", "copied"))
        block = phase.enter_context(nc.Block())

        @block.sync
        def _(sp):
            sp.dma_start(k["x"][:, :].rearrange("p (n e) -> p n e", e=DIM),
                         d["x"].rearrange("b (n p) e -> p (b n) e", p=P)).then_inc(x_in, 16)
            for i, name in enumerate(("qln_w", "qln_b", "kln_w", "kln_b")):
                sp.dma_start(vec_row[0:1, i * HD:(i + 1) * HD],
                             d[name].rearrange("(a s) -> a s", a=1)).then_inc(vec_in, 16)
            sp.dma_start(vec_row[0:1, 4 * HD:], d["bo"].rearrange("(a s) -> a s", a=1)).then_inc(vec_in, 16)
            for i, name in enumerate(("Wq", "Wk", "Wv")):
                sp.dma_start(k["w_qkv"][:, i * DIM:(i + 1) * DIM], d[name]).then_inc(attn_in, 16)
            sp.dma_start(k["w_o"][:, :], d["Wo"]).then_inc(attn_in, 16)
            sp.dma_start(small_raw[:, 0, :], d["attn_w"]).then_inc(small_in, 16)
            sp.dma_start(small_raw[0:EXPERTS, 1, :], d["gate_w"]).then_inc(small_in, 16)
            for i, name in enumerate(("ln1_g", "ln1_b", "ln2_g", "ln2_b")):
                sp.dma_start(k["ln_cols"][:, i:i + 1], d[name].rearrange("(p a) -> p a", a=1)).then_inc(col_in, 16)
            sp.wait_ge(x_in, 16)
            sp.wait_ge(attn_in, 64)
            sp.wait_ge(col_in, 64)

        @block.scalar
        def _(act):
            act.wait_ge(small_full, 1)
            act.copy(k["attn_wT"][:, :], small_turned[:, 0:DIM])
            act.copy(k["gate_wT"][:, :], small_turned[:, DIM:DIM + EXPERTS]).then_inc(copied, 1)

        @block.gpsimd
        def _(pool):
            pool.memset(k["ident"][:, :], 0.0).then_inc(ident_zero, 1)
            pool.memset(k["mask"][:, :], 0.0).then_inc(ident_zero, 1)
            pool.wait_ge(ident_zero, 2)
            pool.affine_select(out=k["ident"][:, :], in_=k["ident"][:, :], compare_op=ALU.not_equal, fill=1.0,
                               base=0, pattern=[[-1, P]], channel_multiplier=1).then_inc(ident_done, 1)
            pool.affine_select(out=k["mask"][:, :], in_=k["mask"][:, :], compare_op=ALU.is_ge, fill=MASKED,
                               base=0, pattern=[[-1, P]], channel_multiplier=1).then_inc(consts_done, 1)

        @block.vector
        def _(dve):
            dve.memset(ones_row[:, :], 1.0).then_inc(ones_done, 1)
            dve.wait_ge(ident_done, 1)
            dve.tensor_copy(k["ident16"][:, :], k["ident"][:, :]).then_inc(ident16_done, 1)
            dve.wait_ge(vec_full, 1)
            dve.tensor_scalar(k["ln_rows"][:, 0:2 * HD], vec_rows[:, 0:2 * HD], HD ** -0.5, None, ALU.mult)
            dve.tensor_copy(k["ln_rows"][:, 2 * HD:4 * HD], vec_rows[:, 2 * HD:4 * HD])
            dve.tensor_copy(k["bo_rows"][:, :], vec_rows[:, 4 * HD:4 * HD + DIM]).then_inc(copied, 1)

        @block.tensor
        def _(pe):
            pe.wait_ge(ident_done, 1)
            pe.wait_ge(ones_done, 1)
            pe.wait_ge(vec_in, 80)
            pe.matmul(vec_rows[:, 0:4 * HD + DIM], ones_row[:, :], vec_row[:, :], start=True, stop=True).then_inc(vec_full, 1)
            pe.wait_ge(small_in, 32)
            pe.transpose(small_turned[:, 0:DIM], small_raw[:, 0, :], k["ident"][:, :])
            pe.transpose(small_turned[:, DIM:DIM + EXPERTS], small_raw[0:EXPERTS, 1, :],
                         k["ident"][0:EXPERTS, 0:EXPERTS]).then_inc(small_full, 1)

        phase.close()
        clear_semaphores(nc, sems)


def factors_phase(nc, d, k):
    with ExitStack() as ctx, ExitStack() as phase:
        sems = []

        def sem(name):
            sems.append(ctx.enter_context(nc.semaphore(name)))
            return sems[-1]

        turn = [ctx.enter_context(nc.psum_tensor(f"turn{i}", [P, HALF], F32)) for i in range(CH // 4)]
        uv_in, uv_scaled, turn_full = (sem(n) for n in ("uv_in", "uv_scaled", "turn_full"))
        block = phase.enter_context(nc.Block())
        uv = k["uv"][:, :].rearrange("p (c z) -> p c z", z=DIM)

        @block.sync
        def _(sp):
            sp.dma_start(uv[0:RANK], d["u"].rearrange("(c r) z -> r c z", r=RANK)).then_inc(uv_in, 16)

        @block.scalar
        def _(act):
            act.dma_start(uv[RANK:P], d["v"].rearrange("(c r) z -> r c z", r=RANK)).then_inc(uv_in, 16)
            for i in range(1, CH // 4, 2):
                act.wait_ge(turn_full, i + 1)
                act.copy(k["uvT"][:, i * HALF:(i + 1) * HALF], turn[i][:, :])

        @block.vector
        def _(dve):
            dve.wait_ge(uv_in, 32)
            dve.tensor_scalar(k["uv"][:, :], k["uv"][:, :], MSG_SCALE, None, ALU.mult).then_inc(uv_scaled, 1)
            for i in range(0, CH // 4, 2):
                dve.wait_ge(turn_full, i + 1)
                dve.tensor_copy(k["uvT"][:, i * HALF:(i + 1) * HALF], turn[i][:, :])

        @block.tensor
        def _(pe):
            pe.wait_ge(uv_scaled, 1)
            for i in range(CH // 4):
                for j in range(4):
                    c = 4 * i + j
                    mm = pe.transpose(turn[i][:, j * P:(j + 1) * P], k["uv"][:, c * DIM:(c + 1) * DIM], k["ident"][:, :])
                mm.then_inc(turn_full, 1)

        phase.close()
        clear_semaphores(nc, sems)


def attention_phase(nc, k):
    STEPS_BATCH = GROUPS * TILES
    SCORE_UNITS = GROUPS * 22
    MAX_UNITS = 43
    UNITS_AHEAD = 2 + TILES + 4 + MAX_UNITS + 2
    UNITS_BATCH = 2 + TILES + GROUPS * (4 + MAX_UNITS + 2 + 2) + 4
    LINKS_AHEAD = MOMENT_LINKS + 2 + 23 + 2
    LINKS = MOMENT_LINKS + 2 + 23 + GROUPS * (2 + 2) + 2
    with ExitStack() as ctx, ExitStack() as phase:
        def sb(name, shape, dt=F32):
            return ctx.enter_context(nc.sbuf_tensor(name, shape, dt))

        sems = []

        def sem(name):
            sems.append(ctx.enter_context(nc.semaphore(name)))
            return sems[-1]

        stats, mean, spread, work, dev, rstd = (sb(n, [P, TILES, 6] if n == "a_stats" else [P, TILES]) for n in
                                                ("a_stats", "a_mean", "a_spread", "a_work", "a_dev", "a_rstd"))
        z = sb("a_z", [P, TILES, DIM])
        zT = sb("a_zT", [P, SEQ])
        qk = sb("a_qk", [P, TILES, 2, HEADS, HD])
        prob = [sb(f"a_prob{i}", [P, GROUP, SEQ]) for i in range(2)]
        qk_sum, qk_var, qk_dev, qk_rstd = (sb(n, [P, TILES * 2 * HEADS]) for n in ("a_qk_sum", "a_qk_var", "a_qk_dev", "a_qk_rstd"))
        v_next = sb("a_v_next", [P, TILES, HEADS, HD])
        v1 = sb("a_v1", [P, TILES, HEADS, STACK])
        q_st = sb("a_q_st", [P, TILES, HEADS, STACK])
        k_st = sb("a_k_st", [P, TILES, HEADS, STACK])
        qT = [sb(f"a_qT{i}", [P, SEQ], F32R) for i in range(2)]
        qmT = [sb(f"a_qmT{i}", [P, SEQ], F32R) for i in range(2)]
        kT = [sb(f"a_kT{i}", [P, GROUP, SEQ], F32R) for i in range(2)]
        maxima = sb("a_maxima", [P, TILES, GROUP, 2])
        oT = sb("a_oT", [P, SEQ])
        o_den = [sb(f"a_o_den{i}", [P, 4, GROUP]) for i in range(2)]
        o_tok = sb("a_o_tok", [P, TILES, HEADS, HD])
        o_tokT = sb("a_o_tokT", [P, SEQ])
        qk_sq = o_tokT[:, :].rearrange("p (t h s) -> p t h s", h=HEADS, s=HD)
        proj = [sb(f"a_proj{i}", [P, 4, DIM]) for i in range(2)]

        score = [ctx.enter_context(nc.psum_tensor(f"a_score{i}", [P, SEQ], F32)) for i in range(2)]
        o_acc = ctx.enter_context(nc.psum_tensor("a_o_acc", [P, SEQ], F32))
        unit = [ctx.enter_context(nc.psum_tensor(f"a_unit{i}", [P, HALF], F32)) for i in range(2)]

        cleared, link_sem, var_ready, dev_ready, z_ready, stack_ready, shift_ready = (
            sem(n) for n in ("a_cleared", "a_link", "a_var_ready", "a_dev_ready", "a_z_ready", "a_stack_ready", "a_shift_ready"))
        v_ready = sem("a_v_ready")
        unit_full, score_full, o_free, kT_cleared = (sem(n) for n in ("a_unit_full", "a_score_full", "a_o_free", "a_kT_cleared"))
        unit_free = [sem(f"a_unit_free{i}") for i in range(2)]
        prob_ready = [sem(f"a_prob_ready{i}") for i in range(2)]
        pv_done = [sem(f"a_pv_done{i}") for i in range(2)]
        block = phase.enter_context(nc.Block())

        def max_units():
            for qt in range(TILES):
                w = (qt + 1) * P
                if w <= HALF:
                    per = min(GROUP, HALF // w) if w != 384 else 1
                    for h in range(0, GROUP, per):
                        yield qt, range(h, h + per), 0, w, True, 0
                else:
                    for h in range(GROUP):
                        yield qt, range(h, h + 1), 0, HALF, False, 0
                        yield qt, range(h, h + 1), HALF, w - HALF, True, 1

        MAXES = list(max_units())
        assert len(MAXES) == MAX_UNITS

        def stacks_at(g):
            return 0 if g + 1 < GROUPS else 1

        def max_slice(g, j):
            ends = (0, 0, 8, 16, 24, 31, 37, MAX_UNITS, MAX_UNITS) if g + 1 < GROUPS else (0, 0, 0, 9, 18, 27, 35, MAX_UNITS, MAX_UNITS)
            return range(ends[j], ends[j + 1])

        assert all(MAXES[n][0] < 4 for g in range(GROUPS) for n in max_slice(g, stacks_at(g) + 1))

        def score_units(j):
            per = 1 if j < 4 else 2 if j < 6 else 4
            return [range(h, h + per) for h in range(0, GROUP, per)], SEQ // per

        class Units:

            def __init__(self, b, ahead):
                self.b, self.n = b, ahead - 1

            def next(self):
                self.n += 1
                return unit[self.n % 2]

            def wait_empty(self, eng):
                eng.wait_ge(unit_free[self.n % 2], self.b * (UNITS_BATCH // 2) + self.n // 2 + 1)

            def wait_full(self, eng):
                eng.wait_ge(unit_full, self.b * UNITS_BATCH + self.n + 1)

            def wait_emptied(self, eng, n):
                eng.wait_ge(unit_free[n % 2], self.b * (UNITS_BATCH // 2) + n // 2 + 2)

            def free(self):
                return unit_free[self.n % 2]

        @block.tensor
        def _(pe):
            pe.wait_ge(cleared, 5)
            scores_done = []
            for g in range(GROUPS):
                for j in range(TILES):
                    scores_done.append((scores_done or [0])[-1] + len(score_units(j)[0]))

            def program(b, u, ahead, last):
                scores_made = [0]

                def turn(srcs):
                    out = u.next()
                    u.wait_empty(pe)
                    for i, s in enumerate(srcs):
                        mm = pe.transpose(out[:, i * P:(i + 1) * P], s, k["ident"][:, :])
                    mm.then_inc(unit_full, 1)
                    return u.n

                def heads_of(stack, g, t):
                    return stack[:, t, g * GROUP:(g + 1) * GROUP, :].rearrange("p h s -> p (h s)")

                def turn_stacks(g, i):
                    return [turn([heads_of(s, g % GROUPS, t) for t in range(4 * i, 4 * i + 4)]) for s in (q_st, k_st)]

                def project(t):
                    out = u.next()
                    u.wait_empty(pe)
                    pe.matmul(out[:, 0:3 * DIM], zT[:, t * P:(t + 1) * P], k["w_qkv"][:, :], start=True, stop=True)\
                      .then_inc(unit_full, 1)

                def maxima_unit(g, n):
                    qt, heads, first, width, masked, _ = MAXES[n]
                    out = u.next()
                    u.wait_empty(pe)
                    for i, h in enumerate(heads):
                        o = out[:, i * width:(i + 1) * width]
                        mm = pe.matmul(o, qT[g % 2][:, qt * P:(qt + 1) * P], kT[g % 2][:, h, first:first + width],
                                       start=True, stop=not masked)
                        if masked:
                            mm = pe.matmul(o[:, width - P:width], k["ident16"][:, :], k["mask"][:, :],
                                           start=False, stop=True)
                    mm.then_inc(unit_full, 1)

                def turn_shifted(g):
                    pe.wait_ge(shift_ready, b * GROUPS + g + 1)
                    return [turn([heads_of(q_st, g % GROUPS, t) for t in range(4 * i, 4 * i + 4)]) for i in range(2)]

                def scores(g, j, beside):
                    groups, width = score_units(j)
                    lo = j * P
                    base = SEQ - width
                    for heads in groups:
                        s = scores_made[0]
                        scores_made[0] += 1
                        out = score[s % 2]
                        pe.wait_ge(prob_ready[s % 2], b * (SCORE_UNITS // 2) + s // 2 + 1)
                        for i, h in enumerate(heads):
                            at = i * width - base
                            lhs = kT[g % 2][:, h, lo:lo + P]
                            first = True
                            for q0, q1 in ((lo, max(lo, HALF)), (max(lo, HALF), SEQ)):
                                if q0 == q1:
                                    continue
                                mm = pe.matmul(out[:, at + q0:at + q1], lhs, qmT[g % 2][:, q0:q1], start=True, stop=not first)
                                if first:
                                    mm = pe.matmul(out[:, at + lo:at + lo + P], k["mask"][:, :], k["ident16"][:, :],
                                                   start=False, stop=True)
                                first = False
                                if q1 == HALF:
                                    beside()
                        mm.then_inc(score_full, 1)
                        beside()

                def weigh(g, j, beside):
                    step = g * TILES + j
                    if j == 0:
                        pe.wait_ge(o_free, b * GROUPS + g + 1)
                        if g == 0:
                            pe.wait_ge(v_ready, b + 1)
                    done = scores_done[step]
                    for i in range(2):
                        pe.wait_ge(prob_ready[i], b * (SCORE_UNITS // 2) + (done + 1 - i) // 2 + 1)
                    lo = j * P
                    for q0, q1 in ((lo, max(lo, HALF)), (max(lo, HALF), SEQ)):
                        if q0 == q1:
                            continue
                        for h in range(GROUP):
                            mm = pe.matmul(o_acc[h * STACK:(h + 1) * STACK, q0:q1], v1[:, j, g * GROUP + h, :],
                                           prob[step % 2][:, h, q0:q1], start=(j == 0),
                                           stop=(j == (3 if q1 == HALF else TILES - 1)))
                        if q1 == HALF:
                            beside()
                    mm.then_inc(pv_done[step % 2], 1)

                def turn_out(g):
                    pe.wait_ge(o_free, b * GROUPS + g + 2)
                    for i in range(2):
                        out = u.next()
                        u.wait_empty(pe)
                        for t in range(4):
                            mm = pe.transpose(out[:, t * P:(t + 1) * P], oT[:, (4 * i + t) * P:(4 * i + t + 1) * P], k["ident"][:, :])
                        mm.then_inc(unit_full, 1)
                    return u.n

                if ahead:
                    pe.wait_ge(z_ready, 1)
                    for i in range(2):
                        turn([z[:, t, :] for t in range(4 * i, 4 * i + 4)])
                    for n in (u.n - 1, u.n):
                        u.wait_emptied(pe, n)
                    for t in range(TILES):
                        project(t)
                    pe.wait_ge(stack_ready, 1)
                    turn_stacks(0, 0)
                    for n in turn_stacks(0, 1):
                        u.wait_emptied(pe, n)
                    for n in range(MAX_UNITS):
                        maxima_unit(0, n)
                    for n in turn_shifted(0):
                        u.wait_emptied(pe, n)
                    return
                shifted, stacks = [], []
                for g in range(GROUPS):
                    follows = g + 1 < GROUPS or not last
                    for j in range(TILES):
                        todo = list(max_slice(g, j)) if follows else []
                        places = (2 * GROUP if j < 4 else len(score_units(j)[0])) + (2 if 1 <= j <= 4 else 1)
                        whole, placed = len(todo), [0]

                        def beside():
                            placed[0] += 1
                            upto = min(whole, -(-whole * placed[0] // places))
                            for n in stacks if todo else ():
                                u.wait_emptied(pe, n)
                            if todo:
                                stacks.clear()
                            while whole - len(todo) < upto:
                                maxima_unit(g + 1, todo.pop(0))

                        if j == 0:
                            for n in shifted:
                                u.wait_emptied(pe, n)
                        scores(g, j, beside)
                        if follows and j == stacks_at(g):
                            if g + 1 == GROUPS:
                                pe.wait_ge(stack_ready, b + 2)
                            stacks += turn_stacks(g + 1, 0)
                        if follows and j == stacks_at(g) + 1:
                            while todo:
                                maxima_unit(g + 1, todo.pop(0))
                            stacks += turn_stacks(g + 1, 1)
                        if j >= 1:
                            weigh(g, j - 1, beside)
                        while todo:
                            maxima_unit(g + 1, todo.pop(0))
                        if not last and (g, j) == (0, 3):
                            pe.wait_ge(z_ready, b + 2)
                            for i in range(2):
                                turn([z[:, t, :] for t in range(4 * i, 4 * i + 4)])
                        if not last and g == 0 and j >= 4:
                            for t in (2 * j - TILES, 2 * j - TILES + 1):
                                project(t)
                        if follows and j == TILES - 1:
                            shifted = turn_shifted(g + 1)
                        if j == 2 and g > 0:
                            turn_out(g - 1)
                    weigh(g, TILES - 1, lambda: None)
                turned_out = turn_out(GROUPS - 1)
                for n in (turned_out - 1, turned_out):
                    u.wait_emptied(pe, n)
                out_units = [turn([o_tok[:, t, :, :].rearrange("p h s -> p (h s)") for t in range(4 * i, 4 * i + 4)])
                             for i in range(2)]
                for i in range(2):
                    u.wait_emptied(pe, out_units[i])
                    out = u.next()
                    u.wait_empty(pe)
                    for t in range(4):
                        mm = pe.matmul(out[:, t * P:(t + 1) * P], o_tokT[:, (4 * i + t) * P:(4 * i + t + 1) * P],
                                       k["w_o"][:, :], start=True, stop=True)
                    mm.then_inc(unit_full, 1)
                assert last or u.n + 1 == UNITS_AHEAD + UNITS_BATCH, (u.n + 1, UNITS_AHEAD + UNITS_BATCH)

            program(0, Units(0, 0), True, False)
            with pe.Fori(0, BATCH - 1) as b:
                program(b, Units(b, UNITS_AHEAD), False, False)
            program(BATCH - 1, Units(BATCH - 1, UNITS_AHEAD), False, True)

        @block.scalar
        def _(act):
            act.wait_ge(kT_cleared, 1)

            def program(b, u, ahead, last):
                nb = 0 if ahead else b + 1

                def token_dev():
                    act.wait_ge(var_ready, 2 * nb + 1)
                    act.activation(dev[:, :], spread[:, :], ACT.Sqrt).then_inc(dev_ready, 1)

                def head_dev():
                    act.wait_ge(var_ready, 2 * nb + 2)
                    act.activation(qk_dev[:, :], qk_var[:, :], ACT.Sqrt).then_inc(dev_ready, 1)

                def projected(t):
                    src = u.next()
                    u.wait_full(act)
                    act.copy(qk[:, t, :, :, :].rearrange("p a h s -> p (a h s)"), src[:, 0:2 * DIM])
                    act.copy(v_next[:, t, :, :], src[:, 2 * DIM:3 * DIM].rearrange("p (h s) -> p h s", s=HD))\
                       .then_inc(u.free(), 1)

                def values():
                    for n in (u_values - 1, u_values):
                        u.wait_emptied(act, n)
                    act.copy(v1[:, :, :, 0:HD], v_next[:, :, :, :]).then_inc(v_ready, 1)

                def spread_keys(g):
                    u.n += 1
                    src = u.next()
                    u.wait_full(act)
                    for h in range(GROUP):
                        rows = slice(h * STACK, (h + 1) * STACK)
                        ins = act.copy(kT[g % 2][rows, h, HALF:SEQ], src[rows, :])
                    ins.then_inc(u.free(), 1)

                def second_shifted(g):
                    u.n += 1
                    src = u.next()
                    u.wait_full(act)
                    act.copy(qmT[g % 2][:, HALF:SEQ], src[:, :]).then_inc(u.free(), 1)

                if ahead:
                    token_dev()
                    u.n += 2
                    for t in range(TILES):
                        projected(t)
                    u_values = u.n
                    head_dev()
                    values()
                    u.n += 2
                    spread_keys(0)
                    u.n += MAX_UNITS
                    second_shifted(0)
                    return
                s = 0

                def empty_out(g):
                    act.wait_ge(pv_done[1], b * (STEPS_BATCH // 2) + (g + 1) * TILES // 2 + 1)
                    act.copy(oT[:, :], o_acc[:, :]).then_inc(o_free, 1)

                for g in range(GROUPS):
                    follows = g + 1 < GROUPS or not last
                    for j in range(TILES):
                        step = g * TILES + j
                        groups, width = score_units(j)
                        lo, base = j * P, SEQ - width
                        act.wait_ge(pv_done[step % 2], b * (STEPS_BATCH // 2) + step // 2 + 1)
                        for heads in groups:
                            act.wait_ge(score_full, b * SCORE_UNITS + s + 1)
                            src = score[s % 2][:, :].rearrange("p (h q) -> p h q", q=width)
                            act.activation(prob[step % 2][:, heads[0]:heads[-1] + 1, lo:SEQ], src[:, :, lo - base:width],
                                           ACT.Exp).then_inc(prob_ready[s % 2], 1)
                            s += 1
                        if follows and j == stacks_at(g):
                            u.n += 2
                        if follows:
                            u.n += len(max_slice(g, j))
                        if follows and j == stacks_at(g) + 1:
                            spread_keys(g + 1)
                        if not last:
                            if (g, j) == (0, 1):
                                token_dev()
                            if (g, j) == (0, 3):
                                u.n += 2
                            if g == 0 and j >= 4:
                                for t in (2 * j - TILES, 2 * j - TILES + 1):
                                    projected(t)
                                u_values = u.n
                            if (g, j) == (1, 6):
                                head_dev()
                        if follows and j == TILES - 1:
                            second_shifted(g + 1)
                        if j == 2 and g > 0:
                            u.n += 2
                            act.wait_ge(unit_full, b * UNITS_BATCH + u.n + 1)
                    empty_out(g)
                if not last:
                    values()
                u.n += 2
                for i in range(2):
                    src = u.next()
                    u.wait_full(act)
                    act.copy(o_tokT[:, i * HALF:(i + 1) * HALF], src[:, :]).then_inc(u.free(), 1)
                u.n += 2
                assert s == SCORE_UNITS and (last or u.n + 1 == UNITS_AHEAD + UNITS_BATCH)

            program(0, Units(0, 0), True, False)
            with act.Fori(0, BATCH - 1) as b:
                program(b, Units(b, UNITS_AHEAD), False, False)
            program(BATCH - 1, Units(BATCH - 1, UNITS_AHEAD), False, True)

        @block.gpsimd
        def _(pool):
            start_free(pool, *unit_free, *prob_ready, *pv_done, o_free)
            pool.memset(k_st[:, :, :, :], 0.0).then_inc(cleared, 1)
            pool.wait_ge(cleared, 1)
            pool.memset(k_st[:, :, :, 3 * HD:3 * HD + 2], 1.0).then_inc(cleared, 1)
            pool.memset(v1[:, :, :, HD + 1:STACK], 0.0).then_inc(cleared, 1)
            pool.memset(v1[:, :, :, HD:HD + 1], 1.0).then_inc(cleared, 1)
            pool.memset(q_st[:, :, :, :], 0.0).then_inc(cleared, 1)

        @block.vector
        def _(dve):
            for i in range(2):
                ins = dve.memset(kT[i][:, :, :].bitcast(F32), 0.0)
            ins.then_inc(kT_cleared, 1)
            dve.wait_ge(cleared, 5)

            def program(b, u, link, ahead, last):
                nb = 0 if ahead else b + 1

                def x_tile(t):
                    return k["x"][:, ds((nb * TILES + t) * DIM, DIM)]

                def token_moments():
                    for t in range(TILES):
                        ins = dve.bn_stats(stats[:, t, :], x_tile(t))
                    link(ins)
                    row_moments(dve, link, stats, mean[:, :], spread[:, :], work[:, :], TILES).then_inc(var_ready, 1)

                def token_norm():
                    dve.wait_ge(dev_ready, 2 * nb + 1)
                    link(dve.reciprocal(rstd[:, :], dev[:, :]))
                    for t in range(TILES):
                        ins = dve.tensor_scalar(z[:, t, :], x_tile(t), mean[:, t:t + 1], rstd[:, t:t + 1], ALU.subtract, ALU.mult)
                    ins.then_inc(z_ready, 1)

                def token_turned():
                    for i in range(2):
                        src = u.next()
                        u.wait_full(dve)
                        dve.tensor_copy(zT[:, i * HALF:(i + 1) * HALF], src[:, :]).then_inc(u.free(), 1)

                ROWS = TILES * HEADS
                rows = [P, TILES, HEADS, HD]

                def per_head(stat, a):
                    return stat[:, a * ROWS:(a + 1) * ROWS].rearrange("p (t h) -> p t h", h=HEADS)

                def spread_over(stat, a):
                    return per_head(stat, a).unsqueeze(3).broadcast_to(rows)

                def head_moments(a):
                    one = qk[:, :, a, :, :]
                    link(dve.tensor_reduce(per_head(qk_sum, a), one, AX.X, ALU.add))
                    link(dve.tensor_scalar(per_head(qk_sum, a), per_head(qk_sum, a), 1.0 / HD, None, ALU.mult))
                    link(dve.tensor_tensor(one, one, spread_over(qk_sum, a), ALU.subtract))
                    link(dve.tensor_tensor(qk_sq[:, :, :, :], one, one, ALU.mult))
                    link(dve.tensor_reduce(per_head(qk_var, a), qk_sq[:, :, :, :], AX.X, ALU.add))

                def head_spread():
                    dve.tensor_scalar(qk_var[:, :], qk_var[:, :], 1.0 / HD, EPS, ALU.mult, ALU.add).then_inc(var_ready, 1)

                def head_rstd():
                    dve.wait_ge(dev_ready, 2 * nb + 2)
                    link(dve.reciprocal(qk_rstd[:, :], qk_dev[:, :]))

                def head_norm(a):
                    one = qk[:, :, a, :, :]
                    link(dve.tensor_tensor(one, one, spread_over(qk_rstd, a), ALU.mult))
                    for i, op in enumerate((ALU.mult, ALU.add)):
                        w = k["ln_rows"][:, (2 * a + i) * HD:(2 * a + i + 1) * HD]
                        link(dve.tensor_tensor(one, one, w.unsqueeze(1).unsqueeze(1).broadcast_to(rows), op))

                def stack_keys():
                    kk = qk[:, :, 1, :, :]
                    link(dve.tensor_copy(k_st[:, :, :, 0:HD].bitcast(F32R), kk))
                    link(dve.tensor_tensor(k_st[:, :, :, 2 * HD:3 * HD].bitcast(F32R), kk, k_st[:, :, :, 0:HD], ALU.subtract))
                    link(dve.tensor_copy(k_st[:, :, :, HD:2 * HD], k_st[:, :, :, 0:HD]))

                def stack_queries():
                    u.wait_full(dve)
                    q = qk[:, :, 0, :, :]
                    link(dve.tensor_copy(q_st[:, :, :, 0:HD].bitcast(F32R), q))
                    link(dve.tensor_tensor(q_st[:, :, :, HD:2 * HD].bitcast(F32R), q, q_st[:, :, :, 0:HD], ALU.subtract))
                    link(dve.tensor_copy(q_st[:, :, :, 2 * HD:3 * HD], q_st[:, :, :, 0:HD]))
                    dve.memset(q_st[:, :, :, 3 * HD:3 * HD + 2], 0.0).then_inc(stack_ready, 1)

                def empty_queries(dst, i):
                    src = u.next()
                    u.wait_full(dve)
                    dve.tensor_copy(dst[:, i * HALF:(i + 1) * HALF], src[:, :]).then_inc(u.free(), 1)

                def spread_keys(g):
                    src = u.next()
                    u.wait_full(dve)
                    for h in range(GROUP):
                        rows = slice(h * STACK, (h + 1) * STACK)
                        ins = dve.tensor_copy(kT[g % 2][rows, h, 0:HALF], src[rows, :])
                    ins.then_inc(u.free(), 1)

                def maxima_unit(n):
                    qt, heads, _, width, _, part = MAXES[n]
                    src = u.next()
                    u.wait_full(dve)
                    dve.tensor_reduce(maxima[:, qt, heads[0]:heads[-1] + 1, part],
                                      src[:, 0:len(heads) * width].rearrange("p (h w) -> p h w", w=width),
                                      AX.X, ALU.max).then_inc(u.free(), 1)

                def shift(g):
                    u.wait_emptied(dve, u.n)
                    link(dve.tensor_tensor(maxima[:, 4:TILES, :, 0], maxima[:, 4:TILES, :, 0], maxima[:, 4:TILES, :, 1], ALU.max))
                    heads = slice(g % GROUPS * GROUP, (g % GROUPS + 1) * GROUP)
                    hi, lo = q_st[:, :, heads, 3 * HD], q_st[:, :, heads, 3 * HD + 1]
                    link(dve.tensor_scalar(hi.bitcast(F32R), maxima[:, :, :, 0], -1.0, None, ALU.mult))
                    dve.scalar_tensor_tensor(out=lo.bitcast(F32R), in0=maxima[:, :, :, 0], scalar=-1.0, in1=hi,
                                             op0=ALU.mult, op1=ALU.subtract).then_inc(shift_ready, 1)
                    empty_queries(qmT[g % 2], 0)
                    u.n += 1

                def normalise(g):
                    for i in range(2):
                        src = u.next()
                        u.wait_full(dve)
                        o = src[:, :].rearrange("p (t h s) -> p t h s", t=4, s=STACK)
                        link(dve.reciprocal(o_den[i][:, :, :], o[:, :, :, HD]))
                        ins = dve.tensor_tensor(o_tok[:, 4 * i:4 * i + 4, g * GROUP:(g + 1) * GROUP, :], o[:, :, :, 0:HD],
                                                o_den[i][:, :, :].unsqueeze(3).broadcast_to([P, 4, GROUP, HD]), ALU.mult)
                        ins.then_inc(u.free(), 1)

                if ahead:
                    token_moments()
                    token_norm()
                    token_turned()
                    u.n += TILES
                    for n in (u.n - 1, u.n):
                        u.wait_emptied(dve, n)
                    for a in range(2):
                        head_moments(a)
                    head_spread()
                    head_rstd()
                    for a in range(2):
                        head_norm(a)
                    stack_keys()
                    stack_queries()
                    empty_queries(qT[0], 0)
                    spread_keys(0)
                    empty_queries(qT[0], 1)
                    u.n += 1
                    for n in range(MAX_UNITS):
                        maxima_unit(n)
                    shift(0)
                    assert link.n == LINKS_AHEAD, (link.n, LINKS_AHEAD)
                    return
                for g in range(GROUPS):
                    follows = g + 1 < GROUPS or not last
                    for j in range(TILES):
                        if not last and (g, j) == (3, 0):
                            stack_queries()
                        if follows and j == stacks_at(g):
                            empty_queries(qT[(g + 1) % 2], 0)
                            spread_keys(g + 1)
                        for n in max_slice(g, j) if follows else ():
                            maxima_unit(n)
                        if follows and j == stacks_at(g) + 1:
                            empty_queries(qT[(g + 1) % 2], 1)
                            u.n += 1
                        if not last:
                            if (g, j) == (0, 0):
                                token_moments()
                            if (g, j) == (0, 2):
                                token_norm()
                            if (g, j) == (0, 3):
                                token_turned()
                            if g == 0 and j >= 4:
                                u.n += 2
                                projected = u.n
                            if (g, j) == (1, 1):
                                for n in (projected - 1, projected):
                                    u.wait_emptied(dve, n)
                                head_moments(0)
                            if (g, j) == (1, 4):
                                head_moments(1)
                                head_spread()
                            if (g, j) == (2, 0):
                                head_rstd()
                                head_norm(1)
                            if (g, j) == (2, 3):
                                stack_keys()
                            if (g, j) == (2, 5):
                                head_norm(0)
                        if follows and j == TILES - 1:
                            shift(g + 1)
                        if j == 2 and g > 0:
                            normalise(g - 1)
                normalise(GROUPS - 1)
                u.n += 2
                for i in range(2):
                    src = u.next()
                    u.wait_full(dve)
                    o = src[:, :].rearrange("p (t e) -> p t e", e=DIM)
                    bo = k["bo_rows"][:, :].unsqueeze(1).broadcast_to([P, 4, DIM])
                    link(dve.tensor_tensor(proj[i][:, :, :], o, bo, ALU.add))
                    x4 = k["x"][:, ds(b * TILES * DIM + i * HALF, HALF)]
                    ins = dve.tensor_tensor(x4, x4, proj[i][:, :, :].rearrange("p t e -> p (t e)"), ALU.add)
                    ins.then_inc(u.free(), 1)
                assert last or u.n + 1 == UNITS_AHEAD + UNITS_BATCH
                assert last or link.n == LINKS, (link.n, LINKS)

            program(0, Units(0, 0), Link(dve, link_sem), True, False)
            with dve.Fori(0, BATCH - 1) as b:
                program(b, Units(b, UNITS_AHEAD), Link(dve, link_sem, LINKS_AHEAD + b * LINKS), False, False)
            program(BATCH - 1, Units(BATCH - 1, UNITS_AHEAD), Link(dve, link_sem, LINKS_AHEAD + (BATCH - 1) * LINKS), False, True)

        phase.close()
        clear_semaphores(nc, sems)


def moe_phase(nc, d, k, name, clear):
    GROUPS_ALL = ALL // GTOK
    COLS = GTOK * DIM
    CHUNKS = 3 * EXPERTS
    RAWS = 12
    FLAT = ALL * EXPERTS
    HALF_TILES = ALL // HALVES
    SENT = TOP * HALF_TILES
    BATCHED = 8
    with ExitStack() as ctx, ExitStack() as phase:
        def sb(n, shape, dt=F32):
            return ctx.enter_context(nc.sbuf_tensor(f"{name}_{n}", shape, dt))

        sems = []

        def sem(n):
            sems.append(ctx.enter_context(nc.semaphore(f"{name}_{n}")))
            return sems[-1]

        def pair(n):
            return [ctx.enter_context(nc.psum_tensor(f"{name}_{n}{i}", [P, HALF], F32)) for i in range(2)]

        stats = sb("stats", [P, ALL, 6])
        mean, work = sb("mean", [P, ALL]), sb("work", [P, ALL])
        spread, dev, rstd = (sb(n, [P, 2 * ALL]) for n in ("spread", "dev", "rstd"))
        h = sb("h", [P, ALL * DIM])
        norm_all = sb("norm_all", [P, ALL * DIM])
        logits, pick, other = (sb(n, [P, ALL, EXPERTS]) for n in ("logits", "pick", "other"))
        chosen = sb("chosen", [P, ALL, EXPERTS])
        count0, count1, place = (sb(n, [P, HALVES, HALF_TILES, EXPERTS]) for n in ("count0", "count1", "place"))
        rank = sb("rank", [P, EXPERTS])
        blocks_int = sb("blocks_int", [P, HALVES, EXPERTS], U32)
        blocks, first0, first1 = (sb(n, [P, HALVES, EXPERTS]) for n in ("blocks", "first0", "first1"))
        at_block = sb("at_block", [1, NB, EXPERTS])
        expert_sum, expert_of = sb("expert_sum", [1, NB]), sb("expert_of", [1, NB], I32)
        row_of32, row_of = sb("row_of32", [P, TOP, ALL]), sb("row_of", [P, TOP, ALL], U32)
        below, ones, zeros = (sb(n, [P, P]) for n in ("below", "ones", "zeros"))
        best, second, first_at, ratio, share = (sb(n, [P, ALL]) for n in ("best", "second", "first_at", "ratio", "share"))
        raw = [sb(f"raw{i}", [P, HALF]) for i in range(RAWS)]
        w_hi, w_lo = ([sb(f"w_{part}{i}", [P, UNITS * P], F32R) for i in range(2)] for part in ("hi", "lo"))
        w_down = sb("w_down", [P, UNITS * DIM])
        t_rows = [sb(f"t_rows{i}", [P, DIM]) for i in range(UNROLL)]
        t32 = [sb(f"t32{i}", [P, P]) for i in range(2)]
        t_hi, t_lo = ([sb(f"{n}{i}", [P, P], F32R) for i in range(2)] for n in ("t_hi", "t_lo"))
        silu = [sb(f"silu{i}", [P, HALF]) for i in range(2)]
        inner = [sb(f"inner{i}", [P, HALF]) for i in range(2)]
        innerT = [sb(f"innerT{i}", [P, HALF]) for i in range(2)]
        y_rows = [sb(f"y_rows{i}", [P, DIM]) for i in range(2)]
        landing = [h, norm_all]
        norm, normT = inner, silu
        gate, up, out = pair("gate"), pair("up"), pair("out")
        inner_turn = out
        t_turn, y_ps = (ctx.enter_context(nc.psum_tensor(f"{name}_{n}", [P, HALF], F32)) for n in ("t_turn", "y_ps"))

        raw_in = [sem(f"raw_in{i}") for i in range(RAWS // 3)]
        weight_full, weight_hi, weight_free, consts_done, rows_clear = (
            sem(n) for n in ("weight_full", "weight_hi", "weight_free", "consts_done", "rows_clear"))
        link_sem, stats_done, var_ready, dev_ready, y_done, norm_ready, turn_full, normT_ready = (
            sem(n) for n in ("link", "stats_done", "var_ready", "dev_ready", "y_done", "norm_ready", "turn_full", "normT_ready"))
        product_full, product_free, gap_ready, ratio_ready = (
            sem(n) for n in ("product_full", "product_free", "gap_ready", "ratio_ready"))
        norm_kept = [sem(f"norm_kept{i}") for i in range(2)]
        chosen_ready, counts_full, places_ready, table_ready, x_summed = (
            sem(n) for n in ("chosen_ready", "counts_full", "places_ready", "table_ready", "x_summed"))
        sent = [sem(f"sent{i}") for i in range(HALVES)]
        loaded = [sem(f"loaded{i}") for i in range(UNROLL)]
        t_turned, t32_ready, t_hi_ready, t_lo_ready, gate_full, up_full, inner_turned, y_full, y_ready = (
            sem(n) for n in ("t_turned", "t32_ready", "t_hi_ready", "t_lo_ready", "gate_full", "up_full", "inner_turned",
                             "y_full", "y_ready"))
        silu_ready, inner_ready, innerT_ready, y_stored = (
            [sem(f"{n}{i}") for i in range(2)] for n in ("silu_ready", "inner_ready", "innerT_ready", "y_stored"))
        landed = [sem(f"landed{i}") for i in range(HALVES * SENT // BATCHED)]
        first_added = sem("first_added")
        block = phase.enter_context(nc.Block())

        def chunk(c):
            e, mat = divmod(c, 3)
            return e, mat, slice(e * INTER, (e + 1) * INTER)

        def half(b):
            it, i = b
            return it * (UNROLL // 2) + i // 2

        def number(b):
            it, i = b
            return it * UNROLL + i

        def earlier(b, n):
            it, i = b
            return (it, i - n)

        @block.sync
        def _(sp):
            for c in range(CHUNKS):
                e, mat, _ = chunk(c)
                if c >= RAWS:
                    sp.wait_ge(weight_full, c - RAWS + 1)
                if mat == 2:
                    ins = sp.dma_start(raw[c % RAWS][:, :], d["down_proj"][e])
                else:
                    ins = sp.dma_start(raw[c % RAWS][:, :].rearrange("p (n h) -> p n h", h=DIM),
                                       d[("gate_proj", "up_proj")[mat]][e].rearrange("(n p) h -> p n h", p=P))
                ins.then_inc(raw_in[e % (RAWS // 3)], 16)

            def load(n, h, slot):
                sp.dma_start(t_rows[slot][:, :], k["sent_rows"][h][ds((n - h * HALF_NB) * P, P), :]).then_inc(loaded[slot], 16)

            def store(b, h):
                p = b[1] % 2
                sp.wait_ge(y_ready, number(b) + 1)
                sp.dma_start(k["result_rows"][h][ds((number(b) - h * HALF_NB) * P, P), :], y_rows[p][:, :]).then_inc(y_stored[p], 16)

            def body(it, halves):
                for i, (stored, fetched) in enumerate(halves):
                    if fetched is not None:
                        sp.wait_ge(t_turned, number((it, i + AHEAD - UNROLL)) + 1)
                        load(number((it, i + AHEAD)), fetched, (i + AHEAD) % UNROLL)
                    if stored is not None:
                        store(earlier((it, i), 2), stored)

            sp.wait_ge(sent[0], 16 * SENT)
            for n in range(UNROLL):
                load(n, 0, n)
            steps = NB // UNROLL
            crossing = steps // HALVES - 1
            body(0, [(None if i < 2 else 0, None if i + AHEAD < UNROLL else 0) for i in range(UNROLL)])
            with sp.Fori(1, crossing) as it:
                body(it, [(0, 0)] * UNROLL)
            sp.wait_ge(sent[1], 16 * SENT)
            body(crossing, [(0, 0 if i + AHEAD < UNROLL else 1) for i in range(UNROLL)])
            body(crossing + 1, [(0 if i < 2 else 1, 1) for i in range(UNROLL)])
            with sp.Fori(crossing + 2, steps - 1) as it:
                body(it, [(1, 1)] * UNROLL)
            sp.wait_ge(t_turned, NB - UNROLL + 1)
            load(HALF_NB, 1, 0)
            body(steps - 1, [(1, 1 if i + AHEAD < UNROLL else None) for i in range(UNROLL)])
            for n in (2, 1):
                store((steps, -n), 1)

        @block.tensor
        def _(pe):
            def turn_weights():
                for c in range(CHUNKS):
                    pe.wait_ge(raw_in[c // 3 % (RAWS // 3)], 48 * (c // RAWS + 1))
                    if c >= 2:
                        pe.wait_ge(weight_free, c - 1)
                    for j in range(BLOCKS):
                        mm = pe.transpose(out[c % 2][:, j * P:(j + 1) * P], raw[c % RAWS][:, j * P:(j + 1) * P], k["ident"][:, :])
                    mm.then_inc(weight_full, 1)

            for turn_no, w in enumerate((k["attn_wT"], k["gate_wT"])):
                cols = w.shape[1]
                with pe.Fori(0, GROUPS_ALL // 2) as gg:
                    before = turn_no * GROUPS_ALL + 2 * gg
                    for i in range(2):
                        pe.wait_ge(norm_ready, before + i + 1)
                        pe.wait_ge(normT_ready, before + 1)
                        for t in range(GTOK):
                            mm = pe.transpose(gate[i][:, t * P:(t + 1) * P], norm[i][:, t * DIM:(t + 1) * DIM], k["ident"][:, :])
                        mm.then_inc(turn_full, 1)
                    for i in range(2):
                        pe.wait_ge(normT_ready, before + i + 2)
                        pe.wait_ge(product_free, before + 1)
                        for t in range(GTOK):
                            mm = pe.matmul(up[i][:, t * cols:(t + 1) * cols], normT[i][:, t * P:(t + 1) * P], w[:, :],
                                           start=True, stop=True)
                        mm.then_inc(product_full, 1)
            pe.wait_ge(chosen_ready, 1)
            pe.wait_ge(consts_done, CONSTS)
            flat = chosen[:, :, :].rearrange("p t e -> p (t e)")
            pe.matmul(up[0][:, 0:FLAT], below[:, :], flat, start=True, stop=True)
            pe.matmul(up[1][:, 0:FLAT], ones[:, :], flat, start=True, stop=True)
            pe.matmul(up[1][:, FLAT:FLAT + P], ones[:, :], below[:, :], start=True, stop=True).then_inc(counts_full, 1)
            turn_weights()
            pe.wait_ge(weight_free, CHUNKS)
            pe.wait_ge(table_ready, 1)

            def turn_rows(b):
                pe.wait_ge(loaded[b[1] % UNROLL], 16 * (b[0] + b[1] // UNROLL + 1))
                pe.transpose(t_turn[:, 0:P], t_rows[b[1] % UNROLL][:, :], k["ident"][:, :]).then_inc(t_turned, 1)

            def products(to, w, e, i):
                cols = ds(e * INTER, INTER)
                pe.matmul(to[:, :], t_lo[i][:, :], w_hi[w][:, cols], start=True, stop=False)
                pe.matmul(to[:, :], t_hi[i][:, :], w_hi[w][:, cols], start=False, stop=False)
                return pe.matmul(to[:, :], t_hi[i][:, :], w_lo[w][:, cols], start=False, stop=True)

            def turn_inner(b, fresh):
                p = b[1] % 2
                pe.wait_ge(inner_ready[p], half(b) + 1)
                if not fresh:
                    pe.wait_ge(innerT_ready[p], half(b))
                for ib in range(BLOCKS):
                    mm = pe.transpose(inner_turn[p][:, ib * P:(ib + 1) * P], inner[p][:, ib * P:(ib + 1) * P], k["ident"][:, :])
                mm.then_inc(inner_turned, 1)

            def down(b, e, fresh):
                p = b[1] % 2
                pe.wait_ge(innerT_ready[p], half(b) + 1)
                if not fresh:
                    pe.wait_ge(y_ready, number(b))
                for ib in range(BLOCKS):
                    mm = pe.matmul(y_ps[:, 0:DIM], innerT[p][:, ib * P:(ib + 1) * P], w_down[:, ds(e * INTER + ib * DIM, DIM)],
                                   start=(ib == 0), stop=(ib == BLOCKS - 1))
                mm.then_inc(y_full, 1)

            def expert(b):
                return pe.value_load(expert_of[0:1, ds(number(b), 1)], min_val=0, max_val=EXPERTS - 1)

            def body(it, first):
                experts = {i: expert((it, i)) for i in ((0,) if first else (-2, -1, 0))}
                for i in range(UNROLL):
                    b, p, e = (it, i), i % 2, experts[i]
                    pe.wait_ge(t32_ready, number(b) + 1)
                    turn_rows((it, i + 1))
                    pe.wait_ge(t_lo_ready, number(b) + 1)
                    if not (first and i < 2):
                        pe.wait_ge(silu_ready[p], half(b))
                    products(gate[p], 0, e, p).then_inc(gate_full, 1)
                    if not (first and i < 2):
                        pe.wait_ge(inner_ready[p], half(b))
                    products(up[p], 1, e, p).then_inc(up_full, 1)
                    if not (first and i < 1):
                        turn_inner(earlier(b, 1), first and i < 3)
                    if not (first and i < 2):
                        down(earlier(b, 2), experts[i - 2], first and i < 3)
                    if i + 1 < UNROLL:
                        experts[i + 1] = expert((it, i + 1))

            turn_rows((0, 0))
            body(0, True)
            with pe.Fori(1, NB // UNROLL) as it:
                body(it, False)
            end = (NB // UNROLL, 0)
            turn_inner(earlier(end, 1), False)
            for n in (2, 1):
                down(earlier(end, n), expert(earlier(end, n)), False)

        @block.scalar
        def _(act):
            act.wait_ge(var_ready, 1)
            act.activation(dev[:, :], spread[:, :], ACT.Sqrt).then_inc(dev_ready, 1)
            for turn_no in range(2):
                if turn_no:
                    act.wait_ge(var_ready, 2)
                    act.activation(dev[:, 0:ALL], spread[:, 0:ALL], ACT.Sqrt).then_inc(dev_ready, 1)
                with act.Fori(0, GROUPS_ALL // 2) as gg:
                    for i in range(2):
                        before = turn_no * GROUPS_ALL + 2 * gg + i
                        if turn_no:
                            act.wait_ge(norm_ready, before + 1)
                            act.copy(norm_all[:, ds((2 * gg + i) * COLS, COLS)], norm[i][:, :]).then_inc(norm_kept[i], 1)
                        act.wait_ge(turn_full, before + 1)
                        act.activation(normT[i][:, :], gate[i][:, :], ACT.Identity, bias=k["ln_cols"][:, 2 * turn_no + 1:2 * turn_no + 2],
                                       scale=k["ln_cols"][:, 2 * turn_no:2 * turn_no + 1]).then_inc(normT_ready, 1)
            act.wait_ge(gap_ready, 1)
            act.activation(ratio[:, :], second[:, :], ACT.Exp).then_inc(ratio_ready, 1)
            for c in range(CHUNKS):
                _, mat, cols = chunk(c)
                act.wait_ge(weight_full, c + 1)
                if mat < 2:
                    act.copy(w_hi[mat][:, cols], out[c % 2][:, :]).then_inc(weight_hi, 1)

            def high_rows(b, fresh):
                act.wait_ge(t32_ready, number(b) + 1)
                if not fresh:
                    act.wait_ge(up_full, number(b) - 1)
                act.copy(t_hi[b[1] % 2][:, :], t32[b[1] % 2][:, :]).then_inc(t_hi_ready, 1)

            def copy_turned(b, fresh):
                p = b[1] % 2
                act.wait_ge(inner_turned, number(b) + 1)
                if not fresh:
                    act.wait_ge(y_full, number(b) - 1)
                act.copy(innerT[p][:, :], inner_turn[p][:, :]).then_inc(innerT_ready[p], 1)

            def body(it, first):
                for i in range(UNROLL):
                    b, p = (it, i), i % 2
                    high_rows((it, i + 1), first and i < 1)
                    act.wait_ge(gate_full, number(b) + 1)
                    if not (first and i < 2):
                        act.wait_ge(inner_ready[p], half(b))
                    act.activation(silu[p][:, :], gate[p][:, :], ACT.Silu).then_inc(silu_ready[p], 1)
                    if not (first and i < 1):
                        copy_turned(earlier(b, 1), first and i < 3)

            high_rows((0, 0), True)
            body(0, True)
            with act.Fori(1, NB // UNROLL) as it:
                body(it, False)
            copy_turned((NB // UNROLL, -1), False)

        @block.gpsimd
        def _(pool):
            start_free(pool, *norm_kept, normT_ready, product_free)
            pool.memset(zeros[:, :], 0.0).then_inc(consts_done, 1)
            pool.memset(ones[:, :], 1.0).then_inc(consts_done, 1)
            pool.memset(below[:, :], 1.0).then_inc(consts_done, 1)
            pool.wait_ge(consts_done, 3)
            pool.affine_select(out=below[:, :], in_=below[:, :], compare_op=ALU.is_ge, fill=0.0,
                               base=-1, pattern=[[1, P]], channel_multiplier=-1).then_inc(consts_done, 1)
            if clear:
                for rows in k["sent_rows"]:
                    pool.dma_start(rows.rearrange("(n p) e -> p n e", p=P),
                                   zeros[:, :].unsqueeze(1).broadcast_to([P, HALF_NB, DIM])).then_inc(rows_clear, 16)
                pool.wait_ge(rows_clear, 16 * HALVES)
            for i in range(2):
                pool.wait_ge(norm_kept[i], GROUPS_ALL // 2 + 1)
            pool.wait_ge(places_ready, 1)
            for half_no in range(HALVES):
                for j in range(SENT):
                    t, n = half_no * HALF_TILES + j // TOP, j % TOP
                    pool.indirect_dma_start(k["sent_rows"][half_no][:, :], bass.IndirectOffsetOnAxis(ap=row_of[:, n, t:t + 1], axis=0),
                                            norm_all[:, t * DIM:(t + 1) * DIM], None).then_inc(sent[half_no], 16)
            pool.wait_ge(product_free, GROUPS_ALL + 1)
            pool.tensor_tensor(k["x"][:, :], k["x"][:, :], h[:, :], ALU.add).then_inc(x_summed, 1)
            for half_no in range(HALVES):
                pool.wait_ge(x_summed, 1)
                for s in y_stored:
                    pool.wait_ge(s, 16 * (half_no + 1) * (HALF_NB // 2))
                for j in range(half_no * SENT, (half_no + 1) * SENT):
                    t, n = divmod(j, TOP)
                    pool.indirect_dma_start(landing[half_no][:, j % SENT * DIM:(j % SENT + 1) * DIM], None, k["result_rows"][half_no][:, :],
                                            bass.IndirectOffsetOnAxis(ap=row_of[:, n, t:t + 1], axis=0)).then_inc(landed[j // BATCHED], 16)

        @block.vector
        def _(dve):
            link = Link(dve, link_sem)
            for e in range(EXPERTS):
                ins = dve.memset(rank[:, e:e + 1], float(EXPERTS - e))
            link(ins)

            flat_stats = stats[:, :, :].rearrange("p t s -> p (t s)")

            def group_stats(src, g):
                for t in range(GTOK):
                    at = g * GTOK + t
                    ins = dve.bn_stats(flat_stats[:, ds(at * 6, 6)], src[:, ds(at * DIM, DIM)])
                return ins

            def normalise(dst, src, g, t, twice):
                at = g * GTOK + t
                return dve.tensor_scalar(dst, src[:, ds(at * DIM, DIM)], mean[:, ds(at, 1)], rstd[:, ds(at + twice * ALL, 1)],
                                         ALU.subtract, ALU.mult)

            def normalised(gg, turn_no, src):
                for i in range(2):
                    if turn_no:
                        dve.wait_ge(norm_kept[i], gg + 1)
                    dve.wait_ge(normT_ready, turn_no * GROUPS_ALL + 2 * gg + 1)
                    for t in range(GTOK):
                        ins = normalise(norm[i][:, t * DIM:(t + 1) * DIM], src, 2 * gg + i, t, 1 - turn_no)
                    ins.then_inc(norm_ready, 1)

            with dve.Fori(0, GROUPS_ALL) as g:
                group_stats(k["x"], g).then_inc(stats_done, 1)
            dve.wait_ge(stats_done, GROUPS_ALL)
            row_moments(dve, link, stats, mean[:, :], spread[:, 0:ALL], work[:, :], ALL, spread[:, ALL:2 * ALL]).then_inc(var_ready, 1)
            dve.wait_ge(dev_ready, 1)
            link(dve.reciprocal(rstd[:, :], dev[:, :]))
            with dve.Fori(0, GROUPS_ALL // 2) as gg:
                normalised(gg, 0, k["x"])
                for i in range(2):
                    for t in range(GTOK):
                        at = (2 * gg + i) * GTOK + t
                        ins = normalise(h[:, ds(at * DIM, DIM)], k["x"], 2 * gg + i, t, 0)
                    ins.then_inc(y_done, 1)
                for i in range(2):
                    g = 2 * gg + i
                    dve.wait_ge(product_full, g + 1)
                    dve.wait_ge(y_done, g + 1)
                    mine = h[:, ds(g * COLS, COLS)]
                    dve.tensor_tensor(mine, mine, up[i][:, :], ALU.add).then_inc(product_free, 1)
                for i in range(2):
                    dve.wait_ge(product_free, 2 * gg + i + 2)
                    group_stats(h, 2 * gg + i).then_inc(stats_done, 1)
            dve.wait_ge(stats_done, 2 * GROUPS_ALL)
            row_moments(dve, link, stats, mean[:, :], spread[:, 0:ALL], work[:, :], ALL).then_inc(var_ready, 1)
            dve.wait_ge(dev_ready, 2)
            link(dve.reciprocal(rstd[:, 0:ALL], dev[:, 0:ALL]))
            with dve.Fori(0, GROUPS_ALL // 2) as gg:
                normalised(gg, 1, h)
                for i in range(2):
                    g = 2 * gg + i
                    dve.wait_ge(product_full, GROUPS_ALL + g + 1)
                    dve.tensor_copy(logits[:, :, :].rearrange("p t e -> p (t e)")[:, ds(g * GTOK * EXPERTS, GTOK * EXPERTS)],
                                    up[i][:, 0:GTOK * EXPERTS]).then_inc(product_free, 1)
            dve.wait_ge(product_free, 2 * GROUPS_ALL + 1)

            def over_experts(a):
                return a[:, :].unsqueeze(2).broadcast_to([P, ALL, EXPERTS])

            def pick_first(dst, values, top):
                link(dve.tensor_reduce(top[:, :], values[:, :, :], AX.X, ALU.max))
                link(dve.tensor_tensor(dst[:, :, :], values[:, :, :], over_experts(top), ALU.is_equal))
                ranks = rank[:, :].unsqueeze(1).broadcast_to([P, ALL, EXPERTS])
                link(dve.tensor_tensor(dst[:, :, :], dst[:, :, :], ranks, ALU.mult))
                link(dve.tensor_reduce(first_at[:, :], dst[:, :, :], AX.X, ALU.max))
                link(dve.tensor_tensor(dst[:, :, :], dst[:, :, :], over_experts(first_at), ALU.is_equal))

            pick_first(pick, logits, best)
            link(dve.scalar_tensor_tensor(out=logits[:, :, :], in0=pick[:, :, :], scalar=MASKED, in1=logits[:, :, :],
                                          op0=ALU.mult, op1=ALU.add))
            pick_first(other, logits, second)
            dve.tensor_tensor(chosen[:, :, :], pick[:, :, :], other[:, :, :], ALU.add).then_inc(chosen_ready, 1)
            dve.tensor_tensor(second[:, :], second[:, :], best[:, :], ALU.subtract).then_inc(gap_ready, 1)
            dve.wait_ge(ratio_ready, 1)
            link(dve.tensor_scalar(share[:, :], ratio[:, :], 1.0, None, ALU.add))
            link(dve.reciprocal(share[:, :], share[:, :]))
            link(dve.tensor_tensor(ratio[:, :], ratio[:, :], share[:, :], ALU.mult))

            def by_half(flat):
                return flat.rearrange("p (a t e) -> p a t e", a=HALVES, e=EXPERTS)

            dve.wait_ge(counts_full, 1)
            tile_counts = by_half(up[1][:, 0:FLAT])
            src, dst = count0, count1
            link(dve.tensor_copy(src[:, :, :, :], tile_counts))
            reach = 1
            while reach < HALF_TILES:
                dve.tensor_copy(dst[:, :, 0:reach, :], src[:, :, 0:reach, :])
                link(dve.tensor_tensor(dst[:, :, reach:, :], src[:, :, reach:, :], src[:, :, 0:HALF_TILES - reach, :], ALU.add))
                src, dst, reach = dst, src, 2 * reach
            counts = src
            link(dve.tensor_scalar(blocks_int[:, :, :], counts[:, :, HALF_TILES - 1, :], float(P - 1), None, ALU.add))
            link(dve.tensor_scalar(blocks_int[:, :, :], blocks_int[:, :, :], P.bit_length() - 1, None, ALU.logical_shift_right))
            link(dve.tensor_copy(blocks[:, :, :], blocks_int[:, :, :]))
            link(dve.tensor_copy(first0[:, :, :], blocks[:, :, :]))
            f_src, f_dst, reach = first0, first1, 1
            while reach < EXPERTS:
                dve.tensor_copy(f_dst[:, :, 0:reach], f_src[:, :, 0:reach])
                link(dve.tensor_tensor(f_dst[:, :, reach:], f_src[:, :, reach:], f_src[:, :, 0:EXPERTS - reach], ALU.add))
                f_src, f_dst, reach = f_dst, f_src, 2 * reach
            firsts = f_dst
            link(dve.tensor_tensor(firsts[:, :, :], f_src[:, :, :], blocks[:, :, :], ALU.subtract))
            link(dve.tensor_tensor(place[:, :, :, :], counts[:, :, :, :], tile_counts, ALU.subtract))
            link(dve.tensor_tensor(place[:, :, :, :], place[:, :, :, :], by_half(up[0][:, 0:FLAT]), ALU.add))
            for a in range(HALVES):
                ins = dve.scalar_tensor_tensor(out=place[:, a, :, :], in0=firsts[:, a, :].unsqueeze(1).broadcast_to([P, HALF_TILES, EXPERTS]),
                                               scalar=float(P), in1=place[:, a, :, :], op0=ALU.mult, op1=ALU.add)
            link(ins)
            for n, mine in enumerate((pick, other)):
                link(dve.tensor_tensor(dst[:, :, :, :], by_half(mine[:, :, :].rearrange("p t e -> p (t e)")), place[:, :, :, :], ALU.mult))
                link(dve.tensor_reduce(row_of32[:, n, :], dst[:, :, :, :].rearrange("p a t e -> p (a t) e"), AX.X, ALU.add))
            dve.tensor_copy(row_of[:, :, :], row_of32[:, :, :]).then_inc(places_ready, 1)
            numbers = up[1][0:1, FLAT:FLAT + HALF_NB].unsqueeze(2).broadcast_to([1, HALF_NB, EXPERTS])
            for a in range(HALVES):
                ins = dve.tensor_tensor(at_block[:, a * HALF_NB:(a + 1) * HALF_NB, :], numbers,
                                        firsts[0:1, a, :].unsqueeze(1).broadcast_to([1, HALF_NB, EXPERTS]), ALU.is_ge)
            link(ins)
            link(dve.tensor_reduce(expert_sum[:, :], at_block[:, :, :], AX.X, ALU.add))
            dve.tensor_scalar(expert_of[:, :], expert_sum[:, :], -1.0, None, ALU.add).then_inc(table_ready, 1)
            for c in range(CHUNKS):
                e, mat, cols = chunk(c)
                if mat == 2:
                    dve.wait_ge(weight_full, c + 1)
                    ins = dve.tensor_copy(w_down[:, cols], out[c % 2][:, :])
                else:
                    dve.wait_ge(weight_hi, 2 * e + mat + 1)
                    ins = dve.tensor_tensor(w_lo[mat][:, cols], out[c % 2][:, :], w_hi[mat][:, cols].bitcast(F32), ALU.subtract)
                ins.then_inc(weight_free, 1)

            def rows_in(b, fresh):
                p = b[1] % 2
                dve.wait_ge(t_turned, number(b) + 1)
                if not fresh:
                    dve.wait_ge(t_lo_ready, number(b) - 1)
                dve.tensor_scalar(t32[p][:, :], t_turn[:, 0:P], k["ln_cols"][:, 2:3], k["ln_cols"][:, 3:4],
                                  ALU.mult, ALU.add).then_inc(t32_ready, 1)
                dve.wait_ge(t_hi_ready, number(b) + 1)
                dve.tensor_tensor(t_lo[p][:, :], t32[p][:, :], t_hi[p][:, :].bitcast(F32), ALU.subtract).then_inc(t_lo_ready, 1)

            def result(b, fresh):
                p = b[1] % 2
                dve.wait_ge(y_full, number(b) + 1)
                if not fresh:
                    dve.wait_ge(y_stored[p], half(b) * 16)
                dve.tensor_copy(y_rows[p][:, :], y_ps[:, 0:DIM]).then_inc(y_ready, 1)

            def body(it, first):
                for i in range(UNROLL):
                    b, p = (it, i), i % 2
                    rows_in((it, i + 1), first and i < 1)
                    dve.wait_ge(silu_ready[p], half(b) + 1)
                    dve.wait_ge(up_full, number(b) + 1)
                    if not (first and i < 2):
                        dve.wait_ge(inner_turned, number(b) - 1)
                    dve.tensor_tensor(inner[p][:, :], silu[p][:, :], up[p][:, :], ALU.mult).then_inc(inner_ready[p], 1)
                    if not (first and i < 2):
                        result(earlier(b, 2), first and i < 4)

            rows_in((0, 0), True)
            body(0, True)
            with dve.Fori(1, NB // UNROLL) as it:
                body(it, False)
            for n in (2, 1):
                result((NB // UNROLL, -n), False)
            dve.wait_ge(x_summed, 1)
            for j in range(HALVES * SENT):
                t, n = divmod(j, TOP)
                if j % BATCHED == 0:
                    dve.wait_ge(landed[j // BATCHED], 16 * BATCHED)
                if n:
                    dve.wait_ge(first_added, t + 1)
                xs = k["x"][:, t * DIM:(t + 1) * DIM]
                ins = dve.scalar_tensor_tensor(out=xs, in0=landing[j // SENT][:, j % SENT * DIM:(j % SENT + 1) * DIM], scalar=(share, ratio)[n][:, t:t + 1], in1=xs,
                                               op0=ALU.mult, op1=ALU.add)
                if n == 0:
                    ins.then_inc(first_added, 1)

        phase.close()
        clear_semaphores(nc, sems)


def message_phase(nc, k):
    PREP = 6
    UNITS_BATCH = 2 + PREP * CH + 2 + 2
    LINKS = MOMENT_LINKS + 2
    STEPS = CH * TILES
    with ExitStack() as ctx, ExitStack() as phase:
        def sb(n, shape, dt=F32):
            return ctx.enter_context(nc.sbuf_tensor(f"m_{n}", shape, dt))

        sems = []

        def sem(n):
            sems.append(ctx.enter_context(nc.semaphore(f"m_{n}")))
            return sems[-1]

        stats = sb("stats", [P, TILES, 6])
        mean, spread, work, dev, rstd = (sb(n, [P, TILES]) for n in ("mean", "spread", "work", "dev", "rstd"))
        z = sb("z", [P, TILES, DIM])
        zT = sb("zT", [P, SEQ])
        twice = [sb(f"twice{i}", [P, 2, 2, RANK]) for i in range(2)]
        u_st = [sb(f"u_st{i}", [P, SEQ], F32R) for i in range(2)]
        v_hi = [sb(f"v_hi{i}", [P, SEQ], F32R) for i in range(2)]
        v_lo = [sb(f"v_lo{i}", [P, SEQ], F32R) for i in range(2)]
        uv_tok = [sb(f"uv_tok{i}", [P, TILES, 2, RANK]) for i in range(2)]
        f_sig = [sb(f"f_sig{i}", [P, SEQ]) for i in range(2)]
        t_sig = [sb(f"t_sig{i}", [P, SEQ]) for i in range(2)]
        vuT = sb("vuT", [P, CH * SEQ])
        msgT = zT
        f_ps, t_ps, vu_ps = (ctx.enter_context(nc.psum_tensor(f"m_{n}", [P, SEQ], F32)) for n in ("f_ps", "t_ps", "vu_ps"))
        unit = [ctx.enter_context(nc.psum_tensor(f"m_unit{i}", [P, HALF], F32)) for i in range(2)]

        link_sem, var_ready, dev_ready, z_ready, twice_ready, unit_full, hi_ready = (
            sem(n) for n in ("link", "var_ready", "dev_ready", "z_ready", "twice_ready", "unit_full", "hi_ready"))
        f_full, t_full, f_ready, t_ready, vu_free = (sem(n) for n in ("f_full", "t_full", "f_ready", "t_ready", "vu_free"))
        unit_free = [sem(f"unit_free{i}") for i in range(2)]
        used = [sem(f"used{i}") for i in range(2)]
        block = phase.enter_context(nc.Block())

        class Units:

            def __init__(self, base, halves):
                self.base, self.halves, self.n = base, halves, -1

            def next(self):
                self.n += 1
                return unit[self.n % 2]

            def wait_empty(self, eng):
                eng.wait_ge(unit_free[self.n % 2], self.halves + self.n // 2 + 1)

            def wait_full(self, eng):
                eng.wait_ge(unit_full, self.base + self.n + 1)

            def wait_emptied(self, eng, n):
                eng.wait_ge(unit_free[n % 2], self.halves + n // 2 + 2)

            def free(self):
                return unit_free[self.n % 2]

        def units_at(b, pairs):
            return Units(b * UNITS_BATCH + pairs * 2, b * (UNITS_BATCH // 2) + pairs)

        def channels(eng, b, body):
            with eng.Fori(0, CH // 2 - 1) as cc:
                for p in range(2):
                    body(b, 2 * cc + p, p, False)
            for p in range(2):
                body(b, CH - 2 + p, p, True)

        @block.tensor
        def _(pe):
            def prepare(u, i, c, p, b):
                out = u.next()
                u.wait_empty(pe)
                if i == 0:
                    pe.wait_ge(twice_ready, b * CH + c + 1)
                if i < 4:
                    mm = pe.matmul(out[:, :], twice[p][:, i // 2, :, :].rearrange("p d r -> p (d r)"),
                                   zT[:, (i % 2) * HALF:(i % 2 + 1) * HALF], start=True, stop=True)
                else:
                    for t in range(4):
                        tile = (i - 4) * 4 + t
                        mm = pe.matmul(out[:, t * P:(t + 1) * P], zT[:, tile * P:(tile + 1) * P],
                                       k["uvT"][:, ds(c * P, P)], start=True, stop=True)
                mm.then_inc(unit_full, 1)

            def blocks(b, c, i, p):
                step = (b * CH + c) * TILES + i
                rows = slice(i * P, (i + 1) * P)
                pe.wait_ge(f_ready, step + 1)
                for n in range(2):
                    cols = slice(n * HALF, (n + 1) * HALF)
                    pe.matmul(f_ps[:, cols], u_st[p][:, rows], v_hi[p][:, cols], start=True, stop=False)
                    mm = pe.matmul(f_ps[:, cols], u_st[p][:, rows], v_lo[p][:, cols], start=False, stop=True)
                mm.then_inc(f_full, 1)
                pe.wait_ge(t_ready, step + 1)
                for n in range(2):
                    cols = slice(n * HALF, (n + 1) * HALF)
                    pe.matmul(t_ps[:, cols], v_hi[p][:, rows], u_st[p][:, cols], start=True, stop=False)
                    mm = pe.matmul(t_ps[:, cols], v_lo[p][:, rows], u_st[p][:, cols], start=False, stop=True)
                mm.then_inc(t_full, 1)

            def products(b, c, i, p):
                step = (b * CH + c) * TILES + i
                if i == 0:
                    pe.wait_ge(vu_free, b * CH + c + 1)
                pe.wait_ge(f_ready, step + 2)
                pe.wait_ge(t_ready, step + 2)
                for n in range(2):
                    cols = slice(n * HALF, (n + 1) * HALF)
                    pe.matmul(vu_ps[0:RANK, cols], uv_tok[p][:, i, 1, :], t_sig[i % 2][:, cols], start=(i == 0), stop=(i == TILES - 1))
                    mm = pe.matmul(vu_ps[RANK:P, cols], uv_tok[p][:, i, 0, :], f_sig[i % 2][:, cols], start=(i == 0), stop=(i == TILES - 1))
                mm.then_inc(used[i % 2], 1)

            with pe.Fori(0, BATCH) as b:
                u = units_at(b, 0)
                pe.wait_ge(z_ready, b + 1)
                for i in range(2):
                    out = u.next()
                    u.wait_empty(pe)
                    for t in range(4):
                        mm = pe.transpose(out[:, t * P:(t + 1) * P], z[:, 4 * i + t, :], k["ident"][:, :])
                    mm.then_inc(unit_full, 1)
                for n in (0, 1):
                    u.wait_emptied(pe, n)
                for i in range(PREP):
                    prepare(u, i, 0, 0, b)
                for n in (u.n - 1, u.n):
                    u.wait_emptied(pe, n)
                blocks(b, 0, 0, 0)

                def body(b, c, p, last_pair):
                    last = last_pair and p == 1
                    u = units_at(b, 1 + PREP // 2 * (c + 1))
                    for i in range(TILES):
                        if i < TILES - 1:
                            blocks(b, c, i + 1, p)
                        elif not last:
                            for n in (u.n - 1, u.n):
                                u.wait_emptied(pe, n)
                            blocks(b, c + 1, 0, 1 - p)
                        if i < PREP and not last:
                            prepare(u, i, c + 1, 1 - p, b)
                        products(b, c, i, p)
                channels(pe, b, body)

                u = units_at(b, 1 + PREP // 2 * CH)
                pe.wait_ge(vu_free, (b + 1) * CH + 1)
                for i in range(2):
                    out = u.next()
                    u.wait_empty(pe)
                    for c in range(CH):
                        mm = pe.matmul(out[:, :], k["uv"][:, c * DIM:(c + 1) * DIM], vuT[:, c * SEQ + i * HALF:c * SEQ + (i + 1) * HALF],
                                       start=(c == 0), stop=(c == CH - 1))
                    mm.then_inc(unit_full, 1)
                for i in range(2):
                    u.wait_emptied(pe, i)
                    out = u.next()
                    u.wait_empty(pe)
                    for t in range(4):
                        mm = pe.transpose(out[:, t * P:(t + 1) * P], msgT[:, (4 * i + t) * P:(4 * i + t + 1) * P], k["ident"][:, :])
                    mm.then_inc(unit_full, 1)

        @block.gpsimd
        def _(pool):
            start_free(pool, *unit_free, *used, f_ready, t_ready, vu_free)

        @block.scalar
        def _(act):
            def high_parts(u, p):
                for i in range(4):
                    src = u.next()
                    u.wait_full(act)
                    dst = (u_st, v_hi)[i // 2][p]
                    act.copy(dst[:, (i % 2) * HALF:(i % 2 + 1) * HALF], src[:, :]).then_inc(hi_ready, 1)
                u.n += 2

            def sigmoids(b, c, i):
                step = (b * CH + c) * TILES + i
                act.wait_ge(used[i % 2], (b * CH + c) * (TILES // 2) + i // 2 + 1)
                act.wait_ge(f_full, step + 1)
                act.activation(f_sig[i % 2][:, :], f_ps[:, :], ACT.Sigmoid).then_inc(f_ready, 1)
                act.wait_ge(t_full, step + 1)
                act.activation(t_sig[i % 2][:, :], t_ps[:, :], ACT.Sigmoid).then_inc(t_ready, 1)

            with act.Fori(0, BATCH) as b:
                act.wait_ge(var_ready, b + 1)
                act.activation(dev[:, :], spread[:, :], ACT.Sqrt).then_inc(dev_ready, 1)
                high_parts(units_at(b, 1), 0)
                sigmoids(b, 0, 0)

                def body(b, c, p, last_pair):
                    last = last_pair and p == 1
                    u = units_at(b, 1 + PREP // 2 * (c + 1))
                    for i in range(TILES):
                        if i < TILES - 1:
                            sigmoids(b, c, i + 1)
                        elif not last:
                            sigmoids(b, c + 1, 0)
                        if i < 4 and not last:
                            src = u.next()
                            u.wait_full(act)
                            dst = (u_st, v_hi)[i // 2][1 - p]
                            act.copy(dst[:, (i % 2) * HALF:(i % 2 + 1) * HALF], src[:, :]).then_inc(hi_ready, 1)
                channels(act, b, body)
                u = units_at(b, 1 + PREP // 2 * CH)
                for i in range(2):
                    src = u.next()
                    u.wait_full(act)
                    act.copy(msgT[:, i * HALF:(i + 1) * HALF], src[:, :]).then_inc(u.free(), 1)

        @block.vector
        def _(dve):
            def prepared(u, i, c, p, b):
                src = u.next()
                u.wait_full(dve)
                cols = slice((i % 2) * HALF, (i % 2 + 1) * HALF)
                if i < 4:
                    dve.wait_ge(hi_ready, (b * CH + c) * 4 + i + 1)
                if i < 2:
                    ins = dve.tensor_tensor(u_st[p][RANK:P, cols], src[RANK:P, :], u_st[p][RANK:P, cols].bitcast(F32), ALU.subtract)
                elif i < 4:
                    ins = dve.tensor_tensor(v_lo[p][:, cols], src[:, :], v_hi[p][:, cols].bitcast(F32), ALU.subtract)
                else:
                    ins = dve.tensor_copy(uv_tok[p][:, 4 * (i - 4):4 * (i - 3), :, :].rearrange("p t a r -> p (t a r)"), src[:, :])
                ins.then_inc(u.free(), 1)

            def double(c, p):
                src = k["uvT"][:, ds(c * P, P)].rearrange("p (a r) -> p a r", a=2)
                for i in range(2):
                    ins = dve.tensor_scalar(twice[p][:, :, i, :], src, 1.0, None, ALU.mult)
                ins.then_inc(twice_ready, 1)

            with dve.Fori(0, BATCH) as b:
                link = Link(dve, link_sem, b * LINKS)

                def x_tile(t):
                    return k["x"][:, ds((b * TILES + t) * DIM, DIM)]
                for t in range(TILES):
                    ins = dve.bn_stats(stats[:, t, :], x_tile(t))
                link(ins)
                row_moments(dve, link, stats, mean[:, :], spread[:, :], work[:, :], TILES).then_inc(var_ready, 1)
                for p in range(2):
                    double(p, p)
                dve.wait_ge(dev_ready, b + 1)
                link(dve.reciprocal(rstd[:, :], dev[:, :]))
                for t in range(TILES):
                    ins = dve.tensor_scalar(z[:, t, :], x_tile(t), mean[:, t:t + 1], rstd[:, t:t + 1], ALU.subtract, ALU.mult)
                ins.then_inc(z_ready, 1)
                u = units_at(b, 0)
                for i in range(2):
                    src = u.next()
                    u.wait_full(dve)
                    dve.tensor_copy(zT[:, i * HALF:(i + 1) * HALF], src[:, :]).then_inc(u.free(), 1)
                for i in range(PREP):
                    prepared(u, i, 0, 0, b)

                def body(b, c, p, last_pair):
                    last = last_pair and p == 1
                    u = units_at(b, 1 + PREP // 2 * (c + 1))
                    if not last_pair:
                        double(c + 2, p)
                    for i in range(PREP if not last else 0):
                        prepared(u, i, c + 1, 1 - p, b)
                    dve.wait_ge(used[1], (b * CH + c + 1) * (TILES // 2) + 1)
                    dve.tensor_copy(vuT[:, ds(c * SEQ, SEQ)], vu_ps[:, :]).then_inc(vu_free, 1)
                channels(dve, b, body)
                u = units_at(b, 1 + PREP // 2 * CH)
                u.n += 2
                for i in range(2):
                    src = u.next()
                    u.wait_full(dve)
                    x4 = k["x"][:, ds(b * TILES * DIM + i * HALF, HALF)]
                    dve.tensor_tensor(x4, x4, src[:, :], ALU.add).then_inc(u.free(), 1)

        phase.close()
        clear_semaphores(nc, sems)


def store_phase(nc, k, out):
    with ExitStack() as ctx:
        stored = ctx.enter_context(nc.semaphore("stored"))
        block = ctx.enter_context(nc.Block())

        @block.sync
        def _(sp):
            sp.dma_start(out.rearrange("b (n p) e -> p (b n) e", p=P),
                         k["x"][:, :].rearrange("p (n e) -> p n e", e=DIM)).then_inc(stored, 16)
            sp.wait_ge(stored, 16)


def hybrid_kernel(nc, d, out):
    def allocate(ctx, k, shapes):
        for name, (shape, dt) in shapes.items():
            k[name] = ctx.enter_context(nc.sbuf_tensor(name, shape, dt))

    k = {name: [nc.dram_tensor(f"{name}{i}", (HALF_NB * P, DIM), F32, kind="Internal").ap() for i in range(HALVES)]
         for name in ("sent_rows", "result_rows")}
    with ExitStack() as whole:
        allocate(whole, k, {"x": ([P, ALL * DIM], F32),
                            "ident": ([P, P], F32), "ln_cols": ([P, 4], F32),
                            "attn_wT": ([P, DIM], F32), "gate_wT": ([P, EXPERTS], F32)})
        with ExitStack() as attention:
            allocate(attention, k, {"ident16": ([P, P], BF16), "mask": ([P, P], BF16),
                                    "w_qkv": ([P, 3 * DIM], F32), "w_o": ([P, DIM], F32),
                                    "ln_rows": ([P, 4 * HD], F32), "bo_rows": ([P, DIM], F32)})
            setup_phase(nc, d, k)
            attention_phase(nc, k)
        moe_phase(nc, d, k, "f1", True)
        with ExitStack() as message:
            allocate(message, k, {"uv": ([P, CH * DIM], F32), "uvT": ([P, CH * P], F32)})
            factors_phase(nc, d, k)
            message_phase(nc, k)
        moe_phase(nc, d, k, "f2", False)
        store_phase(nc, k, out)


_INS = {'x': 'L0_attn_a_x', 'Wk': 'L0_attn_a_Wk', 'Wq': 'L0_attn_a_Wq', 'Wv': 'L0_attn_a_Wv', 'Wo': 'L0_attn_a_Wo',
        'bo': 'L0_attn_a_bo', 'kln_w': 'L0_attn_a_kln_w', 'kln_b': 'L0_attn_a_kln_b', 'qln_w': 'L0_attn_a_qln_w',
        'qln_b': 'L0_attn_a_qln_b', 'u': 'L0_attn_b_ternary_factor_u', 'v': 'L0_attn_b_ternary_factor_v',
        'ln1_g': 'L0_ffn_ln1_g', 'ln1_b': 'L0_ffn_ln1_b', 'attn_w': 'L0_ffn_attn_w', 'ln2_g': 'L0_ffn_ln2_g',
        'ln2_b': 'L0_ffn_ln2_b', 'gate_w': 'L0_ffn_gate_w', 'gate_proj': 'L0_ffn_gate_proj',
        'up_proj': 'L0_ffn_up_proj', 'down_proj': 'L0_ffn_down_proj'}


def kernel(**inputs):
    import numpy as _np
    import concourse.bacc as _bacc
    from concourse import mybir as _mybir
    from concourse.bass_utils import run_bass_kernel_spmd as _run

    nc = _bacc.Bacc("TRN2", target_bir_lowering=False, num_devices=1)
    arrays, aps = {}, {}
    for short, name in _INS.items():
        a = _np.ascontiguousarray(inputs[name])
        arrays[f"in_{name}_dram"] = a
        aps[short] = nc.dram_tensor(f"in_{name}_dram", a.shape, _mybir.dt.from_np(a.dtype), kind="ExternalInput").ap()
    out = nc.dram_tensor("out_0_dram", (BATCH, SEQ, DIM), F32, kind="ExternalOutput").ap()
    hybrid_kernel(nc, aps, out)
    r = _run(nc, [arrays], core_ids=[0])
    return r.results[0]["out_0_dram"]
```

```python
from contextlib import ExitStack

import concourse.bass as bass
from concourse import mybir

F32 = mybir.dt.float32
F32R = mybir.dt.float32r
BF16 = mybir.dt.bfloat16
U32 = mybir.dt.uint32
I32 = mybir.dt.int32
ALU = mybir.AluOpType
ACT = mybir.ActivationFunctionType
AX = mybir.AxisListType

P = 128
BATCH, SEQ, DIM = 4, 1024, 128
TILES = SEQ // P
ALL = BATCH * TILES
HALF = 512
EPS = 1e-5

HEADS, HD = 16, 8
GROUP = 4
GROUPS = HEADS // GROUP
STACK = P // GROUP
MASKED = -1e30

CH, RANK = 16, 64
MSG_SCALE = 0.03125

EXPERTS, INTER = 8, 512
BLOCKS = INTER // P
UNITS = EXPERTS * BLOCKS
GTOK = 4
TOP = 2
UNROLL = 8
HALVES = 2
HALF_NB = -(-(TOP * ALL // HALVES + EXPERTS - 1) // UNROLL) * UNROLL
NB = HALVES * HALF_NB
AHEAD = 6
CONSTS = 4


def ds(start, size):
    return bass.DynSlice(start, size)


class Link:

    def __init__(self, eng, sem, base=0):
        self.eng, self.sem, self.base, self.n = eng, sem, base, 0

    def __call__(self, ins):
        self.n += 1
        ins.then_inc(self.sem, 1)
        self.eng.wait_ge(self.sem, self.base + self.n)


def row_moments(dve, link, stats, mean, spread, work, tiles, spread_twice=None):
    even, odd = stats[:, 0:tiles, 1], stats[:, 0:tiles, 4]
    link(dve.tensor_tensor(mean, even, odd, ALU.add))
    link(dve.tensor_tensor(work, even, odd, ALU.subtract))
    link(dve.scalar_tensor_tensor(out=work, in0=work, scalar=0.25, in1=work, op0=ALU.mult, op1=ALU.mult))
    link(dve.tensor_tensor(spread, stats[:, 0:tiles, 2], stats[:, 0:tiles, 5], ALU.add))
    link(dve.scalar_tensor_tensor(out=spread, in0=spread, scalar=1.0 / DIM, in1=work, op0=ALU.mult, op1=ALU.add))
    link(dve.tensor_scalar(mean, mean, 0.5, None, ALU.mult))
    if spread_twice is not None:
        link(dve.tensor_scalar(spread_twice, spread, 1.0 + EPS, EPS * EPS, ALU.mult, ALU.add))
    return dve.tensor_scalar(spread, spread, EPS, None, ALU.add)


MOMENT_LINKS = 6


def start_free(eng, *sems):
    for s in sems:
        eng.sem_inc(s, 1)


def clear_semaphores(nc, sems):
    with nc.Block() as block:
        @block.gpsimd
        def _(pool):
            numbers = sorted(s.num for s in sems)
            while numbers:
                n = 1
                while n < len(numbers) and numbers[n] == numbers[0] + n:
                    n += 1
                pool.sem_clear(range(numbers[0], numbers[0] + n))
                del numbers[:n]


def setup_phase(nc, d, k):
    with ExitStack() as ctx, ExitStack() as phase:
        def sb(name, shape, dt=F32):
            return ctx.enter_context(nc.sbuf_tensor(name, shape, dt))

        sems = []

        def sem(name):
            sems.append(ctx.enter_context(nc.semaphore(name)))
            return sems[-1]

        small_raw = sb("small_raw", [P, 2, DIM])
        vec_row = sb("vec_row", [1, 4 * HD + DIM])
        ones_row = sb("ones_row", [1, P])
        vec_rows = ctx.enter_context(nc.psum_tensor("vec_rows", [P, HALF], F32))
        small_turned = ctx.enter_context(nc.psum_tensor("small_turned", [P, HALF], F32))

        x_in, attn_in, small_in, vec_in, col_in = (
            sem(n) for n in ("x_in", "attn_in", "small_in", "vec_in", "col_in"))
        ident_zero, ident_done, consts_done, ones_done, ident16_done, vec_full, small_full, copied = (
            sem(n) for n in ("ident_zero", "ident_done", "consts_done", "ones_done", "ident16_done", "vec_full", "small_full", "copied"))
        block = phase.enter_context(nc.Block())

        @block.sync
        def _(sp):
            sp.dma_start(k["x"][:, :].rearrange("p (n e) -> p n e", e=DIM),
                         d["x"].rearrange("b (n p) e -> p (b n) e", p=P)).then_inc(x_in, 16)
            for i, name in enumerate(("qln_w", "qln_b", "kln_w", "kln_b")):
                sp.dma_start(vec_row[0:1, i * HD:(i + 1) * HD],
                             d[name].rearrange("(a s) -> a s", a=1)).then_inc(vec_in, 16)
            sp.dma_start(vec_row[0:1, 4 * HD:], d["bo"].rearrange("(a s) -> a s", a=1)).then_inc(vec_in, 16)
            for i, name in enumerate(("Wq", "Wk", "Wv")):
                sp.dma_start(k["w_qkv"][:, i * DIM:(i + 1) * DIM], d[name]).then_inc(attn_in, 16)
            sp.dma_start(k["w_o"][:, :], d["Wo"]).then_inc(attn_in, 16)
            sp.dma_start(small_raw[:, 0, :], d["attn_w"]).then_inc(small_in, 16)
            sp.dma_start(small_raw[0:EXPERTS, 1, :], d["gate_w"]).then_inc(small_in, 16)
            for i, name in enumerate(("ln1_g", "ln1_b", "ln2_g", "ln2_b")):
                sp.dma_start(k["ln_cols"][:, i:i + 1], d[name].rearrange("(p a) -> p a", a=1)).then_inc(col_in, 16)
            sp.wait_ge(x_in, 16)
            sp.wait_ge(attn_in, 64)
            sp.wait_ge(col_in, 64)

        @block.scalar
        def _(act):
            act.wait_ge(small_full, 1)
            act.copy(k["attn_wT"][:, :], small_turned[:, 0:DIM])
            act.copy(k["gate_wT"][:, :], small_turned[:, DIM:DIM + EXPERTS]).then_inc(copied, 1)

        @block.gpsimd
        def _(pool):
            pool.memset(k["ident"][:, :], 0.0).then_inc(ident_zero, 1)
            pool.memset(k["mask"][:, :], 0.0).then_inc(ident_zero, 1)
            pool.wait_ge(ident_zero, 2)
            pool.affine_select(out=k["ident"][:, :], in_=k["ident"][:, :], compare_op=ALU.not_equal, fill=1.0,
                               base=0, pattern=[[-1, P]], channel_multiplier=1).then_inc(ident_done, 1)
            pool.affine_select(out=k["mask"][:, :], in_=k["mask"][:, :], compare_op=ALU.is_ge, fill=MASKED,
                               base=0, pattern=[[-1, P]], channel_multiplier=1).then_inc(consts_done, 1)

        @block.vector
        def _(dve):
            dve.memset(ones_row[:, :], 1.0).then_inc(ones_done, 1)
            dve.wait_ge(ident_done, 1)
            dve.tensor_copy(k["ident16"][:, :], k["ident"][:, :]).then_inc(ident16_done, 1)
            dve.wait_ge(vec_full, 1)
            dve.tensor_scalar(k["ln_rows"][:, 0:2 * HD], vec_rows[:, 0:2 * HD], HD ** -0.5, None, ALU.mult)
            dve.tensor_copy(k["ln_rows"][:, 2 * HD:4 * HD], vec_rows[:, 2 * HD:4 * HD])
            dve.tensor_copy(k["bo_rows"][:, :], vec_rows[:, 4 * HD:4 * HD + DIM]).then_inc(copied, 1)

        @block.tensor
        def _(pe):
            pe.wait_ge(ident_done, 1)
            pe.wait_ge(ones_done, 1)
            pe.wait_ge(vec_in, 80)
            pe.matmul(vec_rows[:, 0:4 * HD + DIM], ones_row[:, :], vec_row[:, :], start=True, stop=True).then_inc(vec_full, 1)
            pe.wait_ge(small_in, 32)
            pe.transpose(small_turned[:, 0:DIM], small_raw[:, 0, :], k["ident"][:, :])
            pe.transpose(small_turned[:, DIM:DIM + EXPERTS], small_raw[0:EXPERTS, 1, :],
                         k["ident"][0:EXPERTS, 0:EXPERTS]).then_inc(small_full, 1)

        phase.close()
        clear_semaphores(nc, sems)


def attention_phase(nc, k):
    STEPS_BATCH = GROUPS * TILES
    SCORE_UNITS = GROUPS * 43
    BANKS = 4
    MAX_UNITS = 43
    UNITS_AHEAD = 2 + TILES + 4 + MAX_UNITS + 2
    UNITS_BATCH = 2 + TILES + GROUPS * (4 + MAX_UNITS + 2 + 2) + 6
    LINKS_AHEAD = MOMENT_LINKS + 2 + 23 + 2
    LINKS = MOMENT_LINKS + 2 + 23 + GROUPS * (2 + 2) + 4
    with ExitStack() as ctx, ExitStack() as phase:
        def sb(name, shape, dt=F32):
            return ctx.enter_context(nc.sbuf_tensor(name, shape, dt))

        sems = []

        def sem(name):
            sems.append(ctx.enter_context(nc.semaphore(name)))
            return sems[-1]

        stats, mean, spread, work, dev, rstd = (sb(n, [P, TILES, 6] if n == "a_stats" else [P, TILES]) for n in
                                                ("a_stats", "a_mean", "a_spread", "a_work", "a_dev", "a_rstd"))
        z = sb("a_z", [P, TILES, DIM])
        zT = sb("a_zT", [P, SEQ])
        qk = sb("a_qk", [P, TILES, 2, HEADS, HD])
        prob = [sb(f"a_prob{i}", [P, GROUP, SEQ]) for i in range(2)]
        qk_sum, qk_var, qk_dev, qk_rstd = (sb(n, [P, TILES * 2 * HEADS]) for n in ("a_qk_sum", "a_qk_var", "a_qk_dev", "a_qk_rstd"))
        v_next = sb("a_v_next", [P, TILES, HEADS, HD])
        v1 = sb("a_v1", [P, TILES, HEADS, STACK])
        q_st = sb("a_q_st", [P, TILES, HEADS, STACK])
        k_st = sb("a_k_st", [P, TILES, HEADS, STACK])
        qT = [sb(f"a_qT{i}", [P, SEQ], F32R) for i in range(2)]
        qmT = [sb(f"a_qmT{i}", [P, SEQ], F32R) for i in range(2)]
        kT = [sb(f"a_kT{i}", [P, GROUP, SEQ], F32R) for i in range(2)]
        maxima = sb("a_maxima", [P, TILES, GROUP, 2])
        oT = sb("a_oT", [P, SEQ])
        o_den = [sb(f"a_o_den{i}", [P, 4, GROUP]) for i in range(2)]
        o_tok = sb("a_o_tok", [P, TILES, HEADS, HD])
        o_tokT = sb("a_o_tokT", [P, SEQ])
        qk_sq = o_tokT[:, :].rearrange("p (t h s) -> p t h s", h=HEADS, s=HD)
        proj = [sb(f"a_proj{i}", [P, 2, DIM]) for i in range(BANKS)]

        score = [ctx.enter_context(nc.psum_tensor(f"a_score{i}", [P, HALF], F32)) for i in range(2)]
        o_acc = ctx.enter_context(nc.psum_tensor("a_o_acc", [P, SEQ], F32))
        unit = [ctx.enter_context(nc.psum_tensor(f"a_unit{i}", [P, HALF], F32)) for i in range(BANKS)]

        cleared, link_sem, var_ready, dev_ready, z_ready, stack_ready, shift_ready = (
            sem(n) for n in ("a_cleared", "a_link", "a_var_ready", "a_dev_ready", "a_z_ready", "a_stack_ready", "a_shift_ready"))
        v_ready = sem("a_v_ready")
        unit_full, score_full, o_free, kT_cleared = (sem(n) for n in ("a_unit_full", "a_score_full", "a_o_free", "a_kT_cleared"))
        unit_free = [sem(f"a_unit_free{i}") for i in range(BANKS)]
        prob_ready = [sem(f"a_prob_ready{i}") for i in range(2)]
        pv_done = [sem(f"a_pv_done{i}") for i in range(2)]
        block = phase.enter_context(nc.Block())

        def max_units():
            for qt in range(TILES):
                w = (qt + 1) * P
                if w <= HALF:
                    per = min(GROUP, HALF // w) if w != 384 else 1
                    for h in range(0, GROUP, per):
                        yield qt, range(h, h + per), 0, w, True, 0
                else:
                    for h in range(GROUP):
                        yield qt, range(h, h + 1), 0, HALF, False, 0
                        yield qt, range(h, h + 1), HALF, w - HALF, True, 1

        MAXES = list(max_units())
        assert len(MAXES) == MAX_UNITS

        def stacks_at(g):
            return 0 if g + 1 < GROUPS else 1

        def max_slice(g, j):
            ends = (0, 0, 8, 16, 24, 31, 37, MAX_UNITS, MAX_UNITS) if g + 1 < GROUPS else (0, 0, 0, 9, 18, 27, 35, MAX_UNITS, MAX_UNITS)
            return range(ends[j], ends[j + 1])

        assert all(MAXES[n][0] < 4 for g in range(GROUPS) for n in max_slice(g, stacks_at(g) + 1))

        def projected_at(j):
            return range(2 * j - 4, 2 * j - 2) if 2 <= j < 6 else range(0)

        def score_units(j):
            lo = j * P
            if lo < HALF:
                return [(range(h, h + 1), q0, q1) for h in range(GROUP) for q0, q1 in ((lo, HALF), (HALF, SEQ))]
            per = min(GROUP, HALF // (SEQ - lo))
            return [(range(h, h + per), lo, SEQ) for h in range(0, GROUP, per)]

        assert GROUPS * sum(len(score_units(j)) for j in range(TILES)) == SCORE_UNITS

        class Units:

            def __init__(self, b, ahead):
                self.b, self.n = b, ahead - 1

            def next(self):
                self.n += 1
                return unit[self.n % BANKS]

            def wait_empty(self, eng):
                eng.wait_ge(unit_free[self.n % BANKS], self.b * (UNITS_BATCH // BANKS) + self.n // BANKS + 1)

            def wait_full(self, eng):
                eng.wait_ge(unit_full, self.b * UNITS_BATCH + self.n + 1)

            def wait_emptied(self, eng, n):
                eng.wait_ge(unit_free[n % BANKS], self.b * (UNITS_BATCH // BANKS) + n // BANKS + 2)

            def free(self):
                return unit_free[self.n % BANKS]

        assert UNITS_BATCH % BANKS == 0

        @block.tensor
        def _(pe):
            pe.wait_ge(cleared, 5)
            scores_done = []
            for g in range(GROUPS):
                for j in range(TILES):
                    scores_done.append((scores_done or [0])[-1] + len(score_units(j)))

            def program(b, u, ahead, last):
                scores_made = [0]

                def turn(srcs):
                    out = u.next()
                    u.wait_empty(pe)
                    for i, s in enumerate(srcs):
                        mm = pe.transpose(out[:, i * P:(i + 1) * P], s, k["ident"][:, :])
                    mm.then_inc(unit_full, 1)
                    return u.n

                def heads_of(stack, g, t):
                    return stack[:, t, g * GROUP:(g + 1) * GROUP, :].rearrange("p h s -> p (h s)")

                def turn_stacks(g, i):
                    return [turn([heads_of(s, g % GROUPS, t) for t in range(4 * i, 4 * i + 4)]) for s in (q_st, k_st)]

                def project(t):
                    out = u.next()
                    u.wait_empty(pe)
                    pe.matmul(out[:, 0:3 * DIM], zT[:, t * P:(t + 1) * P], k["w_qkv"][:, :], start=True, stop=True)\
                      .then_inc(unit_full, 1)

                def maxima_unit(g, n):
                    qt, heads, first, width, masked, _ = MAXES[n]
                    out = u.next()
                    u.wait_empty(pe)
                    for i, h in enumerate(heads):
                        o = out[:, i * width:(i + 1) * width]
                        mm = pe.matmul(o, qT[g % 2][:, qt * P:(qt + 1) * P], kT[g % 2][:, h, first:first + width],
                                       start=True, stop=not masked)
                        if masked:
                            mm = pe.matmul(o[:, width - P:width], k["ident16"][:, :], k["mask"][:, :],
                                           start=False, stop=True)
                    mm.then_inc(unit_full, 1)

                def turn_shifted(g):
                    pe.wait_ge(shift_ready, b * GROUPS + g + 1)
                    return [turn([heads_of(q_st, g % GROUPS, t) for t in range(4 * i, 4 * i + 4)]) for i in range(2)]

                def scores(g, j, beside):
                    lo = j * P
                    for heads, q0, q1 in score_units(j):
                        s = scores_made[0]
                        scores_made[0] += 1
                        out = score[s % 2]
                        pe.wait_ge(prob_ready[s % 2], b * (SCORE_UNITS // 2) + s // 2 + 1)
                        for i, h in enumerate(heads):
                            at = i * (q1 - q0)
                            mm = pe.matmul(out[:, at:at + q1 - q0], kT[g % 2][:, h, lo:lo + P], qmT[g % 2][:, q0:q1],
                                           start=True, stop=q0 > lo)
                            if q0 == lo:
                                mm = pe.matmul(out[:, at:at + P], k["mask"][:, :], k["ident16"][:, :], start=False, stop=True)
                        mm.then_inc(score_full, 1)
                        beside()

                def weigh(g, j, beside):
                    step = g * TILES + j
                    if j == 0:
                        pe.wait_ge(o_free, b * GROUPS + g + 1)
                        if g == 0:
                            pe.wait_ge(v_ready, b + 1)
                    done = scores_done[step]
                    for i in range(2):
                        pe.wait_ge(prob_ready[i], b * (SCORE_UNITS // 2) + (done + 1 - i) // 2 + 1)
                    lo = j * P
                    for q0, q1 in ((lo, max(lo, HALF)), (max(lo, HALF), SEQ)):
                        if q0 == q1:
                            continue
                        for h in range(GROUP):
                            mm = pe.matmul(o_acc[h * STACK:(h + 1) * STACK, q0:q1], v1[:, j, g * GROUP + h, :],
                                           prob[step % 2][:, h, q0:q1], start=(j == 0),
                                           stop=(j == (3 if q1 == HALF else TILES - 1)))
                        if q1 == HALF:
                            beside()
                    mm.then_inc(pv_done[step % 2], 1)

                def turn_out(g):
                    pe.wait_ge(o_free, b * GROUPS + g + 2)
                    for i in range(2):
                        out = u.next()
                        u.wait_empty(pe)
                        for t in range(4):
                            mm = pe.transpose(out[:, t * P:(t + 1) * P], oT[:, (4 * i + t) * P:(4 * i + t + 1) * P], k["ident"][:, :])
                        mm.then_inc(unit_full, 1)
                    return u.n

                if ahead:
                    pe.wait_ge(z_ready, 1)
                    for i in range(2):
                        turn([z[:, t, :] for t in range(4 * i, 4 * i + 4)])
                    for n in (u.n - 1, u.n):
                        u.wait_emptied(pe, n)
                    for t in range(TILES):
                        project(t)
                    pe.wait_ge(stack_ready, 1)
                    for n in turn_stacks(0, 0) + turn_stacks(0, 1):
                        u.wait_emptied(pe, n)
                    for n in range(MAX_UNITS):
                        maxima_unit(0, n)
                    for n in turn_shifted(0):
                        u.wait_emptied(pe, n)
                    return
                shifted, stacks = [], []
                for g in range(GROUPS):
                    follows = g + 1 < GROUPS or not last
                    for j in range(TILES):
                        todo = list(max_slice(g, j)) if follows else []
                        places = len(score_units(j)) + (2 if 1 <= j <= 4 else 1)
                        whole, placed = len(todo), [0]

                        def beside():
                            placed[0] += 1
                            if follows and j == stacks_at(g) and placed[0] == 3:
                                if g + 1 == GROUPS:
                                    pe.wait_ge(stack_ready, b + 2)
                                stacks.extend(turn_stacks(g + 1, 0))
                            upto = min(whole, -(-whole * placed[0] // places))
                            for n in stacks if todo else ():
                                u.wait_emptied(pe, n)
                            if todo:
                                stacks.clear()
                            while whole - len(todo) < upto:
                                maxima_unit(g + 1, todo.pop(0))

                        if j == 0:
                            for n in shifted:
                                u.wait_emptied(pe, n)
                        scores(g, j, beside)
                        if follows and j == stacks_at(g) + 1:
                            while todo:
                                maxima_unit(g + 1, todo.pop(0))
                            stacks += turn_stacks(g + 1, 1)
                        if j >= 1:
                            weigh(g, j - 1, beside)
                        while todo:
                            maxima_unit(g + 1, todo.pop(0))
                        if not last and (g, j) == (1, 1):
                            pe.wait_ge(z_ready, b + 2)
                            for i in range(2):
                                turn([z[:, t, :] for t in range(4 * i, 4 * i + 4)])
                        if not last and g == 1:
                            for t in projected_at(j):
                                project(t)
                        if follows and j == TILES - 1:
                            shifted = turn_shifted(g + 1)
                        if j == 2 and g > 0:
                            turn_out(g - 1)
                    weigh(g, TILES - 1, lambda: None)
                turned_out = turn_out(GROUPS - 1)
                for n in shifted if not last else ():
                    u.wait_emptied(pe, n)
                for n in (turned_out - 1, turned_out):
                    u.wait_emptied(pe, n)
                out_units = [turn([o_tok[:, t, :, :].rearrange("p h s -> p (h s)") for t in range(4 * i, 4 * i + 4)])
                             for i in range(2)]
                for i in range(BANKS):
                    if i % 2 == 0:
                        u.wait_emptied(pe, out_units[i // 2])
                    out = u.next()
                    u.wait_empty(pe)
                    for t in range(2):
                        mm = pe.matmul(out[:, t * P:(t + 1) * P], o_tokT[:, (2 * i + t) * P:(2 * i + t + 1) * P],
                                       k["w_o"][:, :], start=True, stop=True)
                    mm.then_inc(unit_full, 1)
                assert last or u.n + 1 == UNITS_AHEAD + UNITS_BATCH, (u.n + 1, UNITS_AHEAD + UNITS_BATCH)

            program(0, Units(0, 0), True, False)
            with pe.Fori(0, BATCH - 1) as b:
                program(b, Units(b, UNITS_AHEAD), False, False)
            program(BATCH - 1, Units(BATCH - 1, UNITS_AHEAD), False, True)

        @block.scalar
        def _(act):
            act.wait_ge(kT_cleared, 1)

            def program(b, u, ahead, last):
                nb = 0 if ahead else b + 1

                def token_dev():
                    act.wait_ge(var_ready, 2 * nb + 1)
                    act.activation(dev[:, :], spread[:, :], ACT.Sqrt).then_inc(dev_ready, 1)

                def head_dev():
                    act.wait_ge(var_ready, 2 * nb + 2)
                    act.activation(qk_dev[:, :], qk_var[:, :], ACT.Sqrt).then_inc(dev_ready, 1)

                def projected(t):
                    src = u.next()
                    u.wait_full(act)
                    act.copy(qk[:, t, :, :, :].rearrange("p a h s -> p (a h s)"), src[:, 0:2 * DIM])
                    act.copy(v_next[:, t, :, :], src[:, 2 * DIM:3 * DIM].rearrange("p (h s) -> p h s", s=HD))\
                       .then_inc(u.free(), 1)

                def values():
                    for n in range(u_values - BANKS + 1, u_values + 1) if ahead else (u_values - 1, u_values):
                        u.wait_emptied(act, n)
                    act.copy(v1[:, :, :, 0:HD], v_next[:, :, :, :]).then_inc(v_ready, 1)

                def spread_keys(g):
                    u.n += 1
                    src = u.next()
                    u.wait_full(act)
                    for h in range(GROUP):
                        rows = slice(h * STACK, (h + 1) * STACK)
                        ins = act.copy(kT[g % 2][rows, h, HALF:SEQ], src[rows, :])
                    ins.then_inc(u.free(), 1)

                def second_shifted(g):
                    u.n += 1
                    src = u.next()
                    u.wait_full(act)
                    act.copy(qmT[g % 2][:, HALF:SEQ], src[:, :]).then_inc(u.free(), 1)

                if ahead:
                    token_dev()
                    u.n += 2
                    for t in range(TILES):
                        projected(t)
                    u_values = u.n
                    head_dev()
                    values()
                    u.n += 2
                    spread_keys(0)
                    u.n += MAX_UNITS
                    second_shifted(0)
                    return
                s = 0

                def empty_out(g):
                    act.wait_ge(pv_done[1], b * (STEPS_BATCH // 2) + (g + 1) * TILES // 2 + 1)
                    act.copy(oT[:, :], o_acc[:, :]).then_inc(o_free, 1)

                for g in range(GROUPS):
                    follows = g + 1 < GROUPS or not last
                    for j in range(TILES):
                        step = g * TILES + j
                        act.wait_ge(pv_done[step % 2], b * (STEPS_BATCH // 2) + step // 2 + 1)
                        for heads, q0, q1 in score_units(j):
                            act.wait_ge(score_full, b * SCORE_UNITS + s + 1)
                            src = score[s % 2][:, 0:len(heads) * (q1 - q0)].rearrange("p (h q) -> p h q", q=q1 - q0)
                            act.activation(prob[step % 2][:, heads[0]:heads[-1] + 1, q0:q1], src,
                                           ACT.Exp).then_inc(prob_ready[s % 2], 1)
                            s += 1
                        if follows and j == stacks_at(g):
                            u.n += 2
                        if follows:
                            u.n += len(max_slice(g, j))
                        if follows and j == stacks_at(g) + 1:
                            spread_keys(g + 1)
                        if not last:
                            if (g, j) == (0, 6):
                                token_dev()
                            if (g, j) == (1, 1):
                                u.n += 2
                            if g == 1:
                                for t in projected_at(j):
                                    projected(t)
                                    u_values = u.n
                            if (g, j) == (2, 2):
                                head_dev()
                        if follows and j == TILES - 1:
                            second_shifted(g + 1)
                        if j == 2 and g > 0:
                            u.n += 2
                            act.wait_ge(unit_full, b * UNITS_BATCH + u.n + 1)
                    empty_out(g)
                if not last:
                    values()
                u.n += 2
                for i in range(2):
                    src = u.next()
                    u.wait_full(act)
                    act.copy(o_tokT[:, i * HALF:(i + 1) * HALF], src[:, :]).then_inc(u.free(), 1)
                u.n += BANKS
                assert s == SCORE_UNITS and (last or u.n + 1 == UNITS_AHEAD + UNITS_BATCH)

            program(0, Units(0, 0), True, False)
            with act.Fori(0, BATCH - 1) as b:
                program(b, Units(b, UNITS_AHEAD), False, False)
            program(BATCH - 1, Units(BATCH - 1, UNITS_AHEAD), False, True)

        @block.gpsimd
        def _(pool):
            start_free(pool, *unit_free, *prob_ready, *pv_done, o_free)
            pool.memset(k_st[:, :, :, :], 0.0).then_inc(cleared, 1)
            pool.wait_ge(cleared, 1)
            pool.memset(k_st[:, :, :, 3 * HD:3 * HD + 2], 1.0).then_inc(cleared, 1)
            pool.memset(v1[:, :, :, HD + 1:STACK], 0.0).then_inc(cleared, 1)
            pool.memset(v1[:, :, :, HD:HD + 1], 1.0).then_inc(cleared, 1)
            pool.memset(q_st[:, :, :, :], 0.0).then_inc(cleared, 1)

        @block.vector
        def _(dve):
            for i in range(2):
                ins = dve.memset(kT[i][:, :, :].bitcast(F32), 0.0)
            ins.then_inc(kT_cleared, 1)
            dve.wait_ge(cleared, 5)

            def program(b, u, link, ahead, last):
                nb = 0 if ahead else b + 1

                def x_tile(t):
                    return k["x"][:, ds((nb * TILES + t) * DIM, DIM)]

                def token_stats(tiles):
                    for t in tiles:
                        ins = dve.bn_stats(stats[:, t, :], x_tile(t))
                    return ins

                def token_moments():
                    row_moments(dve, link, stats, mean[:, :], spread[:, :], work[:, :], TILES).then_inc(var_ready, 1)

                def token_norm():
                    dve.wait_ge(dev_ready, 2 * nb + 1)
                    link(dve.reciprocal(rstd[:, :], dev[:, :]))
                    for t in range(TILES):
                        ins = dve.tensor_scalar(z[:, t, :], x_tile(t), mean[:, t:t + 1], rstd[:, t:t + 1], ALU.subtract, ALU.mult)
                    ins.then_inc(z_ready, 1)

                def token_turned():
                    for i in range(2):
                        src = u.next()
                        u.wait_full(dve)
                        dve.tensor_copy(zT[:, i * HALF:(i + 1) * HALF], src[:, :]).then_inc(u.free(), 1)

                ROWS = TILES * HEADS
                rows = [P, TILES, HEADS, HD]

                def per_head(stat, a):
                    return stat[:, a * ROWS:(a + 1) * ROWS].rearrange("p (t h) -> p t h", h=HEADS)

                def spread_over(stat, a):
                    return per_head(stat, a).unsqueeze(3).broadcast_to(rows)

                def head_means(a):
                    one = qk[:, :, a, :, :]
                    link(dve.tensor_reduce(per_head(qk_sum, a), one, AX.X, ALU.add))
                    link(dve.tensor_scalar(per_head(qk_sum, a), per_head(qk_sum, a), 1.0 / HD, None, ALU.mult))
                    link(dve.tensor_tensor(one, one, spread_over(qk_sum, a), ALU.subtract))

                def head_squares(a):
                    one = qk[:, :, a, :, :]
                    link(dve.tensor_tensor(qk_sq[:, :, :, :], one, one, ALU.mult))
                    link(dve.tensor_reduce(per_head(qk_var, a), qk_sq[:, :, :, :], AX.X, ALU.add))

                def head_spread():
                    dve.tensor_scalar(qk_var[:, :], qk_var[:, :], 1.0 / HD, EPS, ALU.mult, ALU.add).then_inc(var_ready, 1)

                def head_rstd():
                    dve.wait_ge(dev_ready, 2 * nb + 2)
                    link(dve.reciprocal(qk_rstd[:, :], qk_dev[:, :]))

                def head_norm(a):
                    one = qk[:, :, a, :, :]
                    link(dve.tensor_tensor(one, one, spread_over(qk_rstd, a), ALU.mult))
                    for i, op in enumerate((ALU.mult, ALU.add)):
                        w = k["ln_rows"][:, (2 * a + i) * HD:(2 * a + i + 1) * HD]
                        link(dve.tensor_tensor(one, one, w.unsqueeze(1).unsqueeze(1).broadcast_to(rows), op))

                def stack_keys():
                    kk = qk[:, :, 1, :, :]
                    link(dve.tensor_copy(k_st[:, :, :, 0:HD].bitcast(F32R), kk))
                    link(dve.tensor_tensor(k_st[:, :, :, 2 * HD:3 * HD].bitcast(F32R), kk, k_st[:, :, :, 0:HD], ALU.subtract))
                    link(dve.tensor_copy(k_st[:, :, :, HD:2 * HD], k_st[:, :, :, 0:HD]))

                def stack_queries():
                    u.wait_full(dve)
                    q = qk[:, :, 0, :, :]
                    link(dve.tensor_copy(q_st[:, :, :, 0:HD].bitcast(F32R), q))
                    link(dve.tensor_tensor(q_st[:, :, :, HD:2 * HD].bitcast(F32R), q, q_st[:, :, :, 0:HD], ALU.subtract))
                    link(dve.tensor_copy(q_st[:, :, :, 2 * HD:3 * HD], q_st[:, :, :, 0:HD]))
                    dve.memset(q_st[:, :, :, 3 * HD:3 * HD + 2], 0.0).then_inc(stack_ready, 1)

                def empty_queries(dst, i):
                    src = u.next()
                    u.wait_full(dve)
                    dve.tensor_copy(dst[:, i * HALF:(i + 1) * HALF], src[:, :]).then_inc(u.free(), 1)

                def spread_keys(g):
                    src = u.next()
                    u.wait_full(dve)
                    for h in range(GROUP):
                        rows = slice(h * STACK, (h + 1) * STACK)
                        ins = dve.tensor_copy(kT[g % 2][rows, h, 0:HALF], src[rows, :])
                    ins.then_inc(u.free(), 1)

                def maxima_unit(n):
                    qt, heads, _, width, _, part = MAXES[n]
                    src = u.next()
                    u.wait_full(dve)
                    dve.tensor_reduce(maxima[:, qt, heads[0]:heads[-1] + 1, part],
                                      src[:, 0:len(heads) * width].rearrange("p (h w) -> p h w", w=width),
                                      AX.X, ALU.max).then_inc(u.free(), 1)

                def shift(g):
                    u.wait_emptied(dve, u.n)
                    link(dve.tensor_tensor(maxima[:, 4:TILES, :, 0], maxima[:, 4:TILES, :, 0], maxima[:, 4:TILES, :, 1], ALU.max))
                    heads = slice(g % GROUPS * GROUP, (g % GROUPS + 1) * GROUP)
                    hi, lo = q_st[:, :, heads, 3 * HD], q_st[:, :, heads, 3 * HD + 1]
                    link(dve.tensor_scalar(hi.bitcast(F32R), maxima[:, :, :, 0], -1.0, None, ALU.mult))
                    dve.scalar_tensor_tensor(out=lo.bitcast(F32R), in0=maxima[:, :, :, 0], scalar=-1.0, in1=hi,
                                             op0=ALU.mult, op1=ALU.subtract).then_inc(shift_ready, 1)
                    empty_queries(qmT[g % 2], 0)
                    u.n += 1

                def normalise(g):
                    for i in range(2):
                        src = u.next()
                        u.wait_full(dve)
                        o = src[:, :].rearrange("p (t h s) -> p t h s", t=4, s=STACK)
                        link(dve.reciprocal(o_den[i][:, :, :], o[:, :, :, HD]))
                        ins = dve.tensor_tensor(o_tok[:, 4 * i:4 * i + 4, g * GROUP:(g + 1) * GROUP, :], o[:, :, :, 0:HD],
                                                o_den[i][:, :, :].unsqueeze(3).broadcast_to([P, 4, GROUP, HD]), ALU.mult)
                        ins.then_inc(u.free(), 1)

                if ahead:
                    link(token_stats(range(TILES)))
                    token_moments()
                    token_norm()
                    token_turned()
                    u.n += TILES
                    for n in range(u.n - BANKS + 1, u.n + 1):
                        u.wait_emptied(dve, n)
                    for a in range(2):
                        head_means(a)
                        head_squares(a)
                    head_spread()
                    head_rstd()
                    for a in range(2):
                        head_norm(a)
                    stack_keys()
                    stack_queries()
                    empty_queries(qT[0], 0)
                    spread_keys(0)
                    empty_queries(qT[0], 1)
                    u.n += 1
                    for n in range(MAX_UNITS):
                        maxima_unit(n)
                    shift(0)
                    assert link.n == LINKS_AHEAD, (link.n, LINKS_AHEAD)
                    return
                for g in range(GROUPS):
                    follows = g + 1 < GROUPS or not last
                    for j in range(TILES):
                        if not last and (g, j) == (3, 0):
                            stack_queries()
                        if follows and j == stacks_at(g):
                            empty_queries(qT[(g + 1) % 2], 0)
                            spread_keys(g + 1)
                        for n in max_slice(g, j) if follows else ():
                            maxima_unit(n)
                        if follows and j == stacks_at(g) + 1:
                            empty_queries(qT[(g + 1) % 2], 1)
                            u.n += 1
                        if not last:
                            if g == 0 and 1 <= j <= 3:
                                token_stats(range(2 * j - 2, 2 * j))
                            if (g, j) == (0, 4):
                                link(token_stats(range(6, TILES)))
                            if (g, j) == (0, 5):
                                token_moments()
                            if (g, j) == (1, 0):
                                token_norm()
                            if (g, j) == (1, 1):
                                token_turned()
                            if g == 1 and projected_at(j):
                                u.n += len(projected_at(j))
                                projected = u.n
                            if (g, j) == (1, 6):
                                for n in (projected - 1, projected):
                                    u.wait_emptied(dve, n)
                                head_means(0)
                            if (g, j) == (1, 7):
                                head_squares(0)
                            if (g, j) == (2, 0):
                                head_means(1)
                            if (g, j) == (2, 1):
                                head_squares(1)
                                head_spread()
                            if (g, j) == (2, 3):
                                head_rstd()
                                head_norm(1)
                            if (g, j) == (2, 4):
                                stack_keys()
                            if (g, j) == (2, 6):
                                head_norm(0)
                        if follows and j == TILES - 1:
                            shift(g + 1)
                        if j == 2 and g > 0:
                            normalise(g - 1)
                normalise(GROUPS - 1)
                u.n += 2
                for i in range(BANKS):
                    src = u.next()
                    u.wait_full(dve)
                    o = src[:, 0:2 * DIM].rearrange("p (t e) -> p t e", e=DIM)
                    bo = k["bo_rows"][:, :].unsqueeze(1).broadcast_to([P, 2, DIM])
                    link(dve.tensor_tensor(proj[i][:, :, :], o, bo, ALU.add))
                    x2 = k["x"][:, ds((b * TILES + 2 * i) * DIM, 2 * DIM)]
                    ins = dve.tensor_tensor(x2, x2, proj[i][:, :, :].rearrange("p t e -> p (t e)"), ALU.add)
                    ins.then_inc(u.free(), 1)
                assert last or u.n + 1 == UNITS_AHEAD + UNITS_BATCH
                assert last or link.n == LINKS, (link.n, LINKS)

            program(0, Units(0, 0), Link(dve, link_sem), True, False)
            with dve.Fori(0, BATCH - 1) as b:
                program(b, Units(b, UNITS_AHEAD), Link(dve, link_sem, LINKS_AHEAD + b * LINKS), False, False)
            program(BATCH - 1, Units(BATCH - 1, UNITS_AHEAD), Link(dve, link_sem, LINKS_AHEAD + (BATCH - 1) * LINKS), False, True)

        phase.close()
        clear_semaphores(nc, sems)


def moe_phase(nc, d, k, name, first_time):
    GROUPS_ALL = ALL // GTOK
    COLS = GTOK * DIM
    CHUNKS = 3 * EXPERTS
    RAWS = 12
    FACTOR_PARTS = CH * DIM // HALF
    FLAT = ALL * EXPERTS
    HALF_TILES = ALL // HALVES
    SENT = TOP * HALF_TILES
    BATCHED = TOP * GTOK
    with ExitStack() as ctx, ExitStack() as phase:
        def sb(n, shape, dt=F32):
            return ctx.enter_context(nc.sbuf_tensor(f"{name}_{n}", shape, dt))

        sems = []

        def sem(n):
            sems.append(ctx.enter_context(nc.semaphore(f"{name}_{n}")))
            return sems[-1]

        def pair(n):
            return [ctx.enter_context(nc.psum_tensor(f"{name}_{n}{i}", [P, HALF], F32)) for i in range(2)]

        mean, work = sb("mean", [P, ALL]), sb("work", [P, ALL])
        spread, dev, rstd = (sb(n, [P, 2 * ALL]) for n in ("spread", "dev", "rstd"))
        h = sb("h", [P, ALL * DIM])
        norm_all = sb("norm_all", [P, ALL * DIM])
        logits, pick, other = (sb(n, [P, ALL, EXPERTS]) for n in ("logits", "pick", "other"))
        chosen = sb("chosen", [P, ALL, EXPERTS])
        count0, count1, place = (sb(n, [P, HALVES, HALF_TILES, EXPERTS]) for n in ("count0", "count1", "place"))
        rank = sb("rank", [P, EXPERTS])
        blocks_int = sb("blocks_int", [P, HALVES, EXPERTS], U32)
        blocks, first0, first1 = (sb(n, [P, HALVES, EXPERTS]) for n in ("blocks", "first0", "first1"))
        at_block = sb("at_block", [1, NB, EXPERTS])
        expert_sum, expert_of = sb("expert_sum", [1, NB]), sb("expert_of", [1, NB], I32)
        row_of32, row_of = sb("row_of32", [P, TOP, ALL]), sb("row_of", [P, TOP, ALL], U32)
        below, ones, zeros = (sb(n, [P, P]) for n in ("below", "ones", "zeros"))
        best, second, first_at, ratio, share = (sb(n, [P, ALL]) for n in ("best", "second", "first_at", "ratio", "share"))
        raw = [k[n][:, i * HALF:(i + 1) * HALF] for n in ("uv", "uvT") for i in range(FACTOR_PARTS)]
        raw += [sb(f"raw{i}", [P, HALF])[:, :] for i in range(RAWS - len(raw))]
        w_hi, w_lo = ([sb(f"w_{part}{i}", [P, UNITS * P], F32R) for i in range(2)] for part in ("hi", "lo"))
        w_down = sb("w_down", [P, UNITS * DIM])
        t_rows = [sb(f"t_rows{i}", [P, DIM]) for i in range(UNROLL)]
        t32 = [sb(f"t32{i}", [P, P]) for i in range(2)]
        t_hi, t_lo = ([sb(f"{n}{i}", [P, P], F32R) for i in range(2)] for n in ("t_hi", "t_lo"))
        silu = [sb(f"silu{i}", [P, HALF]) for i in range(2)]
        inner = [sb(f"inner{i}", [P, HALF]) for i in range(2)]
        innerT = [sb(f"innerT{i}", [P, HALF]) for i in range(2)]
        y_rows = [sb(f"y_rows{i}", [P, DIM]) for i in range(2)]
        landing = [h, norm_all]
        norm, normT = inner, silu
        gate, up, out = pair("gate"), pair("up"), pair("out")
        inner_turn = out
        t_turn, y_ps = (ctx.enter_context(nc.psum_tensor(f"{name}_{n}", [P, HALF], F32)) for n in ("t_turn", "y_ps"))

        raw_in = [sem(f"raw_in{i}") for i in range(RAWS // 3)]
        weight_full, weight_hi, weight_free, consts_done, rows_clear = (
            sem(n) for n in ("weight_full", "weight_hi", "weight_free", "consts_done", "rows_clear"))
        link_sem, stats_done, var_ready, dev_ready, y_done, norm_ready, turn_full, normT_ready = (
            sem(n) for n in ("link", "stats_done", "var_ready", "dev_ready", "y_done", "norm_ready", "turn_full", "normT_ready"))
        product_full, product_free, gap_ready, ratio_ready = (
            sem(n) for n in ("product_full", "product_free", "gap_ready", "ratio_ready"))
        norm_kept = sem("norm_kept")
        chosen_ready, counts_full, places_ready, table_ready, x_summed = (
            sem(n) for n in ("chosen_ready", "counts_full", "places_ready", "table_ready", "x_summed"))
        sent = [sem(f"sent{i}") for i in range(HALVES)]
        loaded = [sem(f"loaded{i}") for i in range(UNROLL)]
        t_turned, t32_ready, t_hi_ready, t_lo_ready, gate_full, up_full, inner_turned, y_full, y_ready = (
            sem(n) for n in ("t_turned", "t32_ready", "t_hi_ready", "t_lo_ready", "gate_full", "up_full", "inner_turned",
                             "y_full", "y_ready"))
        silu_ready, inner_ready, innerT_ready, y_stored = (
            [sem(f"{n}{i}") for i in range(2)] for n in ("silu_ready", "inner_ready", "innerT_ready", "y_stored"))
        landed = [sem(f"landed{i}") for i in range(HALVES * SENT // BATCHED)]
        first_added, token_done = sem("first_added"), sem("token_done")
        factors_in, factors_scaled, factors_turned = (sem(n) for n in ("factors_in", "factors_scaled", "factors_turned"))
        factor_bank = gate + up
        factors = k["uv"][:, :].rearrange("p (c z) -> p c z", z=DIM)
        block = phase.enter_context(nc.Block())

        def chunk(c):
            e, mat = divmod(c, 3)
            return e, mat, slice(e * INTER, (e + 1) * INTER)

        def half(b):
            it, i = b
            return it * (UNROLL // 2) + i // 2

        def number(b):
            it, i = b
            return it * UNROLL + i

        def earlier(b, n):
            it, i = b
            return (it, i - n)

        @block.sync
        def _(sp):
            for c in range(CHUNKS):
                e, mat, _ = chunk(c)
                if c >= RAWS:
                    sp.wait_ge(weight_full, c - RAWS + 1)
                if mat == 2:
                    ins = sp.dma_start(raw[c % RAWS][:, :], d["down_proj"][e])
                else:
                    ins = sp.dma_start(raw[c % RAWS][:, :].rearrange("p (n h) -> p n h", h=DIM),
                                       d[("gate_proj", "up_proj")[mat]][e].rearrange("(n p) h -> p n h", p=P))
                ins.then_inc(raw_in[e % (RAWS // 3)], 16)

            def load(n, h, slot):
                sp.dma_start(t_rows[slot][:, :], k["sent_rows"][h][ds((n - h * HALF_NB) * P, P), :]).then_inc(loaded[slot], 16)

            def store(b, h):
                p = b[1] % 2
                sp.wait_ge(y_ready, number(b) + 1)
                sp.dma_start(k["result_rows"][h][ds((number(b) - h * HALF_NB) * P, P), :], y_rows[p][:, :]).then_inc(y_stored[p], 16)

            def body(it, halves):
                for i, (stored, fetched) in enumerate(halves):
                    if fetched is not None:
                        sp.wait_ge(t_turned, number((it, i + AHEAD - UNROLL)) + 1)
                        load(number((it, i + AHEAD)), fetched, (i + AHEAD) % UNROLL)
                    if stored is not None:
                        store(earlier((it, i), 2), stored)

            sp.wait_ge(sent[0], 16 * SENT)
            for n in range(UNROLL):
                load(n, 0, n)
            steps = NB // UNROLL
            crossing = steps // HALVES - 1
            body(0, [(None if i < 2 else 0, None if i + AHEAD < UNROLL else 0) for i in range(UNROLL)])
            with sp.Fori(1, crossing) as it:
                body(it, [(0, 0)] * UNROLL)
            sp.wait_ge(sent[1], 16 * SENT)
            if first_time:
                sp.wait_ge(weight_full, CHUNKS)
                for rows, src in ((slice(0, RANK), "u"), (slice(RANK, P), "v")):
                    sp.dma_start(factors[rows], d[src].rearrange("(c r) z -> r c z", r=RANK)).then_inc(factors_in, 16)
            body(crossing, [(0, 0 if i + AHEAD < UNROLL else 1) for i in range(UNROLL)])
            body(crossing + 1, [(0 if i < 2 else 1, 1) for i in range(UNROLL)])
            with sp.Fori(crossing + 2, steps - 1) as it:
                body(it, [(1, 1)] * UNROLL)
            sp.wait_ge(t_turned, NB - UNROLL + 1)
            load(HALF_NB, 1, 0)
            body(steps - 1, [(1, 1 if i + AHEAD < UNROLL else None) for i in range(UNROLL)])
            for n in (2, 1):
                store((steps, -n), 1)

        @block.tensor
        def _(pe):
            def turn_weights():
                for c in range(CHUNKS):
                    pe.wait_ge(raw_in[c // 3 % (RAWS // 3)], 48 * (c // RAWS + 1))
                    if c >= 2:
                        pe.wait_ge(weight_free, c - 1)
                    for j in range(BLOCKS):
                        mm = pe.transpose(out[c % 2][:, j * P:(j + 1) * P], raw[c % RAWS][:, j * P:(j + 1) * P], k["ident"][:, :])
                    mm.then_inc(weight_full, 1)

            for turn_no, w in enumerate((k["attn_wT"], k["gate_wT"])):
                cols = w.shape[1]

                def turn_group(g):
                    q = turn_no * GROUPS_ALL + g
                    pe.wait_ge(norm_ready, q + 1)
                    if q >= 2:
                        pe.wait_ge(normT_ready, q - 1)
                    for t in range(GTOK):
                        mm = pe.transpose(gate[g % 2][:, t * P:(t + 1) * P], norm[g % 2][:, t * DIM:(t + 1) * DIM], k["ident"][:, :])
                    mm.then_inc(turn_full, 1)

                turn_group(0)
                for g in range(GROUPS_ALL):
                    if g + 1 < GROUPS_ALL:
                        turn_group(g + 1)
                    q = turn_no * GROUPS_ALL + g
                    pe.wait_ge(normT_ready, q + 1)
                    if q >= 2:
                        pe.wait_ge(product_free, q - 1)
                    for t in range(GTOK):
                        mm = pe.matmul(up[g % 2][:, t * cols:(t + 1) * cols], normT[g % 2][:, t * P:(t + 1) * P], w[:, :],
                                       start=True, stop=True)
                    mm.then_inc(product_full, 1)
            pe.wait_ge(chosen_ready, 1)
            pe.wait_ge(consts_done, CONSTS)
            flat = chosen[:, :, :].rearrange("p t e -> p (t e)")
            pe.matmul(up[0][:, 0:FLAT], below[:, :], flat, start=True, stop=True)
            pe.matmul(up[1][:, 0:FLAT], ones[:, :], flat, start=True, stop=True)
            pe.matmul(up[1][:, FLAT:FLAT + P], ones[:, :], below[:, :], start=True, stop=True).then_inc(counts_full, 1)
            turn_weights()
            pe.wait_ge(weight_free, CHUNKS)
            pe.wait_ge(table_ready, 1)

            def turn_rows(b):
                pe.wait_ge(loaded[b[1] % UNROLL], 16 * (b[0] + b[1] // UNROLL + 1))
                pe.transpose(t_turn[:, 0:P], t_rows[b[1] % UNROLL][:, :], k["ident"][:, :]).then_inc(t_turned, 1)

            def products(to, w, e, i):
                cols = ds(e * INTER, INTER)
                pe.matmul(to[:, :], t_lo[i][:, :], w_hi[w][:, cols], start=True, stop=False)
                pe.matmul(to[:, :], t_hi[i][:, :], w_hi[w][:, cols], start=False, stop=False)
                return pe.matmul(to[:, :], t_hi[i][:, :], w_lo[w][:, cols], start=False, stop=True)

            def turn_inner(b, fresh):
                p = b[1] % 2
                pe.wait_ge(inner_ready[p], half(b) + 1)
                if not fresh:
                    pe.wait_ge(innerT_ready[p], half(b))
                for ib in range(BLOCKS):
                    mm = pe.transpose(inner_turn[p][:, ib * P:(ib + 1) * P], inner[p][:, ib * P:(ib + 1) * P], k["ident"][:, :])
                mm.then_inc(inner_turned, 1)

            def down(b, e, fresh):
                p = b[1] % 2
                pe.wait_ge(innerT_ready[p], half(b) + 1)
                if not fresh:
                    pe.wait_ge(y_ready, number(b))
                for ib in range(BLOCKS):
                    mm = pe.matmul(y_ps[:, 0:DIM], innerT[p][:, ib * P:(ib + 1) * P], w_down[:, ds(e * INTER + ib * DIM, DIM)],
                                   start=(ib == 0), stop=(ib == BLOCKS - 1))
                mm.then_inc(y_full, 1)

            def expert(b):
                return pe.value_load(expert_of[0:1, ds(number(b), 1)], min_val=0, max_val=EXPERTS - 1)

            def body(it, first):
                experts = {i: expert((it, i)) for i in ((0,) if first else (-2, -1, 0))}
                for i in range(UNROLL):
                    b, p, e = (it, i), i % 2, experts[i]
                    pe.wait_ge(t32_ready, number(b) + 1)
                    turn_rows((it, i + 1))
                    pe.wait_ge(t_lo_ready, number(b) + 1)
                    if not (first and i < 2):
                        pe.wait_ge(silu_ready[p], half(b))
                    products(gate[p], 0, e, p).then_inc(gate_full, 1)
                    if not (first and i < 2):
                        pe.wait_ge(inner_ready[p], half(b))
                    products(up[p], 1, e, p).then_inc(up_full, 1)
                    if not (first and i < 1):
                        turn_inner(earlier(b, 1), first and i < 3)
                    if not (first and i < 2):
                        down(earlier(b, 2), experts[i - 2], first and i < 3)
                    if i + 1 < UNROLL:
                        experts[i + 1] = expert((it, i + 1))

            turn_rows((0, 0))
            body(0, True)
            with pe.Fori(1, NB // UNROLL) as it:
                body(it, False)
            end = (NB // UNROLL, 0)
            turn_inner(earlier(end, 1), False)
            for n in (2, 1):
                down(earlier(end, n), expert(earlier(end, n)), False)
            if first_time:
                pe.wait_ge(factors_scaled, 1)
                for i in range(FACTOR_PARTS):
                    for j in range(HALF // DIM):
                        at = i * HALF + j * DIM
                        mm = pe.transpose(factor_bank[i][:, j * P:(j + 1) * P], k["uv"][:, at:at + DIM], k["ident"][:, :])
                    mm.then_inc(factors_turned, 1)

        @block.scalar
        def _(act):
            act.wait_ge(var_ready, 1)
            act.activation(dev[:, :], spread[:, :], ACT.Sqrt).then_inc(dev_ready, 1)
            for turn_no in range(2):
                if turn_no:
                    act.wait_ge(var_ready, 2)
                    act.activation(dev[:, 0:ALL], spread[:, 0:ALL], ACT.Sqrt).then_inc(dev_ready, 1)
                for g in range(GROUPS_ALL):
                    q = turn_no * GROUPS_ALL + g
                    if turn_no:
                        act.wait_ge(norm_ready, q + 1)
                        act.copy(norm_all[:, g * COLS:(g + 1) * COLS], norm[g % 2][:, :]).then_inc(norm_kept, 1)
                    act.wait_ge(turn_full, q + 1)
                    act.activation(normT[g % 2][:, :], gate[g % 2][:, :], ACT.Identity, bias=k["ln_cols"][:, 2 * turn_no + 1:2 * turn_no + 2],
                                   scale=k["ln_cols"][:, 2 * turn_no:2 * turn_no + 1]).then_inc(normT_ready, 1)
            act.wait_ge(gap_ready, 1)
            act.activation(ratio[:, :], second[:, :], ACT.Exp).then_inc(ratio_ready, 1)
            for c in range(CHUNKS):
                _, mat, cols = chunk(c)
                act.wait_ge(weight_full, c + 1)
                if mat < 2:
                    act.copy(w_hi[mat][:, cols], out[c % 2][:, :]).then_inc(weight_hi, 1)

            def high_rows(b, fresh):
                act.wait_ge(t32_ready, number(b) + 1)
                if not fresh:
                    act.wait_ge(up_full, number(b) - 1)
                act.copy(t_hi[b[1] % 2][:, :], t32[b[1] % 2][:, :]).then_inc(t_hi_ready, 1)

            def copy_turned(b, fresh):
                p = b[1] % 2
                act.wait_ge(inner_turned, number(b) + 1)
                if not fresh:
                    act.wait_ge(y_full, number(b) - 1)
                act.copy(innerT[p][:, :], inner_turn[p][:, :]).then_inc(innerT_ready[p], 1)

            def body(it, first):
                for i in range(UNROLL):
                    b, p = (it, i), i % 2
                    high_rows((it, i + 1), first and i < 1)
                    act.wait_ge(gate_full, number(b) + 1)
                    if not (first and i < 2):
                        act.wait_ge(inner_ready[p], half(b))
                    act.activation(silu[p][:, :], gate[p][:, :], ACT.Silu).then_inc(silu_ready[p], 1)
                    if not (first and i < 1):
                        copy_turned(earlier(b, 1), first and i < 3)

            high_rows((0, 0), True)
            body(0, True)
            with act.Fori(1, NB // UNROLL) as it:
                body(it, False)
            copy_turned((NB // UNROLL, -1), False)
            if first_time:
                for i in range(FACTOR_PARTS):
                    act.wait_ge(factors_turned, i + 1)
                    act.copy(k["uvT"][:, i * HALF:(i + 1) * HALF], factor_bank[i][:, :])

        @block.gpsimd
        def _(pool):
            pool.memset(zeros[:, :], 0.0).then_inc(consts_done, 1)
            pool.memset(ones[:, :], 1.0).then_inc(consts_done, 1)
            pool.memset(below[:, :], 1.0).then_inc(consts_done, 1)
            pool.wait_ge(consts_done, 3)
            pool.affine_select(out=below[:, :], in_=below[:, :], compare_op=ALU.is_ge, fill=0.0,
                               base=-1, pattern=[[1, P]], channel_multiplier=-1).then_inc(consts_done, 1)
            if first_time:
                for rows in k["sent_rows"]:
                    pool.dma_start(rows.rearrange("(n p) e -> p n e", p=P),
                                   zeros[:, :].unsqueeze(1).broadcast_to([P, HALF_NB, DIM])).then_inc(rows_clear, 16)
                pool.wait_ge(rows_clear, 16 * HALVES)
            pool.wait_ge(norm_kept, GROUPS_ALL)
            pool.wait_ge(places_ready, 1)
            for half_no in range(HALVES):
                for j in range(SENT):
                    t, n = half_no * HALF_TILES + j // TOP, j % TOP
                    pool.indirect_dma_start(k["sent_rows"][half_no][:, :], bass.IndirectOffsetOnAxis(ap=row_of[:, n, t:t + 1], axis=0),
                                            norm_all[:, t * DIM:(t + 1) * DIM], None).then_inc(sent[half_no], 16)
            pool.wait_ge(product_free, GROUPS_ALL)
            pool.tensor_tensor(k["x"][:, :], k["x"][:, :], h[:, :], ALU.add).then_inc(x_summed, 1)
            for half_no in range(HALVES):
                pool.wait_ge(x_summed, 1)
                for s in y_stored:
                    pool.wait_ge(s, 16 * (half_no + 1) * (HALF_NB // 2))
                for j in range(half_no * SENT, (half_no + 1) * SENT):
                    t, n = divmod(j, TOP)
                    pool.indirect_dma_start(landing[half_no][:, j % SENT * DIM:(j % SENT + 1) * DIM], None, k["result_rows"][half_no][:, :],
                                            bass.IndirectOffsetOnAxis(ap=row_of[:, n, t:t + 1], axis=0)).then_inc(landed[j // BATCHED], 16)

        @block.vector
        def _(dve):
            link = Link(dve, link_sem)
            for e in range(EXPERTS):
                ins = dve.memset(rank[:, e:e + 1], float(EXPERTS - e))
            link(ins)

            flat_stats = k["stats"][:, :, :].rearrange("p t s -> p (t s)")

            def group_stats(src, g):
                for t in range(GTOK):
                    at = g * GTOK + t
                    ins = dve.bn_stats(flat_stats[:, ds(at * 6, 6)], src[:, ds(at * DIM, DIM)])
                return ins

            def normalise(dst, src, g, t, twice):
                at = g * GTOK + t
                return dve.tensor_scalar(dst, src[:, ds(at * DIM, DIM)], mean[:, ds(at, 1)], rstd[:, ds(at + twice * ALL, 1)],
                                         ALU.subtract, ALU.mult)

            def normalised(g, turn_no, src):
                q = turn_no * GROUPS_ALL + g
                if q >= 2:
                    dve.wait_ge(turn_full, q - 1)
                if turn_no and g >= 2:
                    dve.wait_ge(norm_kept, g - 1)
                for t in range(GTOK):
                    ins = normalise(norm[g % 2][:, t * DIM:(t + 1) * DIM], src, g, t, 1 - turn_no)
                ins.then_inc(norm_ready, 1)

            before = GROUPS_ALL if first_time else 0
            if first_time:
                for g in range(GROUPS_ALL):
                    group_stats(k["x"], g).then_inc(stats_done, 1)
                dve.wait_ge(stats_done, GROUPS_ALL)
            row_moments(dve, link, k["stats"], mean[:, :], spread[:, 0:ALL], work[:, :], ALL, spread[:, ALL:2 * ALL]).then_inc(var_ready, 1)
            dve.wait_ge(dev_ready, 1)
            link(dve.reciprocal(rstd[:, :], dev[:, :]))
            for g in range(2):
                normalised(g, 0, k["x"])
            for g in range(GROUPS_ALL):
                for t in range(GTOK):
                    at = g * GTOK + t
                    ins = normalise(h[:, at * DIM:(at + 1) * DIM], k["x"], g, t, 0)
                ins.then_inc(y_done, 1)
                if g + 2 < GROUPS_ALL:
                    normalised(g + 2, 0, k["x"])
                dve.wait_ge(product_full, g + 1)
                dve.wait_ge(y_done, g + 1)
                mine = h[:, g * COLS:(g + 1) * COLS]
                dve.tensor_tensor(mine, mine, up[g % 2][:, :], ALU.add).then_inc(product_free, 1)
                if g:
                    dve.wait_ge(product_free, g)
                    group_stats(h, g - 1).then_inc(stats_done, 1)
            dve.wait_ge(product_free, GROUPS_ALL)
            group_stats(h, GROUPS_ALL - 1).then_inc(stats_done, 1)
            dve.wait_ge(stats_done, before + GROUPS_ALL)
            row_moments(dve, link, k["stats"], mean[:, :], spread[:, 0:ALL], work[:, :], ALL).then_inc(var_ready, 1)
            dve.wait_ge(dev_ready, 2)
            link(dve.reciprocal(rstd[:, 0:ALL], dev[:, 0:ALL]))
            flat_logits = logits[:, :, :].rearrange("p t e -> p (t e)")
            for g in range(2):
                normalised(g, 1, h)
            for g in range(GROUPS_ALL):
                if g + 2 < GROUPS_ALL:
                    normalised(g + 2, 1, h)
                dve.wait_ge(product_full, GROUPS_ALL + g + 1)
                dve.tensor_copy(flat_logits[:, g * GTOK * EXPERTS:(g + 1) * GTOK * EXPERTS],
                                up[g % 2][:, 0:GTOK * EXPERTS]).then_inc(product_free, 1)
            dve.wait_ge(product_free, 2 * GROUPS_ALL)

            def over_experts(a):
                return a[:, :].unsqueeze(2).broadcast_to([P, ALL, EXPERTS])

            def pick_first(dst, values, top):
                link(dve.tensor_reduce(top[:, :], values[:, :, :], AX.X, ALU.max))
                link(dve.tensor_tensor(dst[:, :, :], values[:, :, :], over_experts(top), ALU.is_equal))
                ranks = rank[:, :].unsqueeze(1).broadcast_to([P, ALL, EXPERTS])
                link(dve.tensor_tensor(dst[:, :, :], dst[:, :, :], ranks, ALU.mult))
                link(dve.tensor_reduce(first_at[:, :], dst[:, :, :], AX.X, ALU.max))
                link(dve.tensor_tensor(dst[:, :, :], dst[:, :, :], over_experts(first_at), ALU.is_equal))

            pick_first(pick, logits, best)
            link(dve.scalar_tensor_tensor(out=logits[:, :, :], in0=pick[:, :, :], scalar=MASKED, in1=logits[:, :, :],
                                          op0=ALU.mult, op1=ALU.add))
            pick_first(other, logits, second)
            dve.tensor_tensor(chosen[:, :, :], pick[:, :, :], other[:, :, :], ALU.add).then_inc(chosen_ready, 1)
            dve.tensor_tensor(second[:, :], second[:, :], best[:, :], ALU.subtract).then_inc(gap_ready, 1)
            dve.wait_ge(ratio_ready, 1)
            link(dve.tensor_scalar(share[:, :], ratio[:, :], 1.0, None, ALU.add))
            link(dve.reciprocal(share[:, :], share[:, :]))
            link(dve.tensor_tensor(ratio[:, :], ratio[:, :], share[:, :], ALU.mult))

            def by_half(flat):
                return flat.rearrange("p (a t e) -> p a t e", a=HALVES, e=EXPERTS)

            dve.wait_ge(counts_full, 1)
            tile_counts = by_half(up[1][:, 0:FLAT])
            src, dst = count0, count1
            link(dve.tensor_copy(src[:, :, :, :], tile_counts))
            reach = 1
            while reach < HALF_TILES:
                dve.tensor_copy(dst[:, :, 0:reach, :], src[:, :, 0:reach, :])
                link(dve.tensor_tensor(dst[:, :, reach:, :], src[:, :, reach:, :], src[:, :, 0:HALF_TILES - reach, :], ALU.add))
                src, dst, reach = dst, src, 2 * reach
            counts = src
            link(dve.tensor_scalar(blocks_int[:, :, :], counts[:, :, HALF_TILES - 1, :], float(P - 1), None, ALU.add))
            link(dve.tensor_scalar(blocks_int[:, :, :], blocks_int[:, :, :], P.bit_length() - 1, None, ALU.logical_shift_right))
            link(dve.tensor_copy(blocks[:, :, :], blocks_int[:, :, :]))
            link(dve.tensor_copy(first0[:, :, :], blocks[:, :, :]))
            f_src, f_dst, reach = first0, first1, 1
            while reach < EXPERTS:
                dve.tensor_copy(f_dst[:, :, 0:reach], f_src[:, :, 0:reach])
                link(dve.tensor_tensor(f_dst[:, :, reach:], f_src[:, :, reach:], f_src[:, :, 0:EXPERTS - reach], ALU.add))
                f_src, f_dst, reach = f_dst, f_src, 2 * reach
            firsts = f_dst
            link(dve.tensor_tensor(firsts[:, :, :], f_src[:, :, :], blocks[:, :, :], ALU.subtract))
            link(dve.tensor_tensor(place[:, :, :, :], counts[:, :, :, :], tile_counts, ALU.subtract))
            link(dve.tensor_tensor(place[:, :, :, :], place[:, :, :, :], by_half(up[0][:, 0:FLAT]), ALU.add))
            for a in range(HALVES):
                ins = dve.scalar_tensor_tensor(out=place[:, a, :, :], in0=firsts[:, a, :].unsqueeze(1).broadcast_to([P, HALF_TILES, EXPERTS]),
                                               scalar=float(P), in1=place[:, a, :, :], op0=ALU.mult, op1=ALU.add)
            link(ins)
            for n, mine in enumerate((pick, other)):
                link(dve.tensor_tensor(dst[:, :, :, :], by_half(mine[:, :, :].rearrange("p t e -> p (t e)")), place[:, :, :, :], ALU.mult))
                link(dve.tensor_reduce(row_of32[:, n, :], dst[:, :, :, :].rearrange("p a t e -> p (a t) e"), AX.X, ALU.add))
            dve.tensor_copy(row_of[:, :, :], row_of32[:, :, :]).then_inc(places_ready, 1)
            numbers = up[1][0:1, FLAT:FLAT + HALF_NB].unsqueeze(2).broadcast_to([1, HALF_NB, EXPERTS])
            for a in range(HALVES):
                ins = dve.tensor_tensor(at_block[:, a * HALF_NB:(a + 1) * HALF_NB, :], numbers,
                                        firsts[0:1, a, :].unsqueeze(1).broadcast_to([1, HALF_NB, EXPERTS]), ALU.is_ge)
            link(ins)
            link(dve.tensor_reduce(expert_sum[:, :], at_block[:, :, :], AX.X, ALU.add))
            dve.tensor_scalar(expert_of[:, :], expert_sum[:, :], -1.0, None, ALU.add).then_inc(table_ready, 1)
            for c in range(CHUNKS):
                e, mat, cols = chunk(c)
                if mat == 2:
                    dve.wait_ge(weight_full, c + 1)
                    ins = dve.tensor_copy(w_down[:, cols], out[c % 2][:, :])
                else:
                    dve.wait_ge(weight_hi, 2 * e + mat + 1)
                    ins = dve.tensor_tensor(w_lo[mat][:, cols], out[c % 2][:, :], w_hi[mat][:, cols].bitcast(F32), ALU.subtract)
                ins.then_inc(weight_free, 1)

            def rows_in(b, fresh):
                p = b[1] % 2
                dve.wait_ge(t_turned, number(b) + 1)
                if not fresh:
                    dve.wait_ge(t_lo_ready, number(b) - 1)
                dve.tensor_scalar(t32[p][:, :], t_turn[:, 0:P], k["ln_cols"][:, 2:3], k["ln_cols"][:, 3:4],
                                  ALU.mult, ALU.add).then_inc(t32_ready, 1)
                dve.wait_ge(t_hi_ready, number(b) + 1)
                dve.tensor_tensor(t_lo[p][:, :], t32[p][:, :], t_hi[p][:, :].bitcast(F32), ALU.subtract).then_inc(t_lo_ready, 1)

            def result(b, fresh):
                p = b[1] % 2
                dve.wait_ge(y_full, number(b) + 1)
                if not fresh:
                    dve.wait_ge(y_stored[p], half(b) * 16)
                dve.tensor_copy(y_rows[p][:, :], y_ps[:, 0:DIM]).then_inc(y_ready, 1)

            def body(it, first):
                for i in range(UNROLL):
                    b, p = (it, i), i % 2
                    rows_in((it, i + 1), first and i < 1)
                    dve.wait_ge(silu_ready[p], half(b) + 1)
                    dve.wait_ge(up_full, number(b) + 1)
                    if not (first and i < 2):
                        dve.wait_ge(inner_turned, number(b) - 1)
                    dve.tensor_tensor(inner[p][:, :], silu[p][:, :], up[p][:, :], ALU.mult).then_inc(inner_ready[p], 1)
                    if not (first and i < 2):
                        result(earlier(b, 2), first and i < 4)

            rows_in((0, 0), True)
            body(0, True)
            with dve.Fori(1, NB // UNROLL) as it:
                body(it, False)
            for n in (2, 1):
                result((NB // UNROLL, -n), False)
            if first_time:
                dve.wait_ge(factors_in, 32)
                dve.tensor_scalar(k["uv"][:, :], k["uv"][:, :], MSG_SCALE, None, ALU.mult).then_inc(factors_scaled, 1)
            dve.wait_ge(x_summed, 1)
            for j in range(HALVES * SENT):
                t, n = divmod(j, TOP)
                if j % BATCHED == 0:
                    dve.wait_ge(landed[j // BATCHED], 16 * BATCHED)
                if n:
                    dve.wait_ge(first_added, t + 1)
                xs = k["x"][:, t * DIM:(t + 1) * DIM]
                ins = dve.scalar_tensor_tensor(out=xs, in0=landing[j // SENT][:, j % SENT * DIM:(j % SENT + 1) * DIM], scalar=(share, ratio)[n][:, t:t + 1], in1=xs,
                                               op0=ALU.mult, op1=ALU.add)
                ins.then_inc((first_added, token_done)[n], 1)
                if first_time and j % BATCHED == BATCHED - 1:
                    dve.wait_ge(token_done, t + 1)
                    group_stats(k["x"], t // GTOK)

        phase.close()
        clear_semaphores(nc, sems)


def message_phase(nc, k):
    PREP = 6
    UNITS_AHEAD = 2 * BATCH + PREP
    UNITS_BATCH = PREP * CH + 2 + 2
    STEPS = CH * TILES
    with ExitStack() as ctx, ExitStack() as phase:
        def sb(n, shape, dt=F32):
            return ctx.enter_context(nc.sbuf_tensor(f"m_{n}", shape, dt))

        sems = []

        def sem(n):
            sems.append(ctx.enter_context(nc.semaphore(f"m_{n}")))
            return sems[-1]

        mean, spread, work, dev, rstd = (sb(n, [P, ALL]) for n in ("mean", "spread", "work", "dev", "rstd"))
        zT_all = sb("zT_all", [P, BATCH * SEQ])
        zT, zT_hi, zT_lo = sb("zT", [P, SEQ]), sb("zT_hi", [P, SEQ], F32R), sb("zT_lo", [P, SEQ], F32R)
        twice_hi, twice_lo = ([sb(f"{n}{i}", [P, 2, 2, RANK], F32R) for i in range(2)] for n in ("twice_hi", "twice_lo"))
        u_st = [sb(f"u_st{i}", [P, SEQ], F32R) for i in range(2)]
        v_hi = [sb(f"v_hi{i}", [P, SEQ], F32R) for i in range(2)]
        v_lo = [sb(f"v_lo{i}", [P, SEQ], F32R) for i in range(2)]
        uv_tok = [sb(f"uv_tok{i}", [P, TILES, 2, RANK]) for i in range(2)]
        f_sig = [sb(f"f_sig{i}", [P, SEQ]) for i in range(2)]
        t_sig = [sb(f"t_sig{i}", [P, SEQ]) for i in range(2)]
        vuT = sb("vuT", [P, CH * SEQ])
        z = vuT[:, 0:ALL * DIM].rearrange("p (t e) -> p t e", e=DIM)
        msgT = sb("msgT", [P, SEQ])
        f_ps, t_ps, vu_ps = (ctx.enter_context(nc.psum_tensor(f"m_{n}", [P, SEQ], F32)) for n in ("f_ps", "t_ps", "vu_ps"))
        unit = [ctx.enter_context(nc.psum_tensor(f"m_unit{i}", [P, HALF], F32)) for i in range(2)]

        tokens_high, tokens_taken = sem("tokens_high"), sem("tokens_taken")
        link_sem, var_ready, dev_ready, z_ready, twice_high, twice_ready, unit_full, hi_ready = (
            sem(n) for n in ("link", "var_ready", "dev_ready", "z_ready", "twice_high", "twice_ready", "unit_full", "hi_ready"))
        f_full, t_full, f_ready, t_ready, vu_free = (sem(n) for n in ("f_full", "t_full", "f_ready", "t_ready", "vu_free"))
        unit_free = [sem(f"unit_free{i}") for i in range(2)]
        used = [sem(f"used{i}") for i in range(2)]
        block = phase.enter_context(nc.Block())

        class Units:

            def __init__(self, base, halves, start):
                self.base, self.halves, self.n = base, halves, start - 1

            def next(self):
                self.n += 1
                return unit[self.n % 2]

            def wait_empty(self, eng):
                eng.wait_ge(unit_free[self.n % 2], self.halves + self.n // 2 + 1)

            def wait_full(self, eng):
                eng.wait_ge(unit_full, self.base + self.n + 1)

            def wait_emptied(self, eng, n):
                eng.wait_ge(unit_free[n % 2], self.halves + n // 2 + 2)

            def free(self):
                return unit_free[self.n % 2]

        def units_at(b, n):
            return Units(b * UNITS_BATCH, b * (UNITS_BATCH // 2), UNITS_AHEAD + n)

        def channels(eng, b, last_batch, body):
            with eng.Fori(0, CH // 2 - 1) as cc:
                for p in range(2):
                    body(b, 2 * cc + p, p, False, False)
            for p in range(2):
                body(b, CH - 2 + p, p, True, last_batch)

        def batches(eng, program):
            with eng.Fori(0, BATCH - 1) as b:
                program(b, False)
            program(BATCH - 1, True)

        def channel(c):
            return c % CH if isinstance(c, int) else c

        def prepared_units(last_batch):
            return PREP * (CH - 1 if last_batch else CH)

        @block.tensor
        def _(pe):
            def prepare(u, i, c, p, b):
                out = u.next()
                u.wait_empty(pe)
                if i == 0:
                    pe.wait_ge(twice_ready, b * CH + c + 1)
                    if isinstance(c, int) and c == CH:
                        pe.wait_ge(tokens_taken, b + 1)
                if i < 4:
                    hi, lo = (a[p][:, i // 2, :, :].rearrange("p d r -> p (d r)") for a in (twice_hi, twice_lo))
                    cols = slice((i % 2) * HALF, (i % 2 + 1) * HALF)
                    pe.matmul(out[:, :], lo, zT_hi[:, cols], start=True, stop=False)
                    pe.matmul(out[:, :], hi, zT_hi[:, cols], start=False, stop=False)
                    mm = pe.matmul(out[:, :], hi, zT_lo[:, cols], start=False, stop=True)
                else:
                    for t in range(4):
                        tile = (i - 4) * 4 + t
                        mm = pe.matmul(out[:, t * P:(t + 1) * P], zT[:, tile * P:(tile + 1) * P],
                                       k["uvT"][:, ds(channel(c) * P, P)], start=True, stop=True)
                mm.then_inc(unit_full, 1)

            def blocks(b, c, i, p):
                step = (b * CH + c) * TILES + i
                rows = slice(i * P, (i + 1) * P)
                pe.wait_ge(f_ready, step + 1)
                for n in range(2):
                    cols = slice(n * HALF, (n + 1) * HALF)
                    pe.matmul(f_ps[:, cols], u_st[p][:, rows], v_hi[p][:, cols], start=True, stop=False)
                    mm = pe.matmul(f_ps[:, cols], u_st[p][:, rows], v_lo[p][:, cols], start=False, stop=True)
                mm.then_inc(f_full, 1)
                pe.wait_ge(t_ready, step + 1)
                for n in range(2):
                    cols = slice(n * HALF, (n + 1) * HALF)
                    pe.matmul(t_ps[:, cols], v_hi[p][:, rows], u_st[p][:, cols], start=True, stop=False)
                    mm = pe.matmul(t_ps[:, cols], v_lo[p][:, rows], u_st[p][:, cols], start=False, stop=True)
                mm.then_inc(t_full, 1)

            def products(b, c, i, p):
                step = (b * CH + c) * TILES + i
                if i == 0:
                    pe.wait_ge(vu_free, b * CH + c + 1)
                pe.wait_ge(f_ready, step + 2)
                pe.wait_ge(t_ready, step + 2)
                for n in range(2):
                    cols = slice(n * HALF, (n + 1) * HALF)
                    pe.matmul(vu_ps[0:RANK, cols], uv_tok[p][:, i, 1, :], t_sig[i % 2][:, cols], start=(i == 0), stop=(i == TILES - 1))
                    mm = pe.matmul(vu_ps[RANK:P, cols], uv_tok[p][:, i, 0, :], f_sig[i % 2][:, cols], start=(i == 0), stop=(i == TILES - 1))
                mm.then_inc(used[i % 2], 1)

            u = Units(0, 0, 0)
            for n in range(2 * BATCH):
                out = u.next()
                u.wait_empty(pe)
                pe.wait_ge(z_ready, n + 1)
                for t in range(4):
                    mm = pe.transpose(out[:, t * P:(t + 1) * P], z[:, 4 * n + t, :], k["ident"][:, :])
                mm.then_inc(unit_full, 1)
            for i in range(PREP):
                prepare(u, i, 0, 0, 0)
            for n in (u.n - 1, u.n):
                u.wait_emptied(pe, n)
            blocks(0, 0, 0, 0)

            def body(b, c, p, last_pair, last_batch):
                last = last_pair and last_batch and p == 1
                u = units_at(b, PREP * c)
                for i in range(TILES):
                    if i < TILES - 1:
                        blocks(b, c, i + 1, p)
                    elif not last:
                        for n in (u.n - 1, u.n):
                            u.wait_emptied(pe, n)
                        blocks(b, c + 1, 0, 1 - p)
                    if i < PREP and not last:
                        prepare(u, i, c + 1, 1 - p, b)
                    products(b, c, i, p)

            def program(b, last_batch):
                channels(pe, b, last_batch, body)
                u = units_at(b, prepared_units(last_batch))
                pe.wait_ge(vu_free, (b + 1) * CH + 1)
                for i in range(2):
                    out = u.next()
                    u.wait_empty(pe)
                    for c in range(CH):
                        mm = pe.matmul(out[:, :], k["uv"][:, c * DIM:(c + 1) * DIM], vuT[:, c * SEQ + i * HALF:c * SEQ + (i + 1) * HALF],
                                       start=(c == 0), stop=(c == CH - 1))
                    mm.then_inc(unit_full, 1)
                sums = (u.n - 1, u.n)
                for i in range(2):
                    u.wait_emptied(pe, sums[i])
                    out = u.next()
                    u.wait_empty(pe)
                    for t in range(4):
                        mm = pe.transpose(out[:, t * P:(t + 1) * P], msgT[:, (4 * i + t) * P:(4 * i + t + 1) * P], k["ident"][:, :])
                    mm.then_inc(unit_full, 1)
            batches(pe, program)

        @block.gpsimd
        def _(pool):
            start_free(pool, *unit_free, *used, f_ready, t_ready, vu_free)

        @block.scalar
        def _(act):
            def high_parts(u, p):
                for i in range(4):
                    src = u.next()
                    u.wait_full(act)
                    dst = (u_st, v_hi)[i // 2][p]
                    act.copy(dst[:, (i % 2) * HALF:(i % 2 + 1) * HALF], src[:, :]).then_inc(hi_ready, 1)
                u.n += 2

            def sigmoids(b, c, i):
                step = (b * CH + c) * TILES + i
                act.wait_ge(used[i % 2], (b * CH + c) * (TILES // 2) + i // 2 + 1)
                act.wait_ge(f_full, step + 1)
                act.activation(f_sig[i % 2][:, :], f_ps[:, :], ACT.Sigmoid).then_inc(f_ready, 1)
                act.wait_ge(t_full, step + 1)
                act.activation(t_sig[i % 2][:, :], t_ps[:, :], ACT.Sigmoid).then_inc(t_ready, 1)

            act.wait_ge(var_ready, 1)
            act.activation(dev[:, :], spread[:, :], ACT.Sqrt).then_inc(dev_ready, 1)
            u = Units(0, 0, 0)
            for n in range(2 * BATCH):
                src = u.next()
                u.wait_full(act)
                act.copy(zT_all[:, n * HALF:(n + 1) * HALF], src[:, :]).then_inc(u.free(), 1)
            high_parts(u, 0)
            sigmoids(0, 0, 0)

            def body(b, c, p, last_pair, last_batch):
                last = last_pair and last_batch and p == 1
                u = units_at(b, PREP * c)
                for i in range(TILES):
                    if i < TILES - 1:
                        sigmoids(b, c, i + 1)
                    elif not last:
                        sigmoids(b, c + 1, 0)
                    if i < 4 and not last:
                        src = u.next()
                        u.wait_full(act)
                        dst = (u_st, v_hi)[i // 2][1 - p]
                        act.copy(dst[:, (i % 2) * HALF:(i % 2 + 1) * HALF], src[:, :]).then_inc(hi_ready, 1)

            def program(b, last_batch):
                channels(act, b, last_batch, body)
                u = units_at(b, prepared_units(last_batch))
                for i in range(2):
                    src = u.next()
                    u.wait_full(act)
                    act.copy(msgT[:, i * HALF:(i + 1) * HALF], src[:, :]).then_inc(u.free(), 1)
            batches(act, program)

        @block.vector
        def _(dve):
            flat_stats = k["stats"][:, :, :].rearrange("p t s -> p (t s)")

            def prepared(u, i, c, p, b):
                src = u.next()
                u.wait_full(dve)
                cols = slice((i % 2) * HALF, (i % 2 + 1) * HALF)
                if i < 4:
                    dve.wait_ge(hi_ready, (b * CH + c) * 4 + i + 1)
                if i < 2:
                    ins = dve.tensor_tensor(u_st[p][RANK:P, cols], src[RANK:P, :], u_st[p][RANK:P, cols].bitcast(F32), ALU.subtract)
                elif i < 4:
                    ins = dve.tensor_tensor(v_lo[p][:, cols], src[:, :], v_hi[p][:, cols].bitcast(F32), ALU.subtract)
                else:
                    ins = dve.tensor_copy(uv_tok[p][:, 4 * (i - 4):4 * (i - 3), :, :].rearrange("p t a r -> p (t a r)"), src[:, :])
                ins.then_inc(u.free(), 1)

            def double(number, c, p):
                src = k["uvT"][:, ds(channel(c) * P, P)].rearrange("p (a r) -> p a r", a=2)
                for i in range(2):
                    ins = dve.tensor_scalar(twice_hi[p][:, :, i, :], src, 1.0, None, ALU.mult)
                ins.then_inc(twice_high, 1)
                dve.wait_ge(twice_high, number)
                for i in range(2):
                    ins = dve.tensor_tensor(twice_lo[p][:, :, i, :], src, twice_hi[p][:, :, i, :].bitcast(F32), ALU.subtract)
                ins.then_inc(twice_ready, 1)

            def take_tokens(b):
                tokens = zT_all[:, ds(b * SEQ, SEQ)]
                dve.tensor_scalar(zT[:, :], tokens, 1.0, None, ALU.mult)
                dve.tensor_scalar(zT_hi[:, :], tokens, 1.0, None, ALU.mult).then_inc(tokens_high, 1)
                dve.wait_ge(tokens_high, b + 1)
                return dve.tensor_tensor(zT_lo[:, :], tokens, zT_hi[:, :].bitcast(F32), ALU.subtract)

            link = Link(dve, link_sem)
            row_moments(dve, link, k["stats"], mean[:, :], spread[:, :], work[:, :], ALL).then_inc(var_ready, 1)
            dve.wait_ge(dev_ready, 1)
            link(dve.reciprocal(rstd[:, :], dev[:, :]))
            for t in range(ALL):
                ins = dve.tensor_scalar(z[:, t, :], k["x"][:, t * DIM:(t + 1) * DIM], mean[:, t:t + 1], rstd[:, t:t + 1],
                                        ALU.subtract, ALU.mult)
                if t % 4 == 3:
                    ins.then_inc(z_ready, 1)
            u = Units(0, 0, 2 * BATCH)
            for n in range(2):
                u.wait_emptied(dve, n)
            link(take_tokens(0))
            for p in range(2):
                double(p + 1, p, p)
            for i in range(PREP):
                prepared(u, i, 0, 0, 0)

            def body(b, c, p, last_pair, last_batch):
                last = last_pair and last_batch and p == 1
                u = units_at(b, PREP * c)
                if not last_pair or not last_batch:
                    double(b * CH + c + 3, c + 2, p)
                for i in range(PREP if not last else 0):
                    prepared(u, i, c + 1, 1 - p, b)
                if last_pair and not last_batch and p == 0:
                    take_tokens(b + 1).then_inc(tokens_taken, 1)
                dve.wait_ge(used[1], (b * CH + c + 1) * (TILES // 2) + 1)
                dve.tensor_copy(vuT[:, ds(c * SEQ, SEQ)], vu_ps[:, :]).then_inc(vu_free, 1)

            def program(b, last_batch):
                channels(dve, b, last_batch, body)
                u = units_at(b, prepared_units(last_batch))
                u.n += 2
                for i in range(2):
                    src = u.next()
                    u.wait_full(dve)
                    x4 = k["x"][:, ds(b * TILES * DIM + i * HALF, HALF)]
                    dve.tensor_tensor(x4, x4, src[:, :], ALU.add).then_inc(u.free(), 1)
                for n in (u.n - 1, u.n):
                    u.wait_emptied(dve, n)
                for t in range(TILES):
                    dve.bn_stats(flat_stats[:, ds((b * TILES + t) * 6, 6)], k["x"][:, ds((b * TILES + t) * DIM, DIM)])
            batches(dve, program)

        phase.close()
        clear_semaphores(nc, sems)


def store_phase(nc, k, out):
    with ExitStack() as ctx:
        stored = ctx.enter_context(nc.semaphore("stored"))
        block = ctx.enter_context(nc.Block())

        @block.sync
        def _(sp):
            sp.dma_start(out.rearrange("b (n p) e -> p (b n) e", p=P),
                         k["x"][:, :].rearrange("p (n e) -> p n e", e=DIM)).then_inc(stored, 16)
            sp.wait_ge(stored, 16)


def hybrid_kernel(nc, d, out):
    def allocate(ctx, k, shapes):
        for name, (shape, dt) in shapes.items():
            k[name] = ctx.enter_context(nc.sbuf_tensor(name, shape, dt))

    k = {name: [nc.dram_tensor(f"{name}{i}", (HALF_NB * P, DIM), F32, kind="Internal").ap() for i in range(HALVES)]
         for name in ("sent_rows", "result_rows")}
    with ExitStack() as whole:
        allocate(whole, k, {"x": ([P, ALL * DIM], F32),
                            "stats": ([P, ALL, 6], F32),
                            "ident": ([P, P], F32), "ln_cols": ([P, 4], F32),
                            "attn_wT": ([P, DIM], F32), "gate_wT": ([P, EXPERTS], F32)})
        with ExitStack() as attention:
            allocate(attention, k, {"ident16": ([P, P], BF16), "mask": ([P, P], BF16),
                                    "w_qkv": ([P, 3 * DIM], F32), "w_o": ([P, DIM], F32),
                                    "ln_rows": ([P, 4 * HD], F32), "bo_rows": ([P, DIM], F32)})
            setup_phase(nc, d, k)
            attention_phase(nc, k)
        allocate(whole, k, {"uv": ([P, CH * DIM], F32), "uvT": ([P, CH * P], F32)})
        moe_phase(nc, d, k, "f1", True)
        message_phase(nc, k)
        moe_phase(nc, d, k, "f2", False)
        store_phase(nc, k, out)


_INS = {'x': 'L0_attn_a_x', 'Wk': 'L0_attn_a_Wk', 'Wq': 'L0_attn_a_Wq', 'Wv': 'L0_attn_a_Wv', 'Wo': 'L0_attn_a_Wo',
        'bo': 'L0_attn_a_bo', 'kln_w': 'L0_attn_a_kln_w', 'kln_b': 'L0_attn_a_kln_b', 'qln_w': 'L0_attn_a_qln_w',
        'qln_b': 'L0_attn_a_qln_b', 'u': 'L0_attn_b_ternary_factor_u', 'v': 'L0_attn_b_ternary_factor_v',
        'ln1_g': 'L0_ffn_ln1_g', 'ln1_b': 'L0_ffn_ln1_b', 'attn_w': 'L0_ffn_attn_w', 'ln2_g': 'L0_ffn_ln2_g',
        'ln2_b': 'L0_ffn_ln2_b', 'gate_w': 'L0_ffn_gate_w', 'gate_proj': 'L0_ffn_gate_proj',
        'up_proj': 'L0_ffn_up_proj', 'down_proj': 'L0_ffn_down_proj'}


def kernel(**inputs):
    import numpy as _np
    import concourse.bacc as _bacc
    from concourse import mybir as _mybir
    from concourse.bass_utils import run_bass_kernel_spmd as _run

    nc = _bacc.Bacc("TRN2", target_bir_lowering=False, num_devices=1)
    arrays, aps = {}, {}
    for short, name in _INS.items():
        a = _np.ascontiguousarray(inputs[name])
        arrays[f"in_{name}_dram"] = a
        aps[short] = nc.dram_tensor(f"in_{name}_dram", a.shape, _mybir.dt.from_np(a.dtype), kind="ExternalInput").ap()
    out = nc.dram_tensor("out_0_dram", (BATCH, SEQ, DIM), F32, kind="ExternalOutput").ap()
    hybrid_kernel(nc, aps, out)
    r = _run(nc, [arrays], core_ids=[0])
    return r.results[0]["out_0_dram"]
```
